# Optimizing a Trainium2 kernel written in Bass

```python
import numpy as np
import jax
import jax.numpy as jnp

def _softmax(x, axis=-1):
    return jax.nn.softmax(x, axis=axis)

def _gelu(x):
    return jax.nn.gelu(x, approximate=True)

def _silu(x):
    return jax.nn.silu(x)

def _sigmoid(x):
    return jax.nn.sigmoid(x)

def _layernorm(x, axis=-1, eps=1e-05):
    m = jnp.mean(x, axis=axis, keepdims=True)
    v = jnp.var(x, axis=axis, keepdims=True)
    return (x - m) / jnp.sqrt(v + eps)

def _scatter_add(tgt, idx, src, axis=0):
    return tgt.at[idx].add(src)

def _segment_sum(src, seg, n):
    return jax.ops.segment_sum(src, seg, n)
kernel_name = 'mk_decoder_preln_d1_seqx_r4_f72567'

def setup_inputs(seed: int=0):
    np.random.seed(seed)
    _w = jnp.asarray

    def _rec_inputs():
        import jax
        import jax.numpy as jnp
        _rk = jax.random.key(seed)
        x = -0.0002928 + 1 * jax.random.normal(jax.random.fold_in(_rk, 1), (4, 1024, 256), jnp.float32)
        _lenS = 1024 - jax.random.randint(jax.random.fold_in(_rk, 7), (4,), 0, max(1, 1024 // 4) + 1, jnp.int32)
        _lenS2 = 77 - jax.random.randint(jax.random.fold_in(_rk, 8), (4,), 0, max(1, 77 // 4) + 1, jnp.int32)
        _ctx_1024P = jax.random.normal(jax.random.fold_in(_rk, 11), (4, 16, 256), jnp.float32)
        _ctx_1024c = jax.random.dirichlet(jax.random.fold_in(_rk, 511), 0.3 * jnp.ones((16,), jnp.float32), (4, 77))
        _ctx_1024t = jnp.einsum('bsk,bkd->bsd', _ctx_1024c, _ctx_1024P)
        _ctx_1024t = _ctx_1024t * jax.lax.rsqrt(jnp.mean(jnp.square(_ctx_1024t)) + 1e-12) * 0.953939
        ctx_1024 = -1.39393e-06 + 0.999914 * (_ctx_1024t + 0.3 * jax.random.normal(jax.random.fold_in(_rk, 611), (4, 77, 256), jnp.float32))
        return (x, ctx_1024)
    x, ctx_1024 = _rec_inputs()

    def _L0_attn_setup():
        import jax, jax.numpy as jnp
        import numpy as np

        def _sin_rpe(Lq, d_model, dtype):
            inv_freq = 1.0 / 10000.0 ** (jnp.arange(0, d_model, 2, dtype=jnp.float32) / d_model)
            pos = jnp.arange(-(Lq - 1), Lq, dtype=jnp.float32)
            ang = pos[:, None] * inv_freq[None, :]
            emb = jnp.zeros((2 * Lq - 1, d_model), dtype=jnp.float32)
            emb = emb.at[:, 0::2].set(jnp.sin(ang)).at[:, 1::2].set(jnp.cos(ang))
            return emb.astype(dtype)

        def _rel_shift(x):
            B, H, Lq, Lr = x.shape
            xp = jnp.concatenate([jnp.zeros((B, H, Lq, 1), x.dtype), x], axis=-1)
            xp = xp.reshape(B, H, Lr + 1, Lq)
            return xp[:, :, 1:].reshape(B, H, Lq, Lr)[..., Lr - Lq:]
        key = jax.random.key(seed)
        ks = jax.random.split(key, 7)
        B, Lq, D, H = (1, 512, 256, 16)
        d_head = D // H
        s = 0.02
        return {'w': jax.random.normal(ks[0], (B, Lq, D), jnp.float32), 'Wq': jax.random.normal(ks[1], (D, D), jnp.float32) * s, 'Wk': jax.random.normal(ks[2], (D, D), jnp.float32) * s, 'Wv': jax.random.normal(ks[3], (D, D), jnp.float32) * s, 'Wr': jax.random.normal(ks[4], (D, D), jnp.float32) * s, 'u_bias': jax.random.normal(ks[5], (H, d_head), jnp.float32) * 0.02, 'v_bias': jax.random.normal(ks[6], (H, d_head), jnp.float32) * 0.02}
    _L0_attn_all = _L0_attn_setup()
    _L0_attn_in = {k: v for k, v in _L0_attn_all.items() if k in ('Wq', 'Wk', 'Wv', 'Wr', 'u_bias', 'v_bias')}
    del _L0_attn_all

    def _L0_xattn_setup():
        import jax, jax.numpy as jnp
        import numpy as np
        B, T, E, H = (2, 512, 256, 16)
        S = E // H
        LN_EPS = 1e-05

        def _layer_norm(x, w, b):
            mu = jnp.mean(x, axis=-1, keepdims=True)
            var = jnp.mean(jnp.square(x - mu), axis=-1, keepdims=True)
            return (x - mu) * jax.lax.rsqrt(var + LN_EPS) * w + b
        key = jax.random.key(seed)
        ks = jax.random.split(key, 7)
        scale = 0.02
        return {'queries': jax.random.normal(ks[0], (B, T, E), dtype=jnp.float32), 'keys': jax.random.normal(ks[1], (B, T, E), dtype=jnp.float32), 'values': jax.random.normal(ks[2], (B, T, E), dtype=jnp.float32), 'Wq': jax.random.normal(ks[3], (E, E), dtype=jnp.float32) * scale, 'Wk': jax.random.normal(ks[4], (E, E), dtype=jnp.float32) * scale, 'Wv': jax.random.normal(ks[5], (E, E), dtype=jnp.float32) * scale, 'Wo': jax.random.normal(ks[6], (E, E), dtype=jnp.float32) * scale, 'bo': jnp.zeros((E,), dtype=jnp.float32), 'q_ln_w': jnp.ones((S,), dtype=jnp.float32), 'q_ln_b': jnp.zeros((S,), dtype=jnp.float32), 'k_ln_w': jnp.ones((S,), dtype=jnp.float32), 'k_ln_b': jnp.zeros((S,), dtype=jnp.float32)}
    _L0_xattn_all = _L0_xattn_setup()
    _L0_xattn_in = {k: v for k, v in _L0_xattn_all.items() if k in ('Wq', 'Wk', 'Wv', 'Wo', 'bo', 'q_ln_w', 'q_ln_b', 'k_ln_w', 'k_ln_b')}
    del _L0_xattn_all

    def _L0_ffn_setup():
        import jax, jax.numpy as jnp
        import numpy as np
        TOP_K = 2
        ROUTE_SCALE = 1.0
        EPS = 1e-20
        B, S, D = (2, 128, 256)
        E = 8
        F = 192
        FS = 192 * 1
        key = jax.random.key(seed)
        ks = jax.random.split(key, 9)
        s = 0.02
        return {'hidden_states': jax.random.normal(ks[0], (B, S, D), dtype=jnp.float32), 'W_gate_router': jax.random.normal(ks[1], (D, E), dtype=jnp.float32) * s, 'expert_bias': jnp.zeros((E,), dtype=jnp.float32), 'Wg': jax.random.normal(ks[2], (E, D, F), dtype=jnp.float32) * s, 'Wu': jax.random.normal(ks[3], (E, D, F), dtype=jnp.float32) * s, 'Wd': jax.random.normal(ks[4], (E, F, D), dtype=jnp.float32) * s, 'Wg_s': jax.random.normal(ks[5], (D, FS), dtype=jnp.float32) * s, 'Wu_s': jax.random.normal(ks[6], (D, FS), dtype=jnp.float32) * s, 'Wd_s': jax.random.normal(ks[7], (FS, D), dtype=jnp.float32) * s}
    _L0_ffn_all = _L0_ffn_setup()
    _L0_ffn_in = {k: v for k, v in _L0_ffn_all.items() if k in ('W_gate_router', 'expert_bias', 'Wg', 'Wu', 'Wd', 'Wg_s', 'Wu_s', 'Wd_s')}
    del _L0_ffn_all
    return {'x': x, 'ctx_1024': ctx_1024, 'L0_attn_Wq': _L0_attn_in['Wq'], 'L0_attn_Wk': _L0_attn_in['Wk'], 'L0_attn_Wv': _L0_attn_in['Wv'], 'L0_attn_Wr': _L0_attn_in['Wr'], 'L0_attn_u_bias': _L0_attn_in['u_bias'], 'L0_attn_v_bias': _L0_attn_in['v_bias'], 'L0_xattn_Wq': _L0_xattn_in['Wq'], 'L0_xattn_Wk': _L0_xattn_in['Wk'], 'L0_xattn_Wv': _L0_xattn_in['Wv'], 'L0_xattn_Wo': _L0_xattn_in['Wo'], 'L0_xattn_bo': _L0_xattn_in['bo'], 'L0_xattn_q_ln_w': _L0_xattn_in['q_ln_w'], 'L0_xattn_q_ln_b': _L0_xattn_in['q_ln_b'], 'L0_xattn_k_ln_w': _L0_xattn_in['k_ln_w'], 'L0_xattn_k_ln_b': _L0_xattn_in['k_ln_b'], 'L0_ffn_W_gate_router': _L0_ffn_in['W_gate_router'], 'L0_ffn_expert_bias': _L0_ffn_in['expert_bias'], 'L0_ffn_Wg': _L0_ffn_in['Wg'], 'L0_ffn_Wu': _L0_ffn_in['Wu'], 'L0_ffn_Wd': _L0_ffn_in['Wd'], 'L0_ffn_Wg_s': _L0_ffn_in['Wg_s'], 'L0_ffn_Wu_s': _L0_ffn_in['Wu_s'], 'L0_ffn_Wd_s': _L0_ffn_in['Wd_s']}

def reference(x, ctx_1024, L0_attn_Wq, L0_attn_Wk, L0_attn_Wv, L0_attn_Wr, L0_attn_u_bias, L0_attn_v_bias, L0_xattn_Wq, L0_xattn_Wk, L0_xattn_Wv, L0_xattn_Wo, L0_xattn_bo, L0_xattn_q_ln_w, L0_xattn_q_ln_b, L0_xattn_k_ln_w, L0_xattn_k_ln_b, L0_ffn_W_gate_router, L0_ffn_expert_bias, L0_ffn_Wg, L0_ffn_Wu, L0_ffn_Wd, L0_ffn_Wg_s, L0_ffn_Wu_s, L0_ffn_Wd_s):
    import jax
    import jax.numpy as jnp

    def _L0_attn_ref(w, Wq, Wk, Wv, Wr, u_bias, v_bias):
        import jax, jax.numpy as jnp
        import numpy as np

        def _sin_rpe(Lq, d_model, dtype):
            inv_freq = 1.0 / 10000.0 ** (jnp.arange(0, d_model, 2, dtype=jnp.float32) / d_model)
            pos = jnp.arange(-(Lq - 1), Lq, dtype=jnp.float32)
            ang = pos[:, None] * inv_freq[None, :]
            emb = jnp.zeros((2 * Lq - 1, d_model), dtype=jnp.float32)
            emb = emb.at[:, 0::2].set(jnp.sin(ang)).at[:, 1::2].set(jnp.cos(ang))
            return emb.astype(dtype)

        def _rel_shift(x):
            B, H, Lq, Lr = x.shape
            xp = jnp.concatenate([jnp.zeros((B, H, Lq, 1), x.dtype), x], axis=-1)
            xp = xp.reshape(B, H, Lr + 1, Lq)
            return xp[:, :, 1:].reshape(B, H, Lq, Lr)[..., Lr - Lq:]
        B, Lq, D = w.shape
        H, d_head = u_bias.shape
        scale = 1.0 / np.sqrt(d_head).astype(np.float32)
        r = _sin_rpe(Lq, D, w.dtype)
        q = (w @ Wq.T).reshape(B, Lq, H, d_head).transpose(0, 2, 1, 3)
        k = (w @ Wk.T).reshape(B, Lq, H, d_head).transpose(0, 2, 1, 3)
        v = (w @ Wv.T).reshape(B, Lq, H, d_head).transpose(0, 2, 1, 3)
        rp = (r @ Wr.T).reshape(2 * Lq - 1, H, d_head).transpose(1, 0, 2)
        AC = jnp.einsum('bhid,bhjd->bhij', q + u_bias[None, :, None, :], k)
        BD = jnp.einsum('bhid,hjd->bhij', q + v_bias[None, :, None, :], rp)
        BD = _rel_shift(BD)
        attn = jax.nn.softmax((AC + BD) * scale, axis=-1)
        out = jnp.einsum('bhij,bhjd->bhid', attn, v)
        return out.transpose(0, 2, 1, 3).reshape(B, Lq, D)

    def _L0_xattn_ref(queries, keys, values, Wq, Wk, Wv, Wo, bo, q_ln_w, q_ln_b, k_ln_w, k_ln_b):
        import jax, jax.numpy as jnp
        import numpy as np
        B, T, E, H = (2, 512, 256, 16)
        S = E // H
        LN_EPS = 1e-05

        def _layer_norm(x, w, b):
            mu = jnp.mean(x, axis=-1, keepdims=True)
            var = jnp.mean(jnp.square(x - mu), axis=-1, keepdims=True)
            return (x - mu) * jax.lax.rsqrt(var + LN_EPS) * w + b
        b, tq, e = queries.shape
        tk = keys.shape[1]
        h, s = (H, S)
        q = (queries @ Wq).reshape(b, tq, h, s)
        k = (keys @ Wk).reshape(b, tk, h, s)
        v = (values @ Wv).reshape(b, tk, h, s)
        q = _layer_norm(q, q_ln_w, q_ln_b)
        k = _layer_norm(k, k_ln_w, k_ln_b)
        inv4 = jnp.asarray(e, q.dtype) ** (-0.25)
        q = q * inv4
        k = k * inv4
        dot = jnp.einsum('bqhs,bkhs->bhqk', q, k)
        causal = jnp.tril(jnp.ones((tq, tk), dtype=bool))
        dot = jnp.where(causal, dot, jnp.asarray(-jnp.inf, dot.dtype))
        attn = jax.nn.softmax(dot, axis=-1)
        out = jnp.einsum('bhqk,bkhs->bqhs', attn, v).reshape(b, tq, e)
        return out @ Wo + bo

    def _L0_ffn_ref(hidden_states, W_gate_router, expert_bias, Wg, Wu, Wd, Wg_s, Wu_s, Wd_s):
        import jax, jax.numpy as jnp
        import numpy as np
        TOP_K = 2
        ROUTE_SCALE = 1.0
        EPS = 1e-20
        B, S, D = (2, 128, 256)
        E = 8
        F = 192
        FS = 192 * 1
        b, s, d = hidden_states.shape
        x = hidden_states.reshape(-1, d)
        T = x.shape[0]
        logits = x @ W_gate_router
        scores = jax.nn.sigmoid(logits.astype(jnp.float32))
        _, sel = jax.lax.top_k(scores + expert_bias, TOP_K)
        top_scores = jnp.take_along_axis(scores, sel, axis=1)
        top_scores = top_scores / (top_scores.sum(-1, keepdims=True) + EPS)
        top_scores = top_scores * ROUTE_SCALE
        shared = jax.nn.silu(x @ Wg_s) * (x @ Wu_s) @ Wd_s
        tok = jnp.repeat(jnp.arange(T), TOP_K)
        exp = sel.reshape(-1)
        w = top_scores.reshape(-1)
        xr = x[tok]
        h = jax.nn.silu(jnp.einsum('nd,edf->enf', xr, Wg)) * jnp.einsum('nd,edf->enf', xr, Wu)
        out_all = jnp.einsum('enf,efd->end', h, Wd)
        routed = out_all[exp, jnp.arange(exp.shape[0])]
        routed = (routed.astype(jnp.float32) * w[:, None]).astype(hidden_states.dtype)
        out = shared.at[tok].add(routed)
        return out.reshape(b, s, d)
    x = x + _L0_attn_ref(_layernorm(x, axis=-1), L0_attn_Wq, L0_attn_Wk, L0_attn_Wv, L0_attn_Wr, L0_attn_u_bias, L0_attn_v_bias)
    x = x + _L0_xattn_ref(_layernorm(x, axis=-1), ctx_1024, ctx_1024, L0_xattn_Wq, L0_xattn_Wk, L0_xattn_Wv, L0_xattn_Wo, L0_xattn_bo, L0_xattn_q_ln_w, L0_xattn_q_ln_b, L0_xattn_k_ln_w, L0_xattn_k_ln_b)
    x = x + _L0_ffn_ref(_layernorm(x, axis=-1), L0_ffn_W_gate_router, L0_ffn_expert_bias, L0_ffn_Wg, L0_ffn_Wu, L0_ffn_Wd, L0_ffn_Wg_s, L0_ffn_Wu_s, L0_ffn_Wd_s)
    return x

_drawn_inputs = setup_inputs


def setup_inputs(seed=0):
    import zlib

    import numpy as np

    out = dict(_drawn_inputs(seed))
    spreads = {'L0_xattn_bo': (0.0, 0.1),
     'L0_xattn_q_ln_w': (1.0, 0.6),
     'L0_xattn_q_ln_b': (0.0, 2.0),
     'L0_xattn_k_ln_w': (1.0, 0.6),
     'L0_xattn_k_ln_b': (0.0, 2.0),
     'L0_ffn_expert_bias': (0.0, 0.781)}
    factors = {'L0_attn_Wq': 8.0,
     'L0_attn_Wk': 8.0,
     'L0_attn_Wv': 5.58,
     'L0_attn_Wr': 8.0,
     'L0_attn_u_bias': 8.0,
     'L0_attn_v_bias': 8.0,
     'L0_xattn_Wq': 8.0,
     'L0_xattn_Wk': 8.0,
     'L0_ffn_W_gate_router': 8.0,
     'L0_ffn_Wg': 5.516,
     'L0_ffn_Wu': 5.458,
     'L0_ffn_Wd': 5.482,
     'L0_ffn_Wg_s': 3.944,
     'L0_ffn_Wu_s': 3.867,
     'L0_ffn_Wd_s': 3.863}
    for name, (base, spread) in spreads.items():
        noise = np.random.default_rng([zlib.crc32(name.encode()), seed]).standard_normal(out[name].shape)
        drawn = base * np.exp(spread * noise) if base else spread * noise
        out[name] = jnp.asarray(drawn.astype(out[name].dtype))
    for name, factor in factors.items():
        out[name] = (out[name] * factor).astype(out[name].dtype)
    return out
```

```python
import concourse.bass as bass
from concourse import mybir
from contextlib import ExitStack

fp32 = mybir.dt.float32
bf16 = mybir.dt.bfloat16
ALU = mybir.AluOpType
ACT = mybir.ActivationFunctionType
AX = mybir.AxisListType

B, L, D = 4, 1024, 256
H, DH = 16, 16
S2 = 77
E, F = 8, 192
P = 128
NT = B * L // P
TPB = L // P
KC = D // P
BLK = 512
NBLK = B * L // BLK
BT = BLK // P
NH = B * H
RW = 2 * L
UW = L + P
UB = UW // 3
VW = DH + 1
EPS = 1e-5
TERMS = [(0, 0), (0, 1), (0, 2), (1, 0), (1, 1), (1, 2), (2, 0), (2, 1)]
QU, QV, KK = range(3)


def build_projections(nc, t, d):
    ctx = ExitStack()
    with ctx:
        def sb(name, shape, dt):
            return ctx.enter_context(nc.sbuf_tensor(name, shape, dt))

        def sem(name):
            return t.ctx.enter_context(nc.semaphore(name))

        wT = sb("wT", [P, 4, KC, D], fp32)
        basis = sb("basis", [P, KC, RW], fp32)
        uvcol = sb("uvcol", [P, 2, KC], fp32)
        uvs = sb("uvs", [P, 2, KC], fp32)
        epsc = sb("epsc", [P, 1], fp32)
        stats = sb("stats", [P, BT, 6], fp32)
        mv = sb("mv", [P, 2, BT, 2], fp32)
        std = sb("std", [P, 2, BT], fp32)
        rstd = sb("rstd", [P, BT], fp32)
        xhat = sb("xhat", [P, BT, D], fp32)
        xT = sb("xT", [P, KC, BLK], fp32)
        full = sb("full", [P, 3, BLK], fp32)
        rest = sb("rest", [P, 3, BLK], fp32)
        parts = sb("parts", [P, 3, 3, BLK], bf16)
        pT = ctx.enter_context(nc.psum_tensor("pT", [P, 2, KC, 2, P], fp32))
        pU = ctx.enter_context(nc.psum_tensor("pU", [P, 4, BLK], fp32))
        pV = ctx.enter_context(nc.psum_tensor("pV", [P, 2, 2, D], fp32))

        s_w = sem("s_weights")
        s_wr = sem("s_position_weights")
        s_basis = sem("s_basis")
        s_uv = sem("s_uv")
        s_x = [sem(f"s_x{i}") for i in range(B)]
        s_const = sem("s_const")
        s_uvs = sem("s_uvs")
        s_mv = sem("s_mv")
        s_bn = sem("s_bn")
        s_std = sem("s_std")
        s_rstd = sem("s_rstd")
        s_xhat = sem("s_xhat")
        s_tr = sem("s_tr")
        s_xT = sem("s_xT")
        s_unit = sem("s_unit")
        s_full = sem("s_full")
        s_hi = sem("s_hi")
        s_rest = sem("s_rest")
        s_mid = sem("s_mid")
        s_lo = sem("s_lo")
        s_kept = [sem(f"s_kept{i}") for i in range(3)]
        s_v = sem("s_v")
        s_vx = sem("s_vx")

        RU = KC * RW // BLK
        CPB = 6
        UPB = 4
        CUTS = [(0, QU, 0), (0, QV, 0), (1, QU, 1), (1, QV, 1), (2, KK, 0), (3, KK, 1)]

        with nc.Block() as block:
            @block.sync
            def _(sp):
                sp.dma_start(wT[:, 3, :, :], d["wr"].rearrange("(c p) o -> p c o", p=P)).then_inc(s_wr, 16)
                sp.dma_start(t.ident[:, :], d["ident"]).then_inc(t.s_ident, 16)
                sp.dma_start(basis[:, :, :], d["basis"].rearrange("(c p) o -> p c o", p=P)).then_inc(s_basis, 16)
                for b in range(B):
                    sp.dma_start(t.x[:, b * TPB:(b + 1) * TPB, :],
                                 d["x"][b, :, :].rearrange("(t p) e -> p t e", p=P)).then_inc(s_x[b], 16)
                for i, w in enumerate(("wq", "wk", "wv")):
                    sp.dma_start(wT[:, i, :, :], d[w].rearrange("(c p) o -> p c o", p=P)).then_inc(s_w, 16)
                sp.dma_start(uvcol[:, :, :], d["uv"]).then_inc(s_uv, 16)
                for c in range(RU):
                    sp.wait_ge(s_lo, c + 1)
                    sp.dma_start(d["rsplit"][:, (c % KC) * P:(c % KC + 1) * P,
                                             (c // KC) * BLK:(c // KC + 1) * BLK].rearrange("s p n -> p s n"),
                                 parts[:, c % 3, :, :]).then_inc(s_kept[c % 3], 16)
                with sp.Fori(0, NBLK) as k:
                    for j, (_, operand, chunk) in enumerate(CUTS):
                        slot = (RU + j) % 3
                        token = sp.snap(k * BLK)
                        sp.wait_ge(s_lo, k * CPB + RU + j + 1)
                        sp.dma_start(d["qsplit"][operand, :, chunk * P:(chunk + 1) * P,
                                                 bass.ds(token, BLK)].rearrange("s p n -> p s n"),
                                     parts[:, slot, :, :]).then_inc(s_kept[slot], 16)
                for slot in range(3):
                    sp.wait_ge(s_kept[slot], 16 * len([c for c in range(RU + NBLK * CPB) if c % 3 == slot]))

            @block.gpsimd
            def _(pool):
                nc.gpsimd.memset(epsc[:, :], EPS).then_inc(s_const, 1)
                nc.gpsimd.memset(t.vx[:, :, :, :], 1.0).then_inc(s_const, 1)

                def third(slot, count):
                    pool.wait_ge(s_mid, count)
                    nc.gpsimd.tensor_tensor(parts[:, slot, 2, :], rest[:, slot, :], parts[:, slot, 1, :],
                                            ALU.subtract).then_inc(s_lo, 1)
                for c in range(RU):
                    if c >= 3:
                        pool.wait_ge(s_kept[c % 3], 16 * (c // 3))
                    third(c % 3, c + 1)
                with pool.Fori(0, NBLK) as k:
                    for j in range(CPB):
                        c = RU + j
                        pool.wait_ge(s_kept[c % 3], (k * (CPB // 3) + c // 3) * 16)
                        third(c % 3, k * CPB + c + 1)

            @block.tensor
            def _(pe):
                pe.wait_ge(s_basis, 16)
                pe.wait_ge(s_wr, 16)
                for r in range(RU):
                    if r >= 4:
                        pe.wait_ge(s_full, r - 3)
                    for c in range(KC):
                        last = nc.tensor.matmul(pU[:, r % 4, :], wT[:, 3, c, (r % KC) * P:(r % KC + 1) * P],
                                                basis[:, c, (r // KC) * BLK:(r // KC + 1) * BLK],
                                                start=c == 0, stop=c == KC - 1)
                    last.then_inc(s_unit, 1)
                pe.wait_ge(s_w, 48)
                pe.wait_ge(t.s_ident, 16)

                with pe.Fori(0, NBLK) as k:
                    for pair in range(BT // 2):
                        for i in range(2):
                            tile = 2 * pair + i
                            pe.wait_ge(s_xhat, k * BT + tile + 1)
                            for c in range(KC):
                                last = nc.tensor.transpose(pT[:, pair, c, i, :],
                                                           xhat[:, tile, c * P:(c + 1) * P], t.ident[:, :])
                        last.then_inc(s_tr, 1)
                    pe.wait_ge(s_xT, k * 2 + 2)
                    for u in range(UPB):
                        pe.wait_ge(s_full, k * CPB + RU - CPB + [2, 4, 5, 6][u])
                        w, oc = u // KC, u % KC
                        for c in range(KC):
                            last = nc.tensor.matmul(pU[:, u, :], wT[:, w, c, oc * P:(oc + 1) * P],
                                                    xT[:, c, :], start=c == 0, stop=c == KC - 1)
                        last.then_inc(s_unit, 1)
                    for pair in range(BT // 2):
                        pe.wait_ge(s_vx, k * 2 + pair + 1)
                        for i in range(2):
                            for c in range(KC):
                                last = nc.tensor.matmul(pV[:, pair, i, :],
                                                        xT[:, c, (2 * pair + i) * P:(2 * pair + i + 1) * P],
                                                        wT[:, 2, c, :], start=c == 0, stop=c == KC - 1)
                        last.then_inc(s_v, 1)

            @block.scalar
            def _(act):
                def first(count, unit, bank, slot, scale, bias):
                    act.wait_ge(s_unit, unit)
                    if bias is None:
                        nc.scalar.activation(full[:, slot, :], pU[:, bank, :], ACT.Copy, scale=scale).then_inc(s_full, 1)
                    else:
                        nc.scalar.activation(full[:, slot, :], pU[:, bank, :], ACT.Identity, scale=scale,
                                             bias=bias).then_inc(s_full, 1)

                def second(count, slot):
                    act.wait_ge(s_rest, count)
                    nc.scalar.activation(parts[:, slot, 1, :], rest[:, slot, :], ACT.Copy).then_inc(s_mid, 1)

                for c in range(RU):
                    if c >= 3:
                        act.wait_ge(s_kept[c % 3], 16 * (c // 3))
                    first(c + 1, c + 1, c % 4, c % 3, 1.0, None)
                    second(c + 1, c % 3)
                act.wait_ge(s_const, 1)
                act.wait_ge(s_uvs, 1)
                with act.Fori(0, NBLK) as k:
                    act.wait_ge(s_mv, k + 1)
                    nc.scalar.activation(std[:, 0, :], mv[:, 0, :, 1], ACT.Sqrt, bias=epsc[:, :]).then_inc(s_std, 1)
                    for pair in range(BT // 2):
                        act.wait_ge(s_tr, k * 2 + pair + 1)
                        nc.scalar.activation(xT[:, :, pair * 2 * P:(pair + 1) * 2 * P],
                                             pT[:, pair, :, :, :].rearrange("p c i n -> p c (i n)"),
                                             ACT.Copy).then_inc(s_xT, 1)
                    for j, (u, operand, chunk) in enumerate(CUTS):
                        c = RU + j
                        act.wait_ge(s_kept[c % 3], (k * (CPB // 3) + c // 3) * 16)
                        bias = None if operand == KK else uvs[:, operand, chunk:chunk + 1]
                        first(None, k * UPB + RU + u + 1, u, c % 3, 1.0 if operand == KK else -0.25, bias)
                        second(k * CPB + c + 1, c % 3)

            @block.vector
            def _(dve):
                dve.wait_ge(s_uv, 16)
                nc.vector.tensor_scalar(uvs[:, :, :], uvcol[:, :, :], -0.25, None, ALU.mult).then_inc(s_uvs, 1)
                dve.sem_inc(s_vx, 2)

                def cut(count, slot):
                    dve.wait_ge(s_full, count)
                    nc.vector.tensor_copy(parts[:, slot, 0, :], full[:, slot, :]).then_inc(s_hi, 1)
                    dve.wait_ge(s_hi, count)
                    nc.vector.tensor_tensor(rest[:, slot, :], full[:, slot, :], parts[:, slot, 0, :],
                                            ALU.subtract).then_inc(s_rest, 1)
                for c in range(RU):
                    cut(c + 1, c % 3)
                for b in range(B):
                    dve.wait_ge(s_x[b], 16)
                dve.wait_ge(s_const, 2)
                with dve.Fori(0, NBLK) as k:
                    for i in range(BT):
                        nc.vector.bn_stats(stats[:, i, :], t.x[:, bass.ds(k * BT + i, 1), :])
                    nc.vector.drain()
                    for i in range(BT):
                        last = nc.vector.bn_aggr(mv[:, 0, i, :], stats[:, i, :])
                    last.then_inc(s_mv, 1)
                    dve.wait_ge(s_std, k + 1)
                    nc.vector.reciprocal(rstd[:, :], std[:, 0, :]).then_inc(s_rstd, 1)
                    dve.wait_ge(s_rstd, k + 1)
                    for i in range(BT):
                        nc.vector.tensor_scalar(xhat[:, i, :], t.x[:, bass.ds(k * BT + i, 1), :],
                                                mv[:, 0, i, 0:1], rstd[:, i:i + 1],
                                                ALU.subtract, ALU.mult).then_inc(s_xhat, 1)
                    for j in range(CPB):
                        cut(k * CPB + RU + j + 1, (RU + j) % 3)
                    for pair in range(BT // 2):
                        dve.wait_ge(s_v, k * 2 + pair + 1)
                        nc.vector.tensor_copy(
                            t.vx[:, bass.ds(k * BT + 2 * pair, 2), :, 0:DH],
                            pV[:, pair, :, :].rearrange("p i (h e) -> p i h e", e=DH)).then_inc(s_vx, 1)


def build_attention(nc, t, d):
    ctx = ExitStack()
    with ctx:
        def sb(name, shape, dt):
            return ctx.enter_context(nc.sbuf_tensor(name, shape, dt))

        def sem(name):
            return t.ctx.enter_context(nc.semaphore(name))

        QW = L + 2
        rp = sb("rp", [P, H, RW], bf16)
        qv = sb("qv", [P, 4, QW], bf16)
        qu = sb("qu", [P, 4, L], bf16)
        kk = sb("kk", [P, 4, L], bf16)
        ub = sb("ub", [P, 2, UW], fp32)
        bd = sb("bd", [P, 4, L], fp32)
        sc = sb("sc", [P, 4, L], fp32)
        pt = sb("pt", [P, 2, L], fp32)
        mn = sb("mn", [P, 4], fp32)
        rs = sb("rs", [P, TPB], fp32)
        on = sb("on", [P, TPB, VW], fp32)
        vh = sb("vh", [P, TPB, 32], fp32)
        pb = sb("pb", [P, 2, P], fp32)
        sel = sb("sel", [P, VW], fp32)
        pu = ctx.enter_context(nc.psum_tensor("pu", [P, 3, 512], fp32))
        pa = ctx.enter_context(nc.psum_tensor("pa", [P, L], fp32))
        pp = ctx.enter_context(nc.psum_tensor("pp", [P, 2, 512], fp32))
        po = ctx.enter_context(nc.psum_tensor("po", [P, 512], fp32))

        s_rp = sem("s_rp")
        s_pad = sem("s_pad")
        s_qv = sem("s_qv")
        s_kq = sem("s_kq")
        s_u = sem("s_u")
        s_ub = sem("s_ub")
        s_wr = [sem(f"s_wr{i}") for i in range(TPB)]
        s_rd = [sem(f"s_rd{i}") for i in range(4)]
        s_ac = sem("s_ac")
        s_sc = sem("s_sc")
        s_exp = sem("s_exp")
        s_tr = sem("s_trp")
        s_pt = sem("s_pt")
        s_pv = sem("s_pv")
        s_fin = sem("s_fin")
        s_sel = sem("s_sel")
        s_vh = sem("s_vh")
        s_pb = sem("s_pb")
        s_comb = sem("s_comb")
        s_fs = sem("s_fs")
        s_go = sem("s_go")
        s_sp = sem("s_sp")

        ring = d["ring"]

        def steps(eng, step):
            step(0, True, False, False)
            step(1, True, True, False)
            with eng.Fori(2, NH) as m:
                step(m, True, True, True)
            step(NH, False, True, True)

        with nc.Block() as block:
            @block.gpsimd
            def _(pool):
                nc.gpsimd.memset(qv[:, :, L:QW], 0.0).then_inc(s_pad, 1)
                nc.gpsimd.memset(vh[:, :, :], 0.0).then_inc(s_pad, 1)

                def load(dst, operand, two, side, s):
                    b, h = two // (H // 2), two % (H // 2)
                    for g, term in enumerate(TERMS):
                        pool.dma_start(dst[g * DH:(g + 1) * DH, bass.ds(two % 2 * 2, 2), 0:L],
                                       d["qsplit"][operand, term[side], bass.ds(h * 2 * DH, 2 * DH),
                                                   bass.ds(b * L, L)].rearrange("(a e) n -> e a n", e=DH)).then_inc(s, 16)
                load(qv, QV, 0, 0, s_qv)
                for g, term in enumerate(TERMS):
                    pool.dma_start(rp[g * DH:(g + 1) * DH, :, :],
                                   d["rsplit"][term[1], :, :].rearrange("(h e) n -> e h n", e=DH)).then_inc(s_rp, 16)
                load(kk, KK, 0, 1, s_kq)
                load(qu, QU, 0, 0, s_kq)
                with pool.Fori(0, NH // 2 - 1) as two:
                    pool.wait_ge(s_u, two * 2 * TPB + 1)
                    load(qv, QV, two + 1, 0, s_qv)
                    pool.wait_ge(s_ac, two * 2 * TPB + 1)
                    load(kk, KK, two + 1, 1, s_kq)
                    load(qu, QU, two + 1, 0, s_kq)

            @block.sync
            def _(sp):
                sp.dma_start(sel[:, :], d["sel"]).then_inc(s_sel, 16)

                def step(m, ahead, main, tail):
                    for it in range(TPB):
                        r = (it + 3) % TPB
                        n = m - 1 if it + 3 < TPB else m
                        reads = it + 3 < TPB and main or it + 3 >= TPB and ahead
                        reused = reads and (it + 3 < TPB or main) and (type(n) is not int or n * TPB + r >= 4)
                        if ahead:
                            sp.wait_ge(s_ub, m * TPB + it + 1)
                            sp.sem_inc(s_sp, 1)
                            if main:
                                sp.wait_ge(s_rd[it % 4], (m * 2 - 1 + it // 4) * 16)
                            sp.dma_start(ring[it, :, :], ub[:, it % 2, :]).then_inc(s_wr[it], 16)
                        if reads:
                            sp.wait_ge(s_wr[r], (n + 1) * 16)
                            sp.sem_inc(s_sp, 1)
                            if reused:
                                sp.wait_ge(s_sc, n * TPB + r - 3)
                            skew = ring[r, :, :].rearrange("p w -> (p w)")[P - 1:P - 1 + P * (UW - 1)]
                            sp.dma_start(bd[:, r % 4, :],
                                         skew.rearrange("(p w) -> p w", p=P)[:, 0:L]).then_inc(s_rd[r % 4], 16)
                steps(sp, step)

            @block.tensor
            def _(pe):
                pe.wait_ge(s_rp, 128)
                pe.wait_ge(s_pad, 1)
                pe.wait_ge(s_sel, 16)
                pe.wait_ge(t.s_ident, 16)

                def unshifted(m, h, par, it):
                    i0 = it * P
                    edge = i0 + P
                    if type(m) is not int or m * TPB + it > 0:
                        pe.wait_ge(s_ub, m * TPB + it)
                    cuts = sorted({0, UB, 2 * UB, UW, edge})
                    for a, b in zip(cuts, cuts[1:]):
                        low = a < edge
                        col = RW - edge + a if low else a - edge
                        row = i0 if low else i0 + 1
                        last = nc.tensor.matmul(pu[:, a // UB, a % UB:a % UB + b - a],
                                                qv[:, par, row:row + P],
                                                rp[:, h, col:col + b - a], start=True, stop=True)
                    last.then_inc(s_u, 1)

                def scores(n, par, it):
                    if type(n) is not int or n * TPB + it > 0:
                        pe.wait_ge(s_sc, n * TPB + it)
                    for c in range(2):
                        last = nc.tensor.matmul(pa[:, c * 512:(c + 1) * 512], qu[:, par, it * P:(it + 1) * P],
                                                kk[:, par, c * 512:(c + 1) * 512], start=True, stop=True)
                    last.then_inc(s_ac, 1)

                def transposes(n, it):
                    g = n * TPB + it
                    pe.wait_ge(s_exp, g + 1)
                    for c in range(2):
                        if type(n) is not int or g > 0:
                            pe.wait_ge(s_pt, g * 2 - 1 + c)
                        for j in range(4):
                            last = nc.tensor.transpose(pp[:, c, j * P:(j + 1) * P],
                                                       sc[:, it % 4, (4 * c + j) * P:(4 * c + j + 1) * P],
                                                       t.ident[:, :])
                        last.then_inc(s_tr, 1)

                def weighted(n, it):
                    g = n * TPB + it
                    pe.wait_ge(s_pt, g * 2 + 2)
                    if it == 0:
                        pe.wait_ge(s_vh, n + 1)
                        if type(n) is not int or n > 0:
                            pe.wait_ge(s_fin, n)
                    if type(n) is not int or g > 0:
                        pe.wait_ge(s_pb, g)
                    for j in range(TPB):
                        c = 32 * (j % 4)
                        last = nc.tensor.matmul(po[c:c + 32, 0:P], vh[:, j, :], pt[:, it % 2, j * P:(j + 1) * P],
                                                start=j < 4, stop=j >= 4)
                    last.then_inc(s_pv, 1)

                def combine(n, it):
                    pe.wait_ge(s_pb, n * TPB + it + 1)
                    nc.tensor.matmul(po[:, P + it * VW:P + (it + 1) * VW], pb[:, it % 2, :], sel[:, :],
                                     start=True, stop=True).then_inc(s_comb, 1)

                def dyn(x):
                    return x if type(x) is int else bass.ds(x, 1)

                def step(m, ahead, main, tail):
                    if ahead:
                        pe.wait_ge(s_qv, (m // 2 + 1) * 128)
                    if main:
                        pe.wait_ge(s_kq, ((m + 1) // 2) * 256)
                    n = m - 1
                    for it in range(TPB):
                        late = [(n, it - 2)] if it >= 2 and main else [(n - 1, it + 6)] if it < 2 and tail else []
                        for nn, i in late:
                            transposes(nn, i)
                        if ahead:
                            unshifted(m, dyn(m % H), dyn(m % 4), it)
                        if main:
                            scores(n, dyn(n % 4), it)
                        if it >= 3 and main:
                            combine(n, it - 3)
                        if it < 3 and tail:
                            combine(n - 1, it + 5)
                        for nn, i in late:
                            weighted(nn, i)
                steps(pe, step)
                for i in (TPB - 2, TPB - 1):
                    transposes(NH - 1, i)
                    combine(NH - 1, i - 1)
                    weighted(NH - 1, i)
                combine(NH - 1, TPB - 1)

            @block.scalar
            def _(act):
                def exponential(n, it):
                    act.wait_ge(s_sc, n * TPB + it + 1)
                    nc.scalar.activation(sc[:, it % 4, :], sc[:, it % 4, :], ACT.Exp, scale=-1.0,
                                         bias=mn[:, it % 4:it % 4 + 1]).then_inc(s_exp, 1)

                def step(m, ahead, main, tail):
                    for it in range(TPB):
                        if it >= 1 and main:
                            exponential(m - 1, it - 1)
                        if it == 0 and tail:
                            exponential(m - 2, TPB - 1)
                        if ahead:
                            act.wait_ge(s_u, m * TPB + it + 1)
                            if it >= 2 or main:
                                act.wait_ge(s_wr[(it - 2) % TPB], (m + (1 if it >= 2 else 0)) * 16)
                            nc.scalar.activation(ub[:, it % 2, :].rearrange("p (c n) -> p c n", c=3),
                                                 pu[:, :, 0:UB], ACT.Copy).then_inc(s_ub, 1)
                steps(act, step)
                exponential(NH - 1, TPB - 1)

            @block.vector
            def _(dve):
                dve.wait_ge(s_pad, 2)

                def evacuate(n, it):
                    g = n * TPB + it
                    for c in range(2):
                        dve.wait_ge(s_tr, g * 2 + c + 1)
                        if c == 0 and (type(n) is not int or g >= 2):
                            dve.wait_ge(s_pv, g - 1)
                        nc.vector.tensor_copy(pt[:, it % 2, c * 512:(c + 1) * 512], pp[:, c, :]).then_inc(s_pt, 1)

                def total(n, it):
                    g = n * TPB + it
                    dve.wait_ge(s_ac, g + 1)
                    dve.wait_ge(s_rd[it % 4], (n * 2 + it // 4 + 1) * 16)
                    if type(n) is not int or g >= 4:
                        dve.wait_ge(s_tr, g * 2 - 6)
                    dve.sem_inc(s_go, 1)
                    nc.vector.tensor_tensor_reduce(out=sc[:, it % 4, :], in0=pa[:, :], in1=bd[:, it % 4, :],
                                                   scale=1.0, scalar=3e38, op0=ALU.add, op1=ALU.min,
                                                   accum_out=mn[:, it % 4:it % 4 + 1]).then_inc(s_sc, 1)

                def partials(n, it):
                    g = n * TPB + it
                    dve.wait_ge(s_pv, g + 1)
                    if type(n) is not int or g >= 2:
                        dve.wait_ge(s_comb, g - 1)
                    nc.vector.tensor_copy(pb[:, it % 2, :], po[:, 0:P]).then_inc(s_pb, 1)

                def values(n):
                    if type(n) is not int or n > 0:
                        dve.wait_ge(s_pv, n * TPB)
                    nc.vector.tensor_copy(vh[:, :, 0:VW].unsqueeze(2),
                                          t.vx[:, bass.ds((n // H) * TPB, TPB), bass.ds(n % H, 1), :]).then_inc(s_vh, 1)

                def finish(n):
                    dve.wait_ge(s_comb, n * TPB + TPB)
                    nc.vector.tensor_copy(on[:, :, :], po[:, P:P + TPB * VW].rearrange("p (i e) -> p i e", e=VW))\
                      .then_inc(s_fin, 1)
                    dve.wait_ge(s_fin, n + 1)
                    nc.vector.reciprocal(rs[:, :], on[:, :, DH]).then_inc(s_fs, 1)
                    dve.wait_ge(s_fs, n * 3 + 1)
                    nc.vector.tensor_tensor(on[:, :, 0:DH], on[:, :, 0:DH],
                                            rs[:, :].unsqueeze(2).to_broadcast([P, TPB, DH]), ALU.mult).then_inc(s_fs, 1)
                    dve.wait_ge(s_fs, n * 3 + 2)
                    xs = t.x[:, bass.ds((n // H) * TPB, TPB), bass.ds((n % H) * DH, DH)]
                    nc.vector.tensor_tensor(xs, xs, on[:, :, 0:DH], ALU.add).then_inc(s_fs, 1)

                def step(m, ahead, main, tail):
                    for it in range(TPB):
                        if it == 2 and main:
                            values(m - 1)
                        if it >= 2 and main:
                            evacuate(m - 1, it - 2)
                        if it < 2 and tail:
                            evacuate(m - 2, it + 6)
                        if main:
                            total(m - 1, it)
                        if it == 2 and tail:
                            finish(m - 2)
                        if it >= 2 and main:
                            partials(m - 1, it - 2)
                        if it < 2 and tail:
                            partials(m - 2, it + 6)
                steps(dve, step)
                for i in (TPB - 2, TPB - 1):
                    evacuate(NH - 1, i)
                    partials(NH - 1, i)
                finish(NH - 1)


def normalise(nc, dve, x, mv, rstd, xhat, tile, i):
    return nc.vector.tensor_scalar(xhat[:, i, :], x[:, bass.ds(tile, 1), :], mv[:, i, 0:1], rstd[:, i:i + 1],
                                   ALU.subtract, ALU.mult)


def build_cross_queries(nc, t, d):
    ctx = ExitStack()
    with ctx:
        def sb(name, shape, dt):
            return ctx.enter_context(nc.sbuf_tensor(name, shape, dt))

        def pb(name, shape, dt):
            return ctx.enter_context(nc.psum_tensor(name, shape, dt))

        def sem(name):
            return t.ctx.enter_context(nc.semaphore(name))

        G = BT * H
        w = sb("xw", [P, 3, KC, D], fp32)
        cx = sb("cx", [S2, B, D], fp32)
        cT = sb("cT", [P, KC, B * S2], fp32)
        ks = sb("ks", [S2, B * H, DH], fp32)
        ksq = sb("ksq", [S2, B * H, DH], fp32)
        k1 = sb("k1", [S2, B * H], fp32)
        k2 = sb("k2", [S2, B * H], fp32)
        kT = sb("kT", [P, KC, B, S2], fp32)
        hm = sb("hm", [P, H // KC], fp32)
        epsc = sb("xepsc", [P, 1], fp32)
        stats = sb("xstats", [P, BT, 6], fp32)
        mv = sb("xmv", [P, BT, 2], fp32)
        std = sb("xstd", [P, BT], fp32)
        rstd = sb("xrstd", [P, BT], fp32)
        xhat = sb("xxhat", [P, BT, D], fp32)
        xT = sb("xxT", [P, KC, BLK], fp32)
        qc = sb("qc", [P, G, DH], fp32)
        qs = sb("qs", [P, G, DH], fp32)
        m1 = sb("m1", [P, G], fp32)
        m2 = sb("m2", [P, G], fp32)
        m3 = sb("m3", [P, G], fp32)
        pC = pb("pC", [P, KC, 512], fp32)
        pK = pb("pK", [S2, B, D], fp32)
        pT = pb("xpT", [P, KC, BLK], fp32)
        pQ = pb("pQ", [P, BT, D], fp32)

        s_w = sem("x_weights")
        s_c = sem("x_context")
        s_cols = sem("x_cols")
        s_const = sem("x_const")
        s_cT = sem("x_cT")
        s_cTs = sem("x_cTs")
        s_k = sem("x_k")
        s_ks = sem("x_ks")
        s_kd = sem("x_kd")
        s_ka = sem("x_ka")
        s_v = sem("x_v")
        s_vs = sem("x_vs")
        s_kt = sem("x_kt")
        s_mv = sem("x_mv")
        s_std = sem("x_std")
        s_rstd = sem("x_rstd")
        s_xhat = sem("x_xhat")
        s_tr = sem("x_tr")
        s_xT = sem("x_xT")
        s_q = sem("x_q")
        s_qd = sem("x_qd")
        s_sq = sem("x_sq")
        s_qstd = sem("x_qstd")
        s_qm = sem("x_qm")
        s_qh = sem("x_qh")

        def heads(v, parts, n):
            return v.unsqueeze(2).to_broadcast([parts, n, DH])

        with nc.Block() as block:
            @block.sync
            def _(sp):
                sp.dma_start(cx[:, :, :], d["ctx"].rearrange("b s e -> s b e")).then_inc(s_c, 16)
                for i, n in enumerate(("xwq", "xwk", "xwv")):
                    sp.dma_start(w[:, i, :, :], d[n].rearrange("(c p) o -> p c o", p=P)).then_inc(s_w, 16)
                sp.dma_start(t.lncol[:, :], d["lncol"]).then_inc(s_cols, 16)
                sp.dma_start(hm[:, :], d["headmask"]).then_inc(s_cols, 16)

            @block.gpsimd
            def _(pool):
                nc.gpsimd.memset(epsc[:, :], EPS).then_inc(s_const, 1)
                nc.gpsimd.memset(t.cv[:, :, :, :], 1.0).then_inc(s_const, 1)
                with pool.Fori(0, NBLK) as k:
                    pool.wait_ge(s_qm, k + 1)
                    nc.gpsimd.tensor_tensor(t.q[:, bass.ds(k * BT, BT), :].rearrange("p t (h e) -> p (t h) e", e=DH),
                                            qc[:, :, :], heads(m3[:, :], P, G), ALU.mult).then_inc(s_qh, 1)

            @block.tensor
            def _(pe):
                pe.wait_ge(s_c, 16)
                for c in range(KC):
                    for b in range(B):
                        last = nc.tensor.transpose(pC[:, c, b * S2:(b + 1) * S2], cx[:, b, c * P:(c + 1) * P],
                                                   t.ident[0:S2, 0:S2])
                last.then_inc(s_cT, 1)
                pe.wait_ge(s_w, 48)
                pe.wait_ge(s_cTs, 1)
                for i in (1, 2):
                    if i == 2:
                        pe.wait_ge(s_ks, 1)
                    for b in range(B):
                        for c in range(KC):
                            last = nc.tensor.matmul(pK[:, b, :], cT[:, c, b * S2:(b + 1) * S2], w[:, i, c, :],
                                                    start=c == 0, stop=c == KC - 1)
                    last.then_inc(s_k if i == 1 else s_v, 1)
                pe.wait_ge(s_kd, 6)
                for c in range(KC):
                    for b in range(B):
                        last = nc.tensor.transpose(pC[:, c, b * S2:(b + 1) * S2],
                                                   ks[:, b * H + c * H // KC:b * H + (c + 1) * H // KC, :]
                                                   .rearrange("s h e -> s (h e)"), t.ident[0:S2, 0:S2])
                last.then_inc(s_kt, 1)
                with pe.Fori(0, NBLK) as k:
                    for i in range(BT):
                        pe.wait_ge(s_xhat, k * BT + i + 1)
                        for c in range(KC):
                            last = nc.tensor.transpose(pT[:, c, i * P:(i + 1) * P], xhat[:, i, c * P:(c + 1) * P],
                                                       t.ident[:, :])
                    last.then_inc(s_tr, 1)
                    pe.wait_ge(s_xT, k + 1)
                    pe.wait_ge(s_qd, k * 4 + 1)
                    for i in range(BT):
                        for c in range(KC):
                            last = nc.tensor.matmul(pQ[:, i, :], xT[:, c, i * P:(i + 1) * P], w[:, 0, c, :],
                                                    start=c == 0, stop=c == KC - 1)
                    last.then_inc(s_q, 1)

            @block.scalar
            def _(act):
                act.wait_ge(s_cT, 1)
                nc.scalar.activation(cT[:, :, :], pC[:, :, 0:B * S2], ACT.Copy).then_inc(s_cTs, 1)
                act.wait_ge(s_kd, 3)
                nc.scalar.activation(ksq[:, :, :], ks[:, :, :], ACT.Square).then_inc(s_ka, 1)
                act.wait_ge(s_kd, 4)
                act.wait_ge(s_const, 2)
                nc.scalar.activation(k2[:, :], k1[:, :], ACT.Sqrt, scale=1.0 / DH, bias=epsc[0:S2, :]).then_inc(s_ka, 1)
                act.wait_ge(s_v, 1)
                nc.scalar.activation(t.cv[:, :, :, 0:DH], pK[:, :, :].rearrange("s b (h e) -> s b h e", e=DH),
                                     ACT.Copy).then_inc(s_vs, 1)
                with act.Fori(0, NBLK) as k:
                    act.wait_ge(s_mv, k + 1)
                    nc.scalar.activation(std[:, :], mv[:, :, 1], ACT.Sqrt, bias=epsc[:, :]).then_inc(s_std, 1)
                    act.wait_ge(s_tr, k + 1)
                    nc.scalar.activation(xT[:, :, :], pT[:, :, :], ACT.Copy).then_inc(s_xT, 1)
                    act.wait_ge(s_qd, k * 4 + 4)
                    nc.scalar.activation(qs[:, :, :], qc[:, :, :], ACT.Square).then_inc(s_sq, 1)
                    act.wait_ge(s_qd, k * 4 + 5)
                    nc.scalar.activation(m2[:, :], m1[:, :], ACT.Sqrt, scale=1.0 / DH, bias=epsc[:, :]).then_inc(s_qstd, 1)

            @block.vector
            def _(dve):
                dve.wait_ge(s_k, 1)
                kp = pK[:, :, :].rearrange("s b (h e) -> s (b h) e", e=DH)
                nc.vector.tensor_reduce(k1[:, :], kp, AX.X, ALU.add).then_inc(s_kd, 1)
                dve.wait_ge(s_kd, 1)
                nc.vector.tensor_scalar(k2[:, :], k1[:, :], 1.0 / DH, None, ALU.mult).then_inc(s_kd, 1)
                dve.wait_ge(s_kd, 2)
                nc.vector.tensor_tensor(ks[:, :, :], kp, heads(k2[:, :], S2, B * H), ALU.subtract).then_inc(s_kd, 1)
                dve.wait_ge(s_kd, 3)
                dve.sem_inc(s_ks, 1)
                dve.wait_ge(s_ka, 1)
                nc.vector.tensor_reduce(k1[:, :], ksq[:, :, :], AX.X, ALU.add).then_inc(s_kd, 1)
                dve.wait_ge(s_ka, 2)
                nc.vector.reciprocal(k1[:, :], k2[:, :]).then_inc(s_kd, 1)
                dve.wait_ge(s_kd, 5)
                nc.vector.tensor_tensor(ks[:, :, :], ks[:, :, :], heads(k1[:, :], S2, B * H), ALU.mult).then_inc(s_kd, 1)
                dve.wait_ge(s_kt, 1)
                dve.wait_ge(s_cols, 32)
                nc.vector.tensor_scalar(kT[:, :, :, :].rearrange("p c b s -> p c (b s)"), pC[:, :, 0:B * S2],
                                        t.lncol[:, 2:3], t.lncol[:, 3:4], ALU.mult, ALU.add).then_inc(s_kd, 1)
                dve.wait_ge(s_kd, 7)
                for c in range(KC):
                    for b in range(B):
                        nc.vector.tensor_tensor(t.kbd[:, c, b, :, :],
                                                kT[:, c, b:b + 1, :].to_broadcast([P, H // KC, S2]),
                                                hm[:, :].unsqueeze(2).to_broadcast([P, H // KC, S2]), ALU.mult)
                dve.sem_inc(s_qd, 1)
                with dve.Fori(0, NBLK) as k:
                    for i in range(BT):
                        nc.vector.bn_stats(stats[:, i, :], t.x[:, bass.ds(k * BT + i, 1), :])
                    nc.vector.drain()
                    for i in range(BT):
                        last = nc.vector.bn_aggr(mv[:, i, :], stats[:, i, :])
                    last.then_inc(s_mv, 1)
                    dve.wait_ge(s_std, k + 1)
                    nc.vector.reciprocal(rstd[:, :], std[:, :]).then_inc(s_rstd, 1)
                    dve.wait_ge(s_rstd, k + 1)
                    for i in range(BT):
                        normalise(nc, dve, t.x, mv, rstd, xhat, k * BT + i, i).then_inc(s_xhat, 1)
                    dve.wait_ge(s_q, k + 1)
                    qp = pQ[:, :, :].rearrange("p t (h e) -> p (t h) e", e=DH)
                    nc.vector.tensor_reduce(m1[:, :], qp, AX.X, ALU.add).then_inc(s_qd, 1)
                    dve.wait_ge(s_qd, k * 4 + 2)
                    nc.vector.tensor_scalar(m3[:, :], m1[:, :], 1.0 / DH, None, ALU.mult).then_inc(s_qd, 1)
                    dve.wait_ge(s_qd, k * 4 + 3)
                    nc.vector.tensor_tensor(qc[:, :, :], qp, heads(m3[:, :], P, G), ALU.subtract).then_inc(s_qd, 1)
                    dve.wait_ge(s_sq, k + 1)
                    nc.vector.tensor_reduce(m1[:, :], qs[:, :, :], AX.X, ALU.add).then_inc(s_qd, 1)
                    dve.wait_ge(s_qstd, k + 1)
                    nc.vector.reciprocal(m3[:, :], m2[:, :]).then_inc(s_qm, 1)
                    dve.wait_ge(s_qh, k + 1)


def build_cross_attention(nc, t, d):
    ctx = ExitStack()
    with ctx:
        def sb(name, shape, dt):
            return ctx.enter_context(nc.sbuf_tensor(name, shape, dt))

        def pb(name, shape, dt):
            return ctx.enter_context(nc.psum_tensor(name, shape, dt))

        def sem(name):
            return t.ctx.enter_context(nc.semaphore(name))

        HC = H // KC
        UN = TPB * KC
        wo = sb("wo", [P, KC, D], fp32)
        bo = sb("bo", [P, D], fp32)
        mask = sb("mask", [P, S2], fp32)
        qt = sb("qt", [P, 2, D], fp32)
        od = sb("od", [P, 2, D], fp32)
        qT = sb("qT", [P, 2, KC, P], fp32)
        ss = sb("ss", [P, 3, HC, S2], fp32)
        mx = sb("mx", [P, 2, HC], fp32)
        pT = sb("ypT", [S2, 2, HC, P], fp32)
        on = sb("yon", [P, 2, H, VW], fp32)
        rr = sb("yrr", [P, 2, H], fp32)
        oT = sb("oT", [P, 2, KC, P], fp32)
        pq = pb("pq", [P, 512], fp32)
        ps = pb("yps", [P, 2, 512], fp32)
        pt = pb("ypt", [S2, 2, 512], fp32)
        po = pb("ypo", [P, 512], fp32)
        pot = pb("pot", [P, 512], fp32)
        pw = pb("pw", [P, 512], fp32)

        s_ld = sem("y_loads")
        s_xb = sem("y_xb")
        s_take = sem("y_take")
        s_qt = sem("y_qt")
        s_qts = sem("y_qts")
        s_s = sem("y_s")
        s_mx = sem("y_mx")
        s_sub = sem("y_sub")
        s_exp = sem("y_exp")
        s_pt = sem("y_pt")
        s_pts = sem("y_pts")
        s_o = sem("y_o")
        s_on = sem("y_on")
        s_rr = sem("y_rr")
        s_norm = sem("y_norm")
        s_ot = sem("y_ot")
        s_ots = sem("y_ots")
        s_w = sem("y_w")
        s_add = sem("y_add")
        s_go = sem("y_go")

        with nc.Block() as block:
            @block.sync
            def _(sp):
                sp.dma_start(wo[:, :, :], d["xwo"].rearrange("(c p) o -> p c o", p=P)).then_inc(s_ld, 16)
                sp.dma_start(bo[:, :], d["bo"].partition_broadcast(P)).then_inc(s_ld, 16)
                sp.dma_start(mask[:, :], d["mask"]).then_inc(s_ld, 16)

            @block.gpsimd
            def _(pool):
                pool.wait_ge(s_ld, 48)
                for b in range(B):
                    nc.gpsimd.tensor_tensor(t.x[:, b * TPB:(b + 1) * TPB, :], t.x[:, b * TPB:(b + 1) * TPB, :],
                                            bo[:, :].unsqueeze(1).to_broadcast([P, TPB, D]), ALU.add).then_inc(s_xb, 1)

            @block.tensor
            def _(pe):
                pe.wait_ge(s_ld, 48)
                with pe.Fori(0, B) as b:
                    def queries(tile):
                        if tile > 0:
                            pe.wait_ge(s_qts, b * TPB + tile)
                        for c in range(KC):
                            last = nc.tensor.transpose(pq[:, c * P:(c + 1) * P], qt[:, tile % 2, c * P:(c + 1) * P],
                                                       t.ident[:, :])
                        last.then_inc(s_qt, 1)

                    def scores(u):
                        tile, c = u // KC, u % KC
                        pe.wait_ge(s_qts, b * TPB + tile + 1)
                        if u > 0:
                            pe.wait_ge(s_sub, b * UN + u)
                        for j in range(2):
                            last = nc.tensor.matmul(ps[:, j, 0:HC // 2 * S2], qT[:, tile % 2, c, :],
                                                    t.kbd[:, c, bass.ds(b, 1), j * HC // 2:(j + 1) * HC // 2, :],
                                                    start=True, stop=True)
                        last.then_inc(s_s, 1)

                    def transposes(u):
                        pe.wait_ge(s_exp, b * UN + u + 1)
                        if u > 0:
                            pe.wait_ge(s_pts, b * UN + u)
                        for h in range(HC):
                            last = nc.tensor.transpose(pt[:, h // 4, h % 4 * P:(h % 4 + 1) * P], ss[:, u % 3, h, :],
                                                       t.ident[:, :])
                        last.then_inc(s_pt, 1)

                    def weighted(u):
                        tile, c = u // KC, u % KC
                        pe.wait_ge(s_pts, b * UN + u + 1)
                        if c == 0 and tile > 0:
                            pe.wait_ge(s_on, b * TPB + tile)
                        for h in range(HC):
                            last = nc.tensor.matmul(po[:, (c * HC + h) * VW:(c * HC + h + 1) * VW],
                                                    pT[:, u % 2, h, :],
                                                    t.cv[:, bass.ds(b, 1), c * HC + h, :], start=True, stop=True)
                        last.then_inc(s_o, 1)

                    def turned(tile):
                        pe.wait_ge(s_norm, b * TPB + tile + 1)
                        if tile > 0:
                            pe.wait_ge(s_ots, b * TPB + tile)
                        for c in range(KC):
                            last = nc.tensor.transpose(pot[:, c * P:(c + 1) * P],
                                                       od[:, tile % 2, c * P:(c + 1) * P], t.ident[:, :])
                        last.then_inc(s_ot, 1)

                    def output(tile):
                        pe.wait_ge(s_ots, b * TPB + tile + 1)
                        if tile > 0:
                            pe.wait_ge(s_add, b * TPB + tile)
                        for c in range(KC):
                            last = nc.tensor.matmul(pw[:, 0:D], oT[:, tile % 2, c, :], wo[:, c, :],
                                                    start=c == 0, stop=c == KC - 1)
                        last.then_inc(s_w, 1)

                    for u in range(UN + 8):
                        if u % 2 == 0 and u // 2 < TPB:
                            pe.wait_ge(s_take, b * TPB + u // 2 + 1)
                            queries(u // 2)
                        if u < UN:
                            scores(u)
                        if 1 <= u <= UN:
                            transposes(u - 1)
                        if 2 <= u <= UN + 1:
                            weighted(u - 2)
                        if u % 2 == 1 and 0 <= (u - 5) // 2 < TPB and u >= 5:
                            turned((u - 5) // 2)
                        if u % 2 == 1 and 0 <= (u - 7) // 2 < TPB and u >= 7:
                            output((u - 7) // 2)

            @block.scalar
            def _(act):
                with act.Fori(0, B) as b:
                    for u in range(UN + 8):
                        if u % 2 == 0 and u // 2 < TPB:
                            tile = u // 2
                            act.wait_ge(s_qt, b * TPB + tile + 1)
                            nc.scalar.activation(qT[:, tile % 2, :, :], pq[:, 0:KC * P].rearrange("p (c n) -> p c n", c=KC),
                                                 ACT.Identity, scale=t.lncol[:, 0:1], bias=t.lncol[:, 1:2]).then_inc(s_qts, 1)
                        if u < UN:
                            act.wait_ge(s_sub, b * UN + u + 1)
                            nc.scalar.activation(ss[:, u % 3, :, :], ss[:, u % 3, :, :], ACT.Exp,
                                                 scale=D ** -0.5).then_inc(s_exp, 1)
                        if 1 <= u <= UN:
                            act.wait_ge(s_pt, b * UN + u)
                            nc.scalar.activation(pT[:, (u - 1) % 2, :, :].rearrange("s (j h) n -> s j (h n)", j=2),
                                                 pt[:, :, :], ACT.Copy).then_inc(s_pts, 1)
                        if u % 2 == 1 and 0 <= (u - 5) // 2 < TPB and u >= 5:
                            tile = (u - 5) // 2
                            act.wait_ge(s_ot, b * TPB + tile + 1)
                            nc.scalar.activation(oT[:, tile % 2, :, :], pot[:, 0:KC * P].rearrange("p (c n) -> p c n", c=KC),
                                                 ACT.Copy).then_inc(s_ots, 1)

            @block.vector
            def _(dve):
                dve.wait_ge(s_ld, 48)
                with dve.Fori(0, B) as b:
                    def take(tile):
                        if tile >= 2:
                            dve.wait_ge(s_qt, b * TPB + tile - 1)
                        nc.vector.tensor_copy(qt[:, tile % 2:tile % 2 + 1, :],
                                              t.q[:, bass.ds(b * TPB + tile, 1), :]).then_inc(s_take, 1)
                    take(0)
                    for u in range(UN + 8):
                        if u % 2 == 0 and u // 2 + 1 < TPB:
                            take(u // 2 + 1)
                        if u < UN:
                            tile = u // KC
                            dve.wait_ge(s_s, b * UN + u + 1)
                            if u >= 3:
                                dve.wait_ge(s_pt, b * UN + u - 2)
                            sp4 = ps[:, :, 0:HC // 2 * S2].rearrange("p j (h s) -> p j h s", s=S2)
                            out4 = ss[:, u % 3, :, :].rearrange("p (j h) s -> p j h s", j=2)
                            if tile == 0:
                                m4 = mask[:, :].unsqueeze(1).to_broadcast([P, HC // 2, S2])
                                for j in range(2):
                                    nc.vector.tensor_tensor(out4[:, j, :, :], sp4[:, j, :, :], m4, ALU.add).then_inc(s_go, 1)
                                dve.wait_ge(s_go, b * 4 + u * 2 + 2)
                                src = out4
                            else:
                                src = sp4
                            nc.vector.tensor_reduce(mx[:, u % 2, :].rearrange("p (j h) -> p j h", j=2), src, AX.X,
                                                    ALU.max).then_inc(s_mx, 1)
                            dve.wait_ge(s_mx, b * UN + u + 1)
                            for j in range(2):
                                last = nc.vector.tensor_tensor(
                                    out4[:, j, :, :], src[:, j, :, :],
                                    mx[:, u % 2, j * HC // 2:(j + 1) * HC // 2].unsqueeze(2).to_broadcast([P, HC // 2, S2]),
                                    ALU.subtract)
                            last.then_inc(s_sub, 1)
                        if u % 2 == 0 and u >= 4 and (u - 4) // 2 < TPB:
                            tile = (u - 4) // 2
                            dve.wait_ge(s_o, b * UN + 2 * tile + 2)
                            nc.vector.tensor_copy(on[:, tile % 2, :, :],
                                                  po[:, 0:H * VW].rearrange("p (h e) -> p h e", e=VW)).then_inc(s_on, 1)
                            dve.wait_ge(s_on, b * TPB + tile + 1)
                            nc.vector.reciprocal(rr[:, tile % 2, :], on[:, tile % 2, :, DH]).then_inc(s_rr, 1)
                            dve.wait_ge(s_rr, b * TPB + tile + 1)
                            if tile >= 2:
                                dve.wait_ge(s_ot, b * TPB + tile - 1)
                            nc.vector.tensor_tensor(od[:, tile % 2, :].rearrange("p (h e) -> p h e", e=DH),
                                                    on[:, tile % 2, :, 0:DH],
                                                    rr[:, tile % 2, :].unsqueeze(2).to_broadcast([P, H, DH]),
                                                    ALU.mult).then_inc(s_norm, 1)
                        if u % 2 == 0 and u >= 8 and (u - 8) // 2 < TPB:
                            tile = (u - 8) // 2
                            if tile == 0:
                                dve.wait_ge(s_xb, b + 1)
                            dve.wait_ge(s_w, b * TPB + tile + 1)
                            xs = t.x[:, bass.ds(b * TPB + tile, 1), :]
                            nc.vector.tensor_tensor(xs, xs, pw[:, 0:D].unsqueeze(1), ALU.add).then_inc(s_add, 1)


def build_experts(nc, t, d):
    ctx = ExitStack()
    with ctx:
        def sb(name, shape, dt):
            return ctx.enter_context(nc.sbuf_tensor(name, shape, dt))

        def pb(name, shape, dt):
            return ctx.enter_context(nc.psum_tensor(name, shape, dt))

        def sem(name):
            return t.ctx.enter_context(nc.semaphore(name))

        NE = E + 1
        F2 = F // 2
        wg = sb("wg", [P, NE, KC, F], fp32)
        wu = sb("wu", [P, NE, KC, F], fp32)
        wd = sb("wd", [F2, NE, 2, D], fp32)
        wr = sb("zwr", [P, KC, E], fp32)
        eb = sb("eb", [P, E], fp32)
        order = sb("order", [P, E], fp32)
        epsc = sb("zepsc", [P, 1], fp32)
        stats = sb("zstats", [P, BT, 6], fp32)
        mv = sb("zmv", [P, BT, 2], fp32)
        std = sb("zstd", [P, BT], fp32)
        rstd = sb("zrstd", [P, BT], fp32)
        xhat = sb("zxhat", [P, BT, D], fp32)
        xT = sb("zxT", [P, NBLK, KC, BLK], fp32)
        xb = sb("zxb", [P, KC, BLK], fp32)
        s0 = sb("s0", [P, NT, E], fp32)
        s1 = sb("s1", [P, NT, E], fp32)
        c1 = sb("c1", [P, NT, E], fp32)
        o1 = sb("o1", [P, NT, E], fp32)
        o2 = sb("o2", [P, NT, E], fp32)
        ms = sb("ms", [P, NT], fp32)
        gate = sb("gate", [P, NT, NE], fp32)
        sg = sb("sg", [F2, 2, 2, BLK], fp32)
        hT = sb("hT", [F2, 2, 2, BLK], fp32)
        pT = pb("zpT", [P, 2, BLK], fp32)
        pG = pb("pG", [P, 2, BLK], fp32)
        pU = pb("zpU", [P, 2, BLK], fp32)
        pD = pb("pD", [P, 2, 512], fp32)

        s_w = sem("z_weights")
        s_wr = sem("z_router")
        s_const = sem("z_const")
        s_mv = sem("z_mv")
        s_std = sem("z_std")
        s_rstd = sem("z_rstd")
        s_xhat = sem("z_xhat")
        s_tr = sem("z_tr")
        s_xT = sem("z_xT")
        s_xb = sem("z_xb")
        s_lg = sem("z_lg")
        s_lgs = sem("z_lgs")
        s_sig = sem("z_sig")
        s_r = sem("z_r")
        s_gate = sem("z_gate")
        s_g = sem("z_g")
        s_sg = sem("z_sg")
        s_h = sem("z_h")
        s_d = sem("z_d")
        s_acc = sem("z_acc")
        s_out = sem("z_out")

        with nc.Block() as block:
            @block.sync
            def _(sp):
                sp.dma_start(wr[:, :, :], d["router"].rearrange("(c p) e -> p c e", p=P)).then_inc(s_wr, 16)
                sp.dma_start(eb[:, :], d["ebias"].partition_broadcast(P)).then_inc(s_wr, 16)
                for e in range(E):
                    sp.dma_start(wg[:, e, :, :], d["eg"][e, :, :].rearrange("(c p) f -> p c f", p=P)).then_inc(s_w, 16)
                    sp.dma_start(wu[:, e, :, :], d["eu"][e, :, :].rearrange("(c p) f -> p c f", p=P)).then_inc(s_w, 16)
                    sp.dma_start(wd[:, e, :, :], d["ed"][e, :, :].rearrange("(c p) o -> p c o", p=F2)).then_inc(s_w, 16)
                sp.dma_start(wg[:, E, :, :], d["sg"].rearrange("(c p) f -> p c f", p=P)).then_inc(s_w, 16)
                sp.dma_start(wu[:, E, :, :], d["su"].rearrange("(c p) f -> p c f", p=P)).then_inc(s_w, 16)
                sp.dma_start(wd[:, E, :, :], d["sd"].rearrange("(c p) o -> p c o", p=F2)).then_inc(s_w, 16)
                for k in range(NBLK):
                    sp.wait_ge(s_acc, (k + 1) * NE * BT + BT)
                    b, i = k // 2, k % 2 * BT
                    sp.dma_start(d["out"][b, i * P:(i + BT) * P, :].rearrange("(t p) e -> p t e", p=P),
                                 t.x[:, k * BT:(k + 1) * BT, :]).then_inc(s_out, 16)
                sp.wait_ge(s_out, NBLK * 16)

            @block.gpsimd
            def _(pool):
                nc.gpsimd.memset(epsc[:, :], EPS).then_inc(s_const, 1)
                for e in range(E):
                    nc.gpsimd.memset(order[:, e:e + 1], float(E - e)).then_inc(s_const, 1)
                nc.gpsimd.memset(gate[:, :, E:NE], 1.0).then_inc(s_const, 1)

            @block.tensor
            def _(pe):
                pe.wait_ge(s_wr, 32)
                with pe.Fori(0, NBLK) as k:
                    for i in range(BT):
                        pe.wait_ge(s_xhat, k * BT + i + 1)
                        for c in range(KC):
                            last = nc.tensor.transpose(pT[:, c, i * P:(i + 1) * P], xhat[:, i, c * P:(c + 1) * P],
                                                       t.ident[:, :])
                    last.then_inc(s_tr, 1)
                    pe.wait_ge(s_xb, k + 1)
                    pe.wait_ge(s_lgs, k + 1)
                    for i in range(BT):
                        for c in range(KC):
                            last = nc.tensor.matmul(pG[:, 0, i * E:(i + 1) * E], xb[:, c, i * P:(i + 1) * P],
                                                    wr[:, c, :], start=c == 0, stop=c == KC - 1)
                    last.then_inc(s_lg, 1)
                pe.wait_ge(s_w, NE * 3 * 16)
                pe.wait_ge(s_gate, 1)
                pe.wait_ge(s_lgs, NBLK + 1)

                with pe.Fori(0, NBLK) as k:
                    def up(e):
                        v = k * NE + e
                        pe.wait_ge(s_h, v + 1)
                        for w, bank in ((wg, pG), (wu, pU)):
                            for f in range(2):
                                for c in range(KC):
                                    last = nc.tensor.matmul(bank[0:F2, f, :], w[:, e, c, f * F2:(f + 1) * F2],
                                                            xT[:, bass.ds(k, 1), c, :], start=c == 0, stop=c == KC - 1)
                        last.then_inc(s_g, 1)

                    def down(e):
                        v = k * NE + e
                        pe.wait_ge(s_h, v + 2)
                        for i in range(BT):
                            if i % 2 == 0:
                                pe.wait_ge(s_acc, v * BT + i + 2)
                            for f in range(2):
                                last = nc.tensor.matmul(pD[:, i // 2, i % 2 * D:(i % 2 + 1) * D],
                                                        hT[:, e % 2, f, i * P:(i + 1) * P], wd[:, e, f, :],
                                                        start=f == 0, stop=f == 1)
                            if i % 2 == 1:
                                last.then_inc(s_d, 1)
                    for e in range(NE):
                        up(e)
                        if e > 0:
                            down(e - 1)
                    down(NE - 1)

            @block.scalar
            def _(act):
                act.wait_ge(s_const, 1)
                with act.Fori(0, NBLK) as k:
                    act.wait_ge(s_mv, k + 1)
                    nc.scalar.activation(std[:, :], mv[:, :, 1], ACT.Sqrt, bias=epsc[:, :]).then_inc(s_std, 1)
                    act.wait_ge(s_tr, k + 1)
                    nc.scalar.activation(xT[:, bass.ds(k, 1), :, :].rearrange("p k c n -> p (k c) n"), pT[:, :, :],
                                         ACT.Copy).then_inc(s_xT, 1)
                act.wait_ge(s_lgs, NBLK + 1)
                nc.scalar.activation(s0[:, :, :], c1[:, :, :], ACT.Sigmoid).then_inc(s_sig, 1)
                with act.Fori(0, NBLK) as k:
                    for e in range(NE):
                        act.wait_ge(s_g, k * NE + e + 1)
                        nc.scalar.activation(sg[:, e % 2, :, :], pG[0:F2, :, :], ACT.Silu).then_inc(s_sg, 1)

            @block.vector
            def _(dve):
                dve.wait_ge(s_const, 2 + E)
                dve.sem_inc(s_lgs, 1)
                with dve.Fori(0, NBLK) as k:
                    for i in range(BT):
                        nc.vector.bn_stats(stats[:, i, :], t.x[:, bass.ds(k * BT + i, 1), :])
                    nc.vector.drain()
                    for i in range(BT):
                        last = nc.vector.bn_aggr(mv[:, i, :], stats[:, i, :])
                    last.then_inc(s_mv, 1)
                    dve.wait_ge(s_std, k + 1)
                    nc.vector.reciprocal(rstd[:, :], std[:, :]).then_inc(s_rstd, 1)
                    dve.wait_ge(s_rstd, k + 1)
                    for i in range(BT):
                        normalise(nc, dve, t.x, mv, rstd, xhat, k * BT + i, i).then_inc(s_xhat, 1)
                    dve.wait_ge(s_xT, k + 1)
                    nc.vector.tensor_copy(xb[:, :, :], xT[:, bass.ds(k, 1), :, :].rearrange("p k c n -> p (k c) n"))\
                      .then_inc(s_xb, 1)
                    dve.wait_ge(s_lg, k + 1)
                    nc.vector.tensor_copy(c1[:, bass.ds(k * BT, BT), :],
                                          pG[:, 0, 0:BT * E].rearrange("p (t e) -> p t e", e=E)).then_inc(s_lgs, 1)
                dve.wait_ge(s_sig, 1)
                dve.wait_ge(s_wr, 32)
                steps = [0]

                def link(op):
                    steps[0] += 1
                    op.then_inc(s_r, 1)
                    dve.wait_ge(s_r, steps[0])

                def wide(v):
                    return v.unsqueeze(2).to_broadcast([P, NT, E])

                ebw = eb[:, :].unsqueeze(1).to_broadcast([P, NT, E])
                orw = order[:, :].unsqueeze(1).to_broadcast([P, NT, E])
                link(nc.vector.tensor_tensor(s1[:, :, :], s0[:, :, :], ebw, ALU.add))
                for chosen in (o1, o2):
                    link(nc.vector.tensor_reduce(ms[:, :], s1[:, :, :], AX.X, ALU.max))
                    link(nc.vector.tensor_tensor(c1[:, :, :], s1[:, :, :], wide(ms[:, :]), ALU.is_equal))
                    link(nc.vector.tensor_tensor(c1[:, :, :], c1[:, :, :], orw, ALU.mult))
                    link(nc.vector.tensor_reduce(ms[:, :], c1[:, :, :], AX.X, ALU.max))
                    link(nc.vector.tensor_tensor(chosen[:, :, :], c1[:, :, :], wide(ms[:, :]), ALU.is_equal))
                    if chosen is o1:
                        link(nc.vector.scalar_tensor_tensor(s1[:, :, :], o1[:, :, :], -3e38, s1[:, :, :],
                                                            ALU.mult, ALU.add))
                link(nc.vector.tensor_tensor(o1[:, :, :], o1[:, :, :], o2[:, :, :], ALU.add))
                link(nc.vector.tensor_tensor(o1[:, :, :], o1[:, :, :], s0[:, :, :], ALU.mult))
                link(nc.vector.tensor_reduce(ms[:, :], o1[:, :, :], AX.X, ALU.add))
                link(nc.vector.tensor_scalar(ms[:, :], ms[:, :], 1e-20, None, ALU.add))
                link(nc.vector.reciprocal(ms[:, :], ms[:, :]))
                link(nc.vector.tensor_tensor(gate[:, :, 0:E], o1[:, :, :], wide(ms[:, :]), ALU.mult))
                dve.sem_inc(s_gate, 1)
                dve.sem_inc(s_h, 1)
                dve.sem_inc(s_acc, BT)

                with dve.Fori(0, NBLK) as k:
                    def hidden(e):
                        dve.wait_ge(s_sg, k * NE + e + 1)
                        nc.vector.tensor_tensor(hT[:, e % 2, :, :], sg[:, e % 2, :, :], pU[0:F2, :, :],
                                                ALU.mult).then_inc(s_h, 1)

                    def add(e):
                        for i in range(BT):
                            if i % 2 == 0:
                                dve.wait_ge(s_d, (k * NE + e) * 2 + i // 2 + 1)
                            xs = t.x[:, bass.ds(k * BT + i, 1), :].rearrange("p t e -> p (t e)")
                            nc.vector.scalar_tensor_tensor(
                                xs, pD[:, i // 2, i % 2 * D:(i % 2 + 1) * D],
                                gate[:, bass.ds(k * BT + i, 1), e:e + 1].rearrange("p t e -> p (t e)"), xs,
                                ALU.mult, ALU.add).then_inc(s_acc, 1)
                    for e in range(NE):
                        hidden(e)
                        if e > 0:
                            add(e - 1)
                    add(NE - 1)


class Chip:
    pass


def build_program(nc, d):
    t = Chip()
    t.ctx = ExitStack()
    with t.ctx:
        def sb(ctx, name, shape):
            return ctx.enter_context(nc.sbuf_tensor(name, shape, fp32))

        t.x = sb(t.ctx, "x_sb", [P, NT, D])
        t.ident = sb(t.ctx, "ident_sb", [P, P])
        t.s_ident = t.ctx.enter_context(nc.semaphore("s_ident"))
        with ExitStack() as ctx:
            t.vx = sb(ctx, "vx", [P, NT, H, VW])
            build_projections(nc, t, d)
            build_attention(nc, t, d)
        with ExitStack() as ctx:
            t.q = sb(ctx, "q_sb", [P, NT, D])
            t.kbd = sb(ctx, "kbd", [P, KC, B, H // KC, S2])
            t.cv = sb(ctx, "cv", [S2, B, H, VW])
            t.lncol = sb(ctx, "lncol_sb", [P, 4])
            build_cross_queries(nc, t, d)
            build_cross_attention(nc, t, d)
        build_experts(nc, t, d)


def constants():
    import numpy as np
    inv = (1.0 / np.float32(10000.0) ** (np.arange(0, D, 2, dtype=np.float32) / np.float32(D))).astype(np.float32)
    pos = np.arange(-(L - 1), L, dtype=np.float32)
    ang = (inv[:, None] * pos[None, :]).astype(np.float32)
    basis = np.zeros((D, RW), np.float32)
    basis[0::2, 1:] = np.sin(ang)
    basis[1::2, 1:] = np.cos(ang)
    sel = np.zeros((P, VW), np.float32)
    for p in range(P):
        if p % 32 < VW:
            sel[p, p % 32] = 1.0
    headmask = (np.arange(P)[:, None] // DH == np.arange(H // KC)[None, :]).astype(np.float32)
    mask = np.where(np.arange(S2)[None, :] <= np.arange(P)[:, None], 0.0, -1e30).astype(np.float32)
    return {"basis": basis, "ident": np.eye(P, dtype=np.float32), "sel": sel, "headmask": headmask, "mask": mask}


def kernel(**inputs):
    import numpy as np
    import concourse.bacc as bacc
    from concourse.bass_utils import run_bass_kernel_spmd

    arrays = {"x": inputs["x"], "ctx": inputs["ctx_1024"]}
    for name, src in (("wq", "Wq"), ("wk", "Wk"), ("wv", "Wv"), ("wr", "Wr")):
        arrays[name] = np.asarray(inputs["L0_attn_" + src]).T
    uv = np.stack([np.asarray(inputs["L0_attn_u_bias"]), np.asarray(inputs["L0_attn_v_bias"])])
    arrays["uv"] = uv.reshape(2, KC, P).transpose(2, 0, 1)
    for name, src in (("xwq", "Wq"), ("xwk", "Wk"), ("xwv", "Wv"), ("xwo", "Wo"), ("bo", "bo")):
        arrays[name] = inputs["L0_xattn_" + src]
    cols = [np.asarray(inputs["L0_xattn_" + n]) for n in ("q_ln_w", "q_ln_b", "k_ln_w", "k_ln_b")]
    arrays["lncol"] = np.stack([np.tile(c, P // DH) for c in cols], axis=1)
    for name, src in (("router", "W_gate_router"), ("ebias", "expert_bias"), ("eg", "Wg"), ("eu", "Wu"), ("ed", "Wd"),
                      ("sg", "Wg_s"), ("su", "Wu_s"), ("sd", "Wd_s")):
        arrays[name] = inputs["L0_ffn_" + src]
    arrays.update(constants())
    arrays = {k: np.ascontiguousarray(a) for k, a in arrays.items()}
    nc = bacc.Bacc("TRN2", target_bir_lowering=False, num_devices=1)
    d = {k: nc.dram_tensor("in_" + k, a.shape, mybir.dt.from_np(a.dtype), kind="ExternalInput").ap()
         for k, a in arrays.items()}
    d["out"] = nc.dram_tensor("out_x", (B, L, D), fp32, kind="ExternalOutput").ap()
    d["qsplit"] = nc.dram_tensor("qsplit", (3, 3, D, B * L), bf16, kind="Internal").ap()
    d["rsplit"] = nc.dram_tensor("rsplit", (3, D, RW), bf16, kind="Internal").ap()
    d["ring"] = nc.dram_tensor("ring", (TPB, P, UW), fp32, kind="Internal").ap()
    build_program(nc, d)
    r = run_bass_kernel_spmd(nc, [{"in_" + k: a for k, a in arrays.items()}], core_ids=[0])
    return r.results[0]["out_x"]
```

```python
import concourse.bass as bass
from concourse import mybir
from contextlib import ExitStack

fp32 = mybir.dt.float32
bf16 = mybir.dt.bfloat16
ALU = mybir.AluOpType
ACT = mybir.ActivationFunctionType
AX = mybir.AxisListType

B, L, D = 4, 1024, 256
H, DH = 16, 16
S2 = 77
E, F = 8, 192
P = 128
NT = B * L // P
TPB = L // P
KC = D // P
BLK = 512
NBLK = B * L // BLK
BT = BLK // P
NH = B * H
RW = 2 * L
UW = L + P
UB = UW // 3
VW = DH + 1
EPS = 1e-5
TERMS = [(0, 0), (0, 1), (0, 2), (1, 0), (1, 1), (1, 2), (2, 0), (2, 1)]
QU, QV, KK = range(3)


def slots(eng, groups, size, tail, slot):
    def group(g):
        for u in range(size):
            def unit(lag):
                back = -(-max(lag - u, 0) // size)
                if type(g) is int and back > g:
                    return None
                return (g - back if back else g), u - lag + back * size
            slot(unit)
    peeled = -(-(tail + 1) // size)
    for g in range(peeled):
        group(g)
    with eng.Fori(peeled, groups) as g:
        group(g)
    for n in range(tail):
        def unit(lag):
            if n >= lag:
                return None
            back = -(-(lag - n) // size)
            return groups - back, n - lag + back * size
        slot(unit)


def earlier(g, u, size, n):
    return type(g) is not int or g * size + u >= n


def layer_statistics(nc, dve, x, stats, aggr, mv, s_aggr, s_mv):
    with dve.Fori(0, NBLK) as k:
        for i in range(BT):
            nc.vector.bn_stats(stats[:, i, :], x[:, bass.ds(k * BT + i, 1), :])
        nc.vector.drain()
        for i in range(BT):
            last = nc.vector.bn_aggr(aggr[:, i, :], stats[:, i, :])
        last.then_inc(s_aggr, 1)
        dve.wait_ge(s_aggr, k + 1)
        nc.vector.tensor_copy(mv[:, bass.ds(k * BT, BT), :], aggr[:, :, :]).then_inc(s_mv, 1)


def normalise_tile(nc, x, mv, rstd, xhat, tile):
    return nc.vector.tensor_scalar(xhat, x[:, bass.ds(tile, 1), :].rearrange("p t e -> p (t e)"),
                                   mv[:, bass.ds(tile, 1), 0:1].rearrange("p t v -> p (t v)"),
                                   rstd[:, bass.ds(tile, 1)], ALU.subtract, ALU.mult)


def build_projections(nc, t, d):
    ctx = ExitStack()
    with ctx:
        def sb(name, shape, dt):
            return ctx.enter_context(nc.sbuf_tensor(name, shape, dt))

        def sem(name):
            return t.ctx.enter_context(nc.semaphore(name))

        wT = sb("wT", [P, 4, KC, D], fp32)
        basis = sb("basis", [P, KC, RW], fp32)
        uvcol = sb("uvcol", [P, 2, KC], fp32)
        uvs = sb("uvs", [P, 2, KC], fp32)
        epsc = sb("epsc", [P, 1], fp32)
        stats = sb("stats", [P, BT, 6], fp32)
        mv = sb("mv", [P, 2, BT, 2], fp32)
        std = sb("std", [P, 2, BT], fp32)
        rstd = sb("rstd", [P, BT], fp32)
        xhat = sb("xhat", [P, BT, D], fp32)
        xT = sb("xT", [P, KC, BLK], fp32)
        full = sb("full", [P, 3, BLK], fp32)
        rest = sb("rest", [P, 3, BLK], fp32)
        parts = sb("parts", [P, 3, 3, BLK], bf16)
        pT = ctx.enter_context(nc.psum_tensor("pT", [P, 2, KC, 2, P], fp32))
        pU = ctx.enter_context(nc.psum_tensor("pU", [P, 4, BLK], fp32))
        pV = ctx.enter_context(nc.psum_tensor("pV", [P, 2, 2, D], fp32))

        s_w = sem("s_weights")
        s_wr = sem("s_position_weights")
        s_basis = sem("s_basis")
        s_uv = sem("s_uv")
        s_x = [sem(f"s_x{i}") for i in range(B)]
        s_const = sem("s_const")
        s_uvs = sem("s_uvs")
        s_mv = sem("s_mv")
        s_bn = sem("s_bn")
        s_std = sem("s_std")
        s_rstd = sem("s_rstd")
        s_xhat = sem("s_xhat")
        s_tr = sem("s_tr")
        s_xT = sem("s_xT")
        s_unit = sem("s_unit")
        s_full = sem("s_full")
        s_hi = sem("s_hi")
        s_rest = sem("s_rest")
        s_mid = sem("s_mid")
        s_lo = sem("s_lo")
        s_kept = [sem(f"s_kept{i}") for i in range(3)]
        s_v = sem("s_v")
        s_vx = sem("s_vx")

        RU = KC * RW // BLK
        CPB = 6
        UPB = 4
        CUTS = [(0, QU, 0), (0, QV, 0), (1, QU, 1), (1, QV, 1), (2, KK, 0), (3, KK, 1)]

        with nc.Block() as block:
            @block.sync
            def _(sp):
                sp.dma_start(wT[:, 3, :, :], d["wr"].rearrange("(c p) o -> p c o", p=P)).then_inc(s_wr, 16)
                sp.dma_start(t.ident[:, :], d["ident"]).then_inc(t.s_ident, 16)
                sp.dma_start(basis[:, :, :], d["basis"].rearrange("(c p) o -> p c o", p=P)).then_inc(s_basis, 16)
                for b in range(B):
                    sp.dma_start(t.x[:, b * TPB:(b + 1) * TPB, :],
                                 d["x"][b, :, :].rearrange("(t p) e -> p t e", p=P)).then_inc(s_x[b], 16)
                for i, w in enumerate(("wq", "wk", "wv")):
                    sp.dma_start(wT[:, i, :, :], d[w].rearrange("(c p) o -> p c o", p=P)).then_inc(s_w, 16)
                sp.dma_start(uvcol[:, :, :], d["uv"]).then_inc(s_uv, 16)
                for c in range(RU):
                    sp.wait_ge(s_lo, c + 1)
                    sp.dma_start(d["rsplit"][:, (c % KC) * P:(c % KC + 1) * P,
                                             (c // KC) * BLK:(c // KC + 1) * BLK].rearrange("s p n -> p s n"),
                                 parts[:, c % 3, :, :]).then_inc(s_kept[c % 3], 16)
                with sp.Fori(0, NBLK) as k:
                    for j, (_, operand, chunk) in enumerate(CUTS):
                        slot = (RU + j) % 3
                        token = sp.snap(k * BLK)
                        sp.wait_ge(s_lo, k * CPB + RU + j + 1)
                        sp.dma_start(d["qsplit"][operand, :, chunk * P:(chunk + 1) * P,
                                                 bass.ds(token, BLK)].rearrange("s p n -> p s n"),
                                     parts[:, slot, :, :]).then_inc(s_kept[slot], 16)
                for slot in range(3):
                    sp.wait_ge(s_kept[slot], 16 * len([c for c in range(RU + NBLK * CPB) if c % 3 == slot]))

            @block.gpsimd
            def _(pool):
                nc.gpsimd.memset(epsc[:, :], EPS).then_inc(s_const, 1)
                nc.gpsimd.memset(t.vx[:, :, :, :], 1.0).then_inc(s_const, 1)

                def third(slot, count):
                    pool.wait_ge(s_mid, count)
                    nc.gpsimd.tensor_tensor(parts[:, slot, 2, :], rest[:, slot, :], parts[:, slot, 1, :],
                                            ALU.subtract).then_inc(s_lo, 1)
                for c in range(RU):
                    if c >= 3:
                        pool.wait_ge(s_kept[c % 3], 16 * (c // 3))
                    third(c % 3, c + 1)
                with pool.Fori(0, NBLK) as k:
                    for j in range(CPB):
                        c = RU + j
                        pool.wait_ge(s_kept[c % 3], (k * (CPB // 3) + c // 3) * 16)
                        third(c % 3, k * CPB + c + 1)

            @block.tensor
            def _(pe):
                pe.wait_ge(s_basis, 16)
                pe.wait_ge(s_wr, 16)
                for r in range(RU):
                    if r >= 4:
                        pe.wait_ge(s_full, r - 3)
                    for c in range(KC):
                        last = nc.tensor.matmul(pU[:, r % 4, :], wT[:, 3, c, (r % KC) * P:(r % KC + 1) * P],
                                                basis[:, c, (r // KC) * BLK:(r // KC + 1) * BLK],
                                                start=c == 0, stop=c == KC - 1)
                    last.then_inc(s_unit, 1)
                pe.wait_ge(s_w, 48)
                pe.wait_ge(t.s_ident, 16)

                with pe.Fori(0, NBLK) as k:
                    for pair in range(BT // 2):
                        for i in range(2):
                            tile = 2 * pair + i
                            pe.wait_ge(s_xhat, k * BT + tile + 1)
                            for c in range(KC):
                                last = nc.tensor.transpose(pT[:, pair, c, i, :],
                                                           xhat[:, tile, c * P:(c + 1) * P], t.ident[:, :])
                        last.then_inc(s_tr, 1)
                    pe.wait_ge(s_xT, k * 2 + 2)
                    for u in range(UPB):
                        pe.wait_ge(s_full, k * CPB + RU - CPB + [2, 4, 5, 6][u])
                        w, oc = u // KC, u % KC
                        for c in range(KC):
                            last = nc.tensor.matmul(pU[:, u, :], wT[:, w, c, oc * P:(oc + 1) * P],
                                                    xT[:, c, :], start=c == 0, stop=c == KC - 1)
                        last.then_inc(s_unit, 1)
                    for pair in range(BT // 2):
                        pe.wait_ge(s_vx, k * 2 + pair + 1)
                        for i in range(2):
                            for c in range(KC):
                                last = nc.tensor.matmul(pV[:, pair, i, :],
                                                        xT[:, c, (2 * pair + i) * P:(2 * pair + i + 1) * P],
                                                        wT[:, 2, c, :], start=c == 0, stop=c == KC - 1)
                        last.then_inc(s_v, 1)

            @block.scalar
            def _(act):
                def first(count, unit, bank, slot, scale, bias):
                    act.wait_ge(s_unit, unit)
                    if bias is None:
                        nc.scalar.activation(full[:, slot, :], pU[:, bank, :], ACT.Copy, scale=scale).then_inc(s_full, 1)
                    else:
                        nc.scalar.activation(full[:, slot, :], pU[:, bank, :], ACT.Identity, scale=scale,
                                             bias=bias).then_inc(s_full, 1)

                def second(count, slot):
                    act.wait_ge(s_rest, count)
                    nc.scalar.activation(parts[:, slot, 1, :], rest[:, slot, :], ACT.Copy).then_inc(s_mid, 1)

                for c in range(RU):
                    if c >= 3:
                        act.wait_ge(s_kept[c % 3], 16 * (c // 3))
                    first(c + 1, c + 1, c % 4, c % 3, 1.0, None)
                    second(c + 1, c % 3)
                act.wait_ge(s_const, 1)
                act.wait_ge(s_uvs, 1)
                with act.Fori(0, NBLK) as k:
                    act.wait_ge(s_mv, k + 1)
                    nc.scalar.activation(std[:, 0, :], mv[:, 0, :, 1], ACT.Sqrt, bias=epsc[:, :]).then_inc(s_std, 1)
                    for pair in range(BT // 2):
                        act.wait_ge(s_tr, k * 2 + pair + 1)
                        nc.scalar.activation(xT[:, :, pair * 2 * P:(pair + 1) * 2 * P],
                                             pT[:, pair, :, :, :].rearrange("p c i n -> p c (i n)"),
                                             ACT.Copy).then_inc(s_xT, 1)
                    for j, (u, operand, chunk) in enumerate(CUTS):
                        c = RU + j
                        act.wait_ge(s_kept[c % 3], (k * (CPB // 3) + c // 3) * 16)
                        bias = None if operand == KK else uvs[:, operand, chunk:chunk + 1]
                        first(None, k * UPB + RU + u + 1, u, c % 3, 1.0 if operand == KK else -0.25, bias)
                        second(k * CPB + c + 1, c % 3)

            @block.vector
            def _(dve):
                dve.wait_ge(s_uv, 16)
                nc.vector.tensor_scalar(uvs[:, :, :], uvcol[:, :, :], -0.25, None, ALU.mult).then_inc(s_uvs, 1)
                dve.sem_inc(s_vx, 2)

                def cut(count, slot):
                    dve.wait_ge(s_full, count)
                    nc.vector.tensor_copy(parts[:, slot, 0, :], full[:, slot, :]).then_inc(s_hi, 1)
                    dve.wait_ge(s_hi, count)
                    nc.vector.tensor_tensor(rest[:, slot, :], full[:, slot, :], parts[:, slot, 0, :],
                                            ALU.subtract).then_inc(s_rest, 1)
                for c in range(RU):
                    cut(c + 1, c % 3)
                for b in range(B):
                    dve.wait_ge(s_x[b], 16)
                dve.wait_ge(s_const, 2)
                with dve.Fori(0, NBLK) as k:
                    for i in range(BT):
                        nc.vector.bn_stats(stats[:, i, :], t.x[:, bass.ds(k * BT + i, 1), :])
                    nc.vector.drain()
                    for i in range(BT):
                        last = nc.vector.bn_aggr(mv[:, 0, i, :], stats[:, i, :])
                    last.then_inc(s_mv, 1)
                    dve.wait_ge(s_std, k + 1)
                    nc.vector.reciprocal(rstd[:, :], std[:, 0, :]).then_inc(s_rstd, 1)
                    dve.wait_ge(s_rstd, k + 1)
                    for i in range(BT):
                        nc.vector.tensor_scalar(xhat[:, i, :], t.x[:, bass.ds(k * BT + i, 1), :],
                                                mv[:, 0, i, 0:1], rstd[:, i:i + 1],
                                                ALU.subtract, ALU.mult).then_inc(s_xhat, 1)
                    for j in range(CPB):
                        cut(k * CPB + RU + j + 1, (RU + j) % 3)
                    for pair in range(BT // 2):
                        dve.wait_ge(s_v, k * 2 + pair + 1)
                        nc.vector.tensor_copy(
                            t.vx[:, bass.ds(k * BT + 2 * pair, 2), :, 0:DH],
                            pV[:, pair, :, :].rearrange("p i (h e) -> p i h e", e=DH)).then_inc(s_vx, 1)


def build_attention(nc, t, d):
    ctx = ExitStack()
    with ctx:
        def sb(name, shape, dt):
            return ctx.enter_context(nc.sbuf_tensor(name, shape, dt))

        def sem(name):
            return t.ctx.enter_context(nc.semaphore(name))

        QW = L + 2
        rp = sb("rp", [P, H, RW], bf16)
        qv = sb("qv", [P, 4, QW], bf16)
        qu = sb("qu", [P, 4, L], bf16)
        kk = sb("kk", [P, 4, L], bf16)
        ub = sb("ub", [P, 2, UW], fp32)
        bd = sb("bd", [P, 4, L], fp32)
        sc = sb("sc", [P, 4, L], fp32)
        pt = sb("pt", [P, 2, L], fp32)
        mn = sb("mn", [P, 4], fp32)
        rs = sb("rs", [P, TPB], fp32)
        on = sb("on", [P, TPB, VW], fp32)
        vh = sb("vh", [P, TPB, 32], fp32)
        pb = sb("pb", [P, 2, P], fp32)
        sel = sb("sel", [P, VW], fp32)
        pu = ctx.enter_context(nc.psum_tensor("pu", [P, 3, 512], fp32))
        pa = ctx.enter_context(nc.psum_tensor("pa", [P, L], fp32))
        pp = ctx.enter_context(nc.psum_tensor("pp", [P, 2, 512], fp32))
        po = ctx.enter_context(nc.psum_tensor("po", [P, 512], fp32))

        s_rp = sem("s_rp")
        s_pad = sem("s_pad")
        s_qv = sem("s_qv")
        s_kq = sem("s_kq")
        s_u = sem("s_u")
        s_ub = sem("s_ub")
        s_wr = [sem(f"s_wr{i}") for i in range(TPB)]
        s_rd = [sem(f"s_rd{i}") for i in range(4)]
        s_ac = sem("s_ac")
        s_sc = sem("s_sc")
        s_exp = sem("s_exp")
        s_tr = sem("s_trp")
        s_pt = sem("s_pt")
        s_pv = sem("s_pv")
        s_fin = sem("s_fin")
        s_sel = sem("s_sel")
        s_vh = sem("s_vh")
        s_pb = sem("s_pb")
        s_comb = sem("s_comb")
        s_fs = sem("s_fs")
        s_go = sem("s_go")
        s_sp = sem("s_sp")

        ring = d["ring"]

        def steps(eng, step):
            step(0, True, False, False)
            step(1, True, True, False)
            with eng.Fori(2, NH) as m:
                step(m, True, True, True)
            step(NH, False, True, True)

        with nc.Block() as block:
            @block.gpsimd
            def _(pool):
                nc.gpsimd.memset(qv[:, :, L:QW], 0.0).then_inc(s_pad, 1)
                nc.gpsimd.memset(vh[:, :, :], 0.0).then_inc(s_pad, 1)

                def load(dst, operand, two, side, s):
                    b, h = two // (H // 2), two % (H // 2)
                    for g, term in enumerate(TERMS):
                        pool.dma_start(dst[g * DH:(g + 1) * DH, bass.ds(two % 2 * 2, 2), 0:L],
                                       d["qsplit"][operand, term[side], bass.ds(h * 2 * DH, 2 * DH),
                                                   bass.ds(b * L, L)].rearrange("(a e) n -> e a n", e=DH)).then_inc(s, 16)
                load(qv, QV, 0, 0, s_qv)
                for g, term in enumerate(TERMS):
                    pool.dma_start(rp[g * DH:(g + 1) * DH, :, :],
                                   d["rsplit"][term[1], :, :].rearrange("(h e) n -> e h n", e=DH)).then_inc(s_rp, 16)
                load(kk, KK, 0, 1, s_kq)
                load(qu, QU, 0, 0, s_kq)
                with pool.Fori(0, NH // 2 - 1) as two:
                    pool.wait_ge(s_u, two * 2 * TPB + 1)
                    load(qv, QV, two + 1, 0, s_qv)
                    pool.wait_ge(s_ac, two * 2 * TPB + 1)
                    load(kk, KK, two + 1, 1, s_kq)
                    load(qu, QU, two + 1, 0, s_kq)

            @block.sync
            def _(sp):
                sp.dma_start(sel[:, :], d["sel"]).then_inc(s_sel, 16)

                def step(m, ahead, main, tail):
                    for it in range(TPB):
                        r = (it + 3) % TPB
                        n = m - 1 if it + 3 < TPB else m
                        reads = it + 3 < TPB and main or it + 3 >= TPB and ahead
                        reused = reads and (it + 3 < TPB or main) and (type(n) is not int or n * TPB + r >= 4)
                        if ahead:
                            sp.wait_ge(s_ub, m * TPB + it + 1)
                            sp.sem_inc(s_sp, 1)
                            if main:
                                sp.wait_ge(s_rd[it % 4], (m * 2 - 1 + it // 4) * 16)
                            sp.dma_start(ring[it, :, :], ub[:, it % 2, :]).then_inc(s_wr[it], 16)
                        if reads:
                            sp.wait_ge(s_wr[r], (n + 1) * 16)
                            sp.sem_inc(s_sp, 1)
                            if reused:
                                sp.wait_ge(s_sc, n * TPB + r - 3)
                            skew = ring[r, :, :].rearrange("p w -> (p w)")[P - 1:P - 1 + P * (UW - 1)]
                            sp.dma_start(bd[:, r % 4, :],
                                         skew.rearrange("(p w) -> p w", p=P)[:, 0:L]).then_inc(s_rd[r % 4], 16)
                steps(sp, step)

            @block.tensor
            def _(pe):
                pe.wait_ge(s_rp, 128)
                pe.wait_ge(s_pad, 1)
                pe.wait_ge(s_sel, 16)
                pe.wait_ge(t.s_ident, 16)

                def unshifted(m, h, par, it):
                    i0 = it * P
                    edge = i0 + P
                    if type(m) is not int or m * TPB + it > 0:
                        pe.wait_ge(s_ub, m * TPB + it)
                    cuts = sorted({0, UB, 2 * UB, UW, edge})
                    for a, b in zip(cuts, cuts[1:]):
                        low = a < edge
                        col = RW - edge + a if low else a - edge
                        row = i0 if low else i0 + 1
                        last = nc.tensor.matmul(pu[:, a // UB, a % UB:a % UB + b - a],
                                                qv[:, par, row:row + P],
                                                rp[:, h, col:col + b - a], start=True, stop=True)
                    last.then_inc(s_u, 1)

                def scores(n, par, it):
                    if type(n) is not int or n * TPB + it > 0:
                        pe.wait_ge(s_sc, n * TPB + it)
                    for c in range(2):
                        last = nc.tensor.matmul(pa[:, c * 512:(c + 1) * 512], qu[:, par, it * P:(it + 1) * P],
                                                kk[:, par, c * 512:(c + 1) * 512], start=True, stop=True)
                    last.then_inc(s_ac, 1)

                def transposes(n, it):
                    g = n * TPB + it
                    pe.wait_ge(s_exp, g + 1)
                    for c in range(2):
                        if type(n) is not int or g > 0:
                            pe.wait_ge(s_pt, g * 2 - 1 + c)
                        for j in range(4):
                            last = nc.tensor.transpose(pp[:, c, j * P:(j + 1) * P],
                                                       sc[:, it % 4, (4 * c + j) * P:(4 * c + j + 1) * P],
                                                       t.ident[:, :])
                        last.then_inc(s_tr, 1)

                def weighted(n, it):
                    g = n * TPB + it
                    pe.wait_ge(s_pt, g * 2 + 2)
                    if it == 0:
                        pe.wait_ge(s_vh, n + 1)
                        if type(n) is not int or n > 0:
                            pe.wait_ge(s_fin, n)
                    if type(n) is not int or g > 0:
                        pe.wait_ge(s_pb, g)
                    for j in range(TPB):
                        c = 32 * (j % 4)
                        last = nc.tensor.matmul(po[c:c + 32, 0:P], vh[:, j, :], pt[:, it % 2, j * P:(j + 1) * P],
                                                start=j < 4, stop=j >= 4)
                    last.then_inc(s_pv, 1)

                def combine(n, it):
                    pe.wait_ge(s_pb, n * TPB + it + 1)
                    nc.tensor.matmul(po[:, P + it * VW:P + (it + 1) * VW], pb[:, it % 2, :], sel[:, :],
                                     start=True, stop=True).then_inc(s_comb, 1)

                def dyn(x):
                    return x if type(x) is int else bass.ds(x, 1)

                def step(m, ahead, main, tail):
                    if ahead:
                        pe.wait_ge(s_qv, (m // 2 + 1) * 128)
                    if main:
                        pe.wait_ge(s_kq, ((m + 1) // 2) * 256)
                    n = m - 1
                    for it in range(TPB):
                        late = [(n, it - 2)] if it >= 2 and main else [(n - 1, it + 6)] if it < 2 and tail else []
                        for nn, i in late:
                            transposes(nn, i)
                        if ahead:
                            unshifted(m, dyn(m % H), dyn(m % 4), it)
                        if main:
                            scores(n, dyn(n % 4), it)
                        if it >= 3 and main:
                            combine(n, it - 3)
                        if it < 3 and tail:
                            combine(n - 1, it + 5)
                        for nn, i in late:
                            weighted(nn, i)
                steps(pe, step)
                for i in (TPB - 2, TPB - 1):
                    transposes(NH - 1, i)
                    combine(NH - 1, i - 1)
                    weighted(NH - 1, i)
                combine(NH - 1, TPB - 1)

            @block.scalar
            def _(act):
                def exponential(n, it):
                    act.wait_ge(s_sc, n * TPB + it + 1)
                    nc.scalar.activation(sc[:, it % 4, :], sc[:, it % 4, :], ACT.Exp, scale=-1.0,
                                         bias=mn[:, it % 4:it % 4 + 1]).then_inc(s_exp, 1)

                def step(m, ahead, main, tail):
                    for it in range(TPB):
                        if it >= 1 and main:
                            exponential(m - 1, it - 1)
                        if it == 0 and tail:
                            exponential(m - 2, TPB - 1)
                        if ahead:
                            act.wait_ge(s_u, m * TPB + it + 1)
                            if it >= 2 or main:
                                act.wait_ge(s_wr[(it - 2) % TPB], (m + (1 if it >= 2 else 0)) * 16)
                            nc.scalar.activation(ub[:, it % 2, :].rearrange("p (c n) -> p c n", c=3),
                                                 pu[:, :, 0:UB], ACT.Copy).then_inc(s_ub, 1)
                steps(act, step)
                exponential(NH - 1, TPB - 1)

            @block.vector
            def _(dve):
                dve.wait_ge(s_pad, 2)

                def evacuate(n, it):
                    g = n * TPB + it
                    for c in range(2):
                        dve.wait_ge(s_tr, g * 2 + c + 1)
                        if c == 0 and (type(n) is not int or g >= 2):
                            dve.wait_ge(s_pv, g - 1)
                        nc.vector.tensor_copy(pt[:, it % 2, c * 512:(c + 1) * 512], pp[:, c, :]).then_inc(s_pt, 1)

                def total(n, it):
                    g = n * TPB + it
                    dve.wait_ge(s_ac, g + 1)
                    dve.wait_ge(s_rd[it % 4], (n * 2 + it // 4 + 1) * 16)
                    if type(n) is not int or g >= 4:
                        dve.wait_ge(s_tr, g * 2 - 6)
                    dve.sem_inc(s_go, 1)
                    nc.vector.tensor_tensor_reduce(out=sc[:, it % 4, :], in0=pa[:, :], in1=bd[:, it % 4, :],
                                                   scale=1.0, scalar=3e38, op0=ALU.add, op1=ALU.min,
                                                   accum_out=mn[:, it % 4:it % 4 + 1]).then_inc(s_sc, 1)

                def partials(n, it):
                    g = n * TPB + it
                    dve.wait_ge(s_pv, g + 1)
                    if type(n) is not int or g >= 2:
                        dve.wait_ge(s_comb, g - 1)
                    nc.vector.tensor_copy(pb[:, it % 2, :], po[:, 0:P]).then_inc(s_pb, 1)

                def values(n):
                    if type(n) is not int or n > 0:
                        dve.wait_ge(s_pv, n * TPB)
                    nc.vector.tensor_copy(vh[:, :, 0:VW].unsqueeze(2),
                                          t.vx[:, bass.ds((n // H) * TPB, TPB), bass.ds(n % H, 1), :]).then_inc(s_vh, 1)

                def finish(n):
                    dve.wait_ge(s_comb, n * TPB + TPB)
                    nc.vector.tensor_copy(on[:, :, :], po[:, P:P + TPB * VW].rearrange("p (i e) -> p i e", e=VW))\
                      .then_inc(s_fin, 1)
                    dve.wait_ge(s_fin, n + 1)
                    nc.vector.reciprocal(rs[:, :], on[:, :, DH]).then_inc(s_fs, 1)
                    dve.wait_ge(s_fs, n * 3 + 1)
                    nc.vector.tensor_tensor(on[:, :, 0:DH], on[:, :, 0:DH],
                                            rs[:, :].unsqueeze(2).to_broadcast([P, TPB, DH]), ALU.mult).then_inc(s_fs, 1)
                    dve.wait_ge(s_fs, n * 3 + 2)
                    xs = t.x[:, bass.ds((n // H) * TPB, TPB), bass.ds((n % H) * DH, DH)]
                    nc.vector.tensor_tensor(xs, xs, on[:, :, 0:DH], ALU.add).then_inc(s_fs, 1)

                def step(m, ahead, main, tail):
                    for it in range(TPB):
                        if it == 2 and main:
                            values(m - 1)
                        if it >= 2 and main:
                            evacuate(m - 1, it - 2)
                        if it < 2 and tail:
                            evacuate(m - 2, it + 6)
                        if main:
                            total(m - 1, it)
                        if it == 2 and tail:
                            finish(m - 2)
                        if it >= 2 and main:
                            partials(m - 1, it - 2)
                        if it < 2 and tail:
                            partials(m - 2, it + 6)
                steps(dve, step)
                for i in (TPB - 2, TPB - 1):
                    evacuate(NH - 1, i)
                    partials(NH - 1, i)
                finish(NH - 1)


def build_cross_queries(nc, t, d):
    ctx = ExitStack()
    with ctx:
        def sb(name, shape, dt):
            return ctx.enter_context(nc.sbuf_tensor(name, shape, dt))

        def pb(name, shape, dt):
            return ctx.enter_context(nc.psum_tensor(name, shape, dt))

        def sem(name):
            return t.ctx.enter_context(nc.semaphore(name))

        G = BT * H
        w = sb("xw", [P, 3, KC, D], fp32)
        cx = sb("cx", [S2, B, D], fp32)
        cT = sb("cT", [P, KC, B * S2], fp32)
        ks = sb("ks", [S2, B * H, DH], fp32)
        ksq = sb("ksq", [S2, B * H, DH], fp32)
        k1 = sb("k1", [S2, B * H], fp32)
        k2 = sb("k2", [S2, B * H], fp32)
        kT = sb("kT", [P, KC, B, S2], fp32)
        hm = sb("hm", [P, H // KC], fp32)
        epsc = sb("xepsc", [P, 1], fp32)
        stats = sb("xstats", [P, BT, 6], fp32)
        aggr = sb("xaggr", [P, BT, 2], fp32)
        mv = sb("xmv", [P, NT, 2], fp32)
        std = sb("xstd", [P, NT], fp32)
        rstd = sb("xrstd", [P, NT], fp32)
        xhat = sb("xxhat", [P, 2, BT, D], fp32)
        xT = sb("xxT", [P, 2, KC, BLK], fp32)
        qc = sb("qc", [P, NBLK * G, DH], fp32)
        qs = sb("qs", [P, 2, G, DH], fp32)
        m1 = sb("m1", [P, 2, G], fp32)
        m2 = sb("m2", [P, NBLK * G], fp32)
        m3 = sb("m3", [P, NBLK * G], fp32)
        qn = sb("qn", [P, 2, G, DH], fp32)
        pT = pb("xpT", [P, 2, KC, BLK], fp32)
        pQ = pb("pQ", [P, 2, BT, D], fp32)
        pC = pT[:, 0, :, :]
        pK = pQ[0:S2, 0, :, :]

        s_w = sem("x_weights")
        s_c = sem("x_context")
        s_cols = sem("x_cols")
        s_const = sem("x_const")
        s_cT = sem("x_cT")
        s_cTs = sem("x_cTs")
        s_k = sem("x_k")
        s_ks = sem("x_ks")
        s_kd = sem("x_kd")
        s_ka = sem("x_ka")
        s_v = sem("x_v")
        s_vs = sem("x_vs")
        s_kt = sem("x_kt")
        s_aggr = sem("x_aggr")
        s_mv = sem("x_mv")
        s_std = sem("x_std")
        s_rstd = sem("x_rstd")
        s_xhat = sem("x_xhat")
        s_tr = sem("x_tr")
        s_xT = sem("x_xT")
        s_q = sem("x_q")
        s_sum = sem("x_sum")
        s_qc = sem("x_qc")
        s_sq = sem("x_sq")
        s_m2 = sem("x_m2")
        s_qstd = sem("x_qstd")
        s_m3 = sem("x_m3")
        s_qn = sem("x_qn")
        s_qt = sem("x_qt")
        s_qT = sem("x_qT")

        TRANSPOSE, PROJECT, CENTRE, SQUARE, SUM = 0, 1, 2, 2, 3
        PAIR = 2

        def heads(v, parts, n):
            return v.unsqueeze(2).to_broadcast([parts, n, DH])

        def of_block(v, k):
            return v[:, bass.ds(k * G, G)] if len(v.shape) == 2 else v[:, bass.ds(k * G, G), :]

        with nc.Block() as block:
            @block.sync
            def _(sp):
                sp.dma_start(cx[:, :, :], d["ctx"].rearrange("b s e -> s b e")).then_inc(s_c, 16)
                for i, n in enumerate(("xwq", "xwk", "xwv")):
                    sp.dma_start(w[:, i, :, :], d[n].rearrange("(c p) o -> p c o", p=P)).then_inc(s_w, 16)
                sp.dma_start(t.lncol[:, :], d["lncol"]).then_inc(s_cols, 16)
                sp.dma_start(hm[:, :], d["headmask"]).then_inc(s_cols, 16)

            @block.gpsimd
            def _(pool):
                nc.gpsimd.memset(epsc[:, :], EPS).then_inc(s_const, 1)
                nc.gpsimd.memset(t.cv[:, :, :, :], 1.0).then_inc(s_const, 1)
                pool.wait_ge(s_kd, 7)
                pool.wait_ge(s_cols, 32)
                for c in range(KC):
                    for b in range(B):
                        nc.gpsimd.tensor_tensor(t.kbd[:, c, b, :, :],
                                                kT[:, c, b:b + 1, :].to_broadcast([P, H // KC, S2]),
                                                hm[:, :].unsqueeze(2).to_broadcast([P, H // KC, S2]), ALU.mult)

            @block.tensor
            def _(pe):
                pe.wait_ge(s_c, 16)
                for c in range(KC):
                    for b in range(B):
                        last = nc.tensor.transpose(pC[:, c, b * S2:(b + 1) * S2], cx[:, b, c * P:(c + 1) * P],
                                                   t.ident[0:S2, 0:S2])
                last.then_inc(s_cT, 1)
                pe.wait_ge(s_w, 48)
                pe.wait_ge(s_cTs, 1)
                for i in (1, 2):
                    if i == 2:
                        pe.wait_ge(s_ks, 1)
                    for b in range(B):
                        for c in range(KC):
                            last = nc.tensor.matmul(pK[:, b, :], cT[:, c, b * S2:(b + 1) * S2], w[:, i, c, :],
                                                    start=c == 0, stop=c == KC - 1)
                    last.then_inc(s_k if i == 1 else s_v, 1)
                pe.wait_ge(s_kd, 6)
                for c in range(KC):
                    for b in range(B):
                        last = nc.tensor.transpose(pC[:, c, b * S2:(b + 1) * S2],
                                                   ks[:, b * H + c * H // KC:b * H + (c + 1) * H // KC, :]
                                                   .rearrange("s h e -> s (h e)"), t.ident[0:S2, 0:S2])
                last.then_inc(s_kt, 1)
                pe.wait_ge(s_kd, 7)
                pe.wait_ge(s_vs, 1)

                def transposes(g, par):
                    k = g * PAIR + par
                    if earlier(g, par, PAIR, 2):
                        pe.wait_ge(s_xT, k - 1)
                    for i in range(BT):
                        pe.wait_ge(s_xhat, k * BT + i + 1)
                        for c in range(KC):
                            last = nc.tensor.transpose(pT[:, par, c, i * P:(i + 1) * P],
                                                       xhat[:, par, i, c * P:(c + 1) * P], t.ident[:, :])
                    last.then_inc(s_tr, 1)

                def project(g, par):
                    k = g * PAIR + par
                    pe.wait_ge(s_xT, k + 1)
                    if earlier(g, par, PAIR, 2):
                        pe.wait_ge(s_qc, k - 1)
                    for i in range(BT):
                        for c in range(KC):
                            last = nc.tensor.matmul(pQ[:, par, i, :], xT[:, par, c, i * P:(i + 1) * P], w[:, 0, c, :],
                                                    start=c == 0, stop=c == KC - 1)
                    last.then_inc(s_q, 1)

                def slot(unit):
                    if unit(TRANSPOSE):
                        transposes(*unit(TRANSPOSE))
                    if unit(PROJECT):
                        project(*unit(PROJECT))
                slots(pe, NBLK // PAIR, PAIR, SUM, slot)
                pe.wait_ge(s_qc, NBLK)
                pe.sem_inc(s_qT, PAIR)
                with pe.Fori(0, NBLK // PAIR) as g:
                    for par in range(PAIR):
                        k = g * PAIR + par
                        pe.wait_ge(s_qn, k + 1)
                        pe.wait_ge(s_qT, k + 1)
                        for i in range(BT):
                            for c in range(KC):
                                hs = slice(i * H + c * H // KC, i * H + (c + 1) * H // KC)
                                last = nc.tensor.transpose(pQ[:, par, i, c * P:(c + 1) * P],
                                                           qn[:, par, hs, :].rearrange("p h e -> p (h e)"), t.ident[:, :])
                        last.then_inc(s_qt, 1)

            @block.scalar
            def _(act):
                act.wait_ge(s_cT, 1)
                nc.scalar.activation(cT[:, :, :], pC[:, :, 0:B * S2], ACT.Copy).then_inc(s_cTs, 1)
                act.wait_ge(s_const, 2)
                act.wait_ge(s_mv, NBLK)
                nc.scalar.activation(std[:, :], mv[:, :, 1], ACT.Sqrt, bias=epsc[:, :]).then_inc(s_std, 1)
                act.wait_ge(s_kd, 3)
                nc.scalar.activation(ksq[:, :, :], ks[:, :, :], ACT.Square).then_inc(s_ka, 1)
                act.wait_ge(s_kd, 4)
                nc.scalar.activation(k2[:, :], k1[:, :], ACT.Sqrt, scale=1.0 / DH, bias=epsc[0:S2, :]).then_inc(s_ka, 1)
                act.wait_ge(s_v, 1)
                nc.scalar.activation(t.cv[:, :, :, 0:DH], pK[:, :, :].rearrange("s b (h e) -> s b h e", e=DH),
                                     ACT.Copy).then_inc(s_vs, 1)

                def turned(g, par):
                    act.wait_ge(s_tr, g * PAIR + par + 1)
                    if earlier(g, par, PAIR, 2):
                        act.wait_ge(s_q, g * PAIR + par - 1)
                    nc.scalar.activation(xT[:, par, :, :], pT[:, par, :, :], ACT.Copy).then_inc(s_xT, 1)

                def square(g, par):
                    k = g * PAIR + par
                    act.wait_ge(s_qc, k + 1)
                    if earlier(g, par, PAIR, 2):
                        act.wait_ge(s_m2, k - 1)
                    nc.scalar.activation(qs[:, par, :, :], of_block(qc, k), ACT.Square).then_inc(s_sq, 1)

                def slot(unit):
                    if unit(TRANSPOSE):
                        turned(*unit(TRANSPOSE))
                    if unit(SQUARE):
                        square(*unit(SQUARE))
                slots(act, NBLK // PAIR, PAIR, SUM, slot)
                act.wait_ge(s_m2, NBLK)
                nc.scalar.activation(m2[:, :], m2[:, :], ACT.Sqrt, scale=1.0 / DH, bias=epsc[:, :]).then_inc(s_qstd, 1)
                with act.Fori(0, NBLK // PAIR) as g:
                    for par in range(PAIR):
                        k = g * PAIR + par
                        act.wait_ge(s_qt, k + PAIR + 1)
                        nc.scalar.activation(t.qT[:, bass.ds(k * BT, BT), :, :].rearrange("p t c n -> p t (c n)"),
                                             pQ[:, par, :, :], ACT.Copy).then_inc(s_qT, 1)

            @block.vector
            def _(dve):
                dve.wait_ge(s_const, 2)
                layer_statistics(nc, dve, t.x, stats, aggr, mv, s_aggr, s_mv)
                dve.wait_ge(s_k, 1)
                kp = pK[:, :, :].rearrange("s b (h e) -> s (b h) e", e=DH)
                nc.vector.tensor_reduce(k1[:, :], kp, AX.X, ALU.add).then_inc(s_kd, 1)
                dve.wait_ge(s_kd, 1)
                nc.vector.tensor_scalar(k2[:, :], k1[:, :], 1.0 / DH, None, ALU.mult).then_inc(s_kd, 1)
                dve.wait_ge(s_kd, 2)
                nc.vector.tensor_tensor(ks[:, :, :], kp, heads(k2[:, :], S2, B * H), ALU.subtract).then_inc(s_kd, 1)
                dve.wait_ge(s_kd, 3)
                dve.sem_inc(s_ks, 1)
                dve.wait_ge(s_std, 1)
                nc.vector.reciprocal(rstd[:, :], std[:, :]).then_inc(s_rstd, 1)
                dve.wait_ge(s_ka, 1)
                nc.vector.tensor_reduce(k1[:, :], ksq[:, :, :], AX.X, ALU.add).then_inc(s_kd, 1)
                dve.wait_ge(s_ka, 2)
                nc.vector.reciprocal(k1[:, :], k2[:, :]).then_inc(s_kd, 1)
                dve.wait_ge(s_kd, 5)
                nc.vector.tensor_tensor(ks[:, :, :], ks[:, :, :], heads(k1[:, :], S2, B * H), ALU.mult).then_inc(s_kd, 1)
                dve.wait_ge(s_kt, 1)
                dve.wait_ge(s_cols, 32)
                nc.vector.tensor_scalar(kT[:, :, :, :].rearrange("p c b s -> p c (b s)"), pC[:, :, 0:B * S2],
                                        t.lncol[:, 2:3], t.lncol[:, 3:4], ALU.mult, ALU.add).then_inc(s_kd, 1)
                dve.wait_ge(s_rstd, 1)

                def normalised(g, par):
                    k = g * PAIR + par
                    if earlier(g, par, PAIR, 2):
                        dve.wait_ge(s_tr, k - 1)
                    for i in range(BT):
                        normalise_tile(nc, t.x, mv, rstd, xhat[:, par, i, :], k * BT + i).then_inc(s_xhat, 1)

                def centre(g, par):
                    k = g * PAIR + par
                    dve.wait_ge(s_q, k + 1)
                    qp = pQ[:, par, :, :].rearrange("p t (h e) -> p (t h) e", e=DH)
                    nc.vector.tensor_reduce(m1[:, par, :], qp, AX.X, ALU.add).then_inc(s_sum, 1)
                    dve.wait_ge(s_sum, k * 2 + 1)
                    nc.vector.tensor_scalar(m1[:, par, :], m1[:, par, :], 1.0 / DH, None, ALU.mult).then_inc(s_sum, 1)
                    dve.wait_ge(s_sum, k * 2 + 2)
                    nc.vector.tensor_tensor(of_block(qc, k), qp, heads(m1[:, par, :], P, G), ALU.subtract).then_inc(s_qc, 1)

                def sums(g, par):
                    k = g * PAIR + par
                    dve.wait_ge(s_sq, k + 1)
                    nc.vector.tensor_reduce(of_block(m2, k), qs[:, par, :, :], AX.X, ALU.add).then_inc(s_m2, 1)

                def slot(unit):
                    if unit(TRANSPOSE):
                        normalised(*unit(TRANSPOSE))
                    if unit(CENTRE):
                        centre(*unit(CENTRE))
                    if unit(SUM):
                        sums(*unit(SUM))
                slots(dve, NBLK // PAIR, PAIR, SUM, slot)
                dve.wait_ge(s_qstd, 1)
                nc.vector.reciprocal(m3[:, :], m2[:, :]).then_inc(s_m3, 1)
                dve.wait_ge(s_m3, 1)
                dve.sem_inc(s_qt, PAIR)
                with dve.Fori(0, NBLK // PAIR) as g:
                    for par in range(PAIR):
                        k = g * PAIR + par
                        dve.wait_ge(s_qt, k + 1)
                        nc.vector.tensor_tensor(qn[:, par, :, :], of_block(qc, k),
                                                heads(of_block(m3, k), P, G), ALU.mult).then_inc(s_qn, 1)


def build_cross_attention(nc, t, d):
    ctx = ExitStack()
    with ctx:
        def sb(name, shape, dt):
            return ctx.enter_context(nc.sbuf_tensor(name, shape, dt))

        def pb(name, shape, dt):
            return ctx.enter_context(nc.psum_tensor(name, shape, dt))

        def sem(name):
            return t.ctx.enter_context(nc.semaphore(name))

        HC = H // KC
        UN = TPB * KC
        SLOTS = 4
        wo = sb("wo", [P, KC, D], fp32)
        bo = sb("bo", [P, D], fp32)
        mask = sb("mask", [P, S2], fp32)
        od = sb("od", [P, 2, D], fp32)
        qT = sb("qT", [P, 2, KC, P], fp32)
        ss = sb("ss", [P, SLOTS, HC, S2], fp32)
        mx = sb("mx", [P, 2, HC], fp32)
        pT = sb("ypT", [S2, 2, HC, P], fp32)
        on = sb("yon", [P, 2, H, VW], fp32)
        rr = sb("yrr", [P, 2, H], fp32)
        oT = sb("oT", [P, 2, KC, P], fp32)
        ps = pb("yps", [P, 2, 2, 512], fp32)
        pt = pb("ypt", [S2, 2, 512], fp32)
        po = pb("ypo", [P, 512], fp32)
        pw = pb("pw", [P, 2, D], fp32)

        s_ld = sem("y_loads")
        s_xb = sem("y_xb")
        s_qts = sem("y_qts")
        s_s = sem("y_s")
        s_mx = sem("y_mx")
        s_sub = sem("y_sub")
        s_exp = sem("y_exp")
        s_pt = sem("y_pt")
        s_pts = sem("y_pts")
        s_o = sem("y_o")
        s_on = sem("y_on")
        s_rr = sem("y_rr")
        s_norm = sem("y_norm")
        s_ot = sem("y_ot")
        s_ots = sem("y_ots")
        s_w = sem("y_w")
        s_add = sem("y_add")
        s_go = sem("y_go")
        s_free = sem("y_free")

        QUERIES, SCORES, TURN, WEIGHT, DIVIDE, BACK, PRODUCT, ADD = 0, 1, 2, 3, 5, 5, 6, 7
        def tile_of(unit):
            return None if unit is None or unit[1] % 2 else (unit[0], unit[1] // 2)

        with nc.Block() as block:
            @block.sync
            def _(sp):
                sp.dma_start(wo[:, :, :], d["xwo"].rearrange("(c p) o -> p c o", p=P)).then_inc(s_ld, 16)
                sp.dma_start(bo[:, :], d["bo"].partition_broadcast(P)).then_inc(s_ld, 16)
                sp.dma_start(mask[:, :], d["mask"]).then_inc(s_ld, 16)

            @block.gpsimd
            def _(pool):
                pool.wait_ge(s_ld, 48)
                for b in range(B):
                    nc.gpsimd.tensor_tensor(t.x[:, b * TPB:(b + 1) * TPB, :], t.x[:, b * TPB:(b + 1) * TPB, :],
                                            bo[:, :].unsqueeze(1).to_broadcast([P, TPB, D]), ALU.add).then_inc(s_xb, 1)

            @block.tensor
            def _(pe):
                pe.wait_ge(s_ld, 48)

                def scores(b, u):
                    tile, c = u // KC, u % KC
                    if c == 0:
                        pe.wait_ge(s_qts, b * TPB + tile + 1)
                    if earlier(b, u, UN, 2):
                        pe.wait_ge(s_sub, b * UN + u - 1)
                    for j in range(2):
                        last = nc.tensor.matmul(ps[:, u % 2, j, 0:HC // 2 * S2], qT[:, tile % 2, c, :],
                                                t.kbd[:, c, bass.ds(b, 1), j * HC // 2:(j + 1) * HC // 2, :],
                                                start=True, stop=True)
                    last.then_inc(s_s, 1)

                def transposes(b, u):
                    pe.wait_ge(s_exp, b * UN + u + 1)
                    if earlier(b, u, UN, 1):
                        pe.wait_ge(s_pts, b * UN + u)
                    for h in range(HC):
                        last = nc.tensor.transpose(pt[:, h // 4, h % 4 * P:(h % 4 + 1) * P], ss[:, u % SLOTS, h, :],
                                                   t.ident[:, :])
                    last.then_inc(s_pt, 1)

                def weighted(b, u):
                    tile, c = u // KC, u % KC
                    pe.wait_ge(s_pts, b * UN + u + 1)
                    if c == 0 and earlier(b, u, UN, KC):
                        pe.wait_ge(s_on, b * TPB + tile)
                    for h in range(HC):
                        last = nc.tensor.matmul(po[:, (c * HC + h) * VW:(c * HC + h + 1) * VW],
                                                pT[:, u % 2, h, :],
                                                t.cv[:, bass.ds(b, 1), c * HC + h, :], start=True, stop=True)
                    last.then_inc(s_o, 1)

                def turned(b, tile):
                    pe.wait_ge(s_norm, b * TPB + tile + 1)
                    if earlier(b, tile * KC, UN, KC):
                        pe.wait_ge(s_add, b * TPB + tile)
                    for c in range(KC):
                        last = nc.tensor.transpose(pw[:, 0, c * P:(c + 1) * P],
                                                   od[:, tile % 2, c * P:(c + 1) * P], t.ident[:, :])
                    last.then_inc(s_ot, 1)

                def output(b, tile):
                    pe.wait_ge(s_ots, b * TPB + tile + 1)
                    for c in range(KC):
                        last = nc.tensor.matmul(pw[:, 1, :], oT[:, tile % 2, c, :], wo[:, c, :],
                                                start=c == 0, stop=c == KC - 1)
                    last.then_inc(s_w, 1)

                def slot(unit):
                    if unit(SCORES):
                        scores(*unit(SCORES))
                    if unit(TURN):
                        transposes(*unit(TURN))
                    if tile_of(unit(PRODUCT)):
                        output(*tile_of(unit(PRODUCT)))
                    if unit(WEIGHT):
                        weighted(*unit(WEIGHT))
                    if tile_of(unit(BACK)):
                        turned(*tile_of(unit(BACK)))
                slots(pe, B, UN, ADD, slot)

            @block.scalar
            def _(act):
                act.wait_ge(s_ld, 48)

                def queries(b, tile):
                    if earlier(b, tile * KC, UN, 2 * KC):
                        act.wait_ge(s_s, b * UN + (tile - 1) * KC)
                    nc.scalar.activation(qT[:, tile % 2, :, :], t.qT[:, bass.ds(b * TPB + tile, 1), :, :]
                                         .rearrange("p t c n -> p (t c) n"),
                                         ACT.Identity, scale=t.lncol[:, 0:1], bias=t.lncol[:, 1:2]).then_inc(s_qts, 1)

                def back(b, tile):
                    act.wait_ge(s_ot, b * TPB + tile + 1)
                    nc.scalar.activation(oT[:, tile % 2, :, :], pw[:, 0, :].rearrange("p (c n) -> p c n", c=KC),
                                         ACT.Copy).then_inc(s_ots, 1)

                def transposed(b, u):
                    act.wait_ge(s_pt, b * UN + u + 1)
                    if earlier(b, u, UN, 2):
                        act.wait_ge(s_o, b * UN + u - 1)
                    nc.scalar.activation(pT[:, u % 2, :, :].rearrange("s (j h) n -> s j (h n)", j=2),
                                         pt[:, :, :], ACT.Copy).then_inc(s_pts, 1)

                def exponentials(b, u):
                    act.wait_ge(s_sub, b * UN + u + 1)
                    nc.scalar.activation(ss[:, u % SLOTS, :, :], ss[:, u % SLOTS, :, :], ACT.Exp,
                                         scale=D ** -0.5).then_inc(s_exp, 1)

                def slot(unit):
                    if tile_of(unit(QUERIES)):
                        queries(*tile_of(unit(QUERIES)))
                    if tile_of(unit(BACK + 1)):
                        back(*tile_of(unit(BACK + 1)))
                    if unit(TURN):
                        transposed(*unit(TURN))
                    if unit(SCORES):
                        exponentials(*unit(SCORES))
                slots(act, B, UN, ADD, slot)

            @block.vector
            def _(dve):
                dve.wait_ge(s_ld, 48)

                def less_maximum(b, u):
                    tile = u // KC
                    dve.wait_ge(s_s, b * UN + u + 1)
                    if earlier(b, u, UN, SLOTS):
                        dve.wait_ge(s_pt, b * UN + u - SLOTS + 1)
                    sp4 = ps[:, u % 2, :, 0:HC // 2 * S2].rearrange("p j (h s) -> p j h s", s=S2)
                    out4 = ss[:, u % SLOTS, :, :].rearrange("p (j h) s -> p j h s", j=2)
                    if tile == 0:
                        m4 = mask[:, :].unsqueeze(1).to_broadcast([P, HC // 2, S2])
                        for j in range(2):
                            nc.vector.tensor_tensor(out4[:, j, :, :], sp4[:, j, :, :], m4, ALU.add).then_inc(s_go, 1)
                        dve.wait_ge(s_go, b * 4 + u * 2 + 2)
                        src = out4
                    else:
                        src = sp4
                    nc.vector.tensor_reduce(mx[:, u % 2, :].rearrange("p (j h) -> p j h", j=2), src, AX.X,
                                            ALU.max).then_inc(s_mx, 1)
                    dve.wait_ge(s_mx, b * UN + u + 1)
                    for j in range(2):
                        last = nc.vector.tensor_tensor(
                            out4[:, j, :, :], src[:, j, :, :],
                            mx[:, u % 2, j * HC // 2:(j + 1) * HC // 2].unsqueeze(2).to_broadcast([P, HC // 2, S2]),
                            ALU.subtract)
                    last.then_inc(s_sub, 1)

                def divide(b, tile):
                    dve.wait_ge(s_o, b * UN + 2 * tile + 2)
                    nc.vector.tensor_copy(on[:, tile % 2, :, :],
                                          po[:, 0:H * VW].rearrange("p (h e) -> p h e", e=VW)).then_inc(s_on, 1)
                    dve.wait_ge(s_on, b * TPB + tile + 1)
                    nc.vector.reciprocal(rr[:, tile % 2, :], on[:, tile % 2, :, DH]).then_inc(s_rr, 1)
                    dve.wait_ge(s_rr, b * TPB + tile + 1)
                    nc.vector.tensor_tensor(od[:, tile % 2, :].rearrange("p (h e) -> p h e", e=DH),
                                            on[:, tile % 2, :, 0:DH],
                                            rr[:, tile % 2, :].unsqueeze(2).to_broadcast([P, H, DH]),
                                            ALU.mult).then_inc(s_norm, 1)

                def add(b, tile):
                    if tile == 0:
                        dve.wait_ge(s_xb, b + 1)
                    dve.wait_ge(s_w, b * TPB + tile + 1)
                    xs = t.x[:, bass.ds(b * TPB + tile, 1), :]
                    nc.vector.tensor_tensor(xs, xs, pw[:, 1, :].unsqueeze(1), ALU.add).then_inc(s_add, 1)

                def slot(unit):
                    if tile_of(unit(ADD)):
                        add(*tile_of(unit(ADD)))
                    if tile_of(unit(DIVIDE)):
                        divide(*tile_of(unit(DIVIDE)))
                    if unit(SCORES):
                        less_maximum(*unit(SCORES))
                slots(dve, B, UN, ADD, slot)


def build_experts(nc, t, d):
    fp32r = mybir.dt.float32r
    NE = E + 1
    FW = NE * F
    CH = -(-FW // P)
    GC = E * F // P
    rows = [min(P, FW - c * P) for c in range(CH)]
    outer = ExitStack()
    with outer:
        def sem(name):
            return t.ctx.enter_context(nc.semaphore(name))

        def keep(name, shape, dt):
            return outer.enter_context(nc.sbuf_tensor(name, shape, dt))

        wg = [keep(f"wg{n}", [P, KC, FW], fp32r) for n in ("_high", "_low")]
        wu = [keep(f"wu{n}", [P, KC, FW], fp32r) for n in ("_high", "_low")]
        wd = [keep(f"wd{n}", [P, CH, D], fp32r) for n in ("_high", "_low")]
        xT = keep("zxT", [P, NBLK, KC, BLK], fp32)
        gT = keep("gT", [2 * E, NT * P], fp32r)

        with ExitStack() as ctx:
            def sb(name, shape, dt):
                return ctx.enter_context(nc.sbuf_tensor(name, shape, dt))

            def pb(name, shape, dt):
                return ctx.enter_context(nc.psum_tensor(name, shape, dt))

            PIECE = CH // 2 * D
            raw = sb("raw", [P, 2, PIECE], fp32)
            wr = sb("zwr", [P, KC, E], fp32)
            eb = sb("eb", [P, E], fp32)
            order = sb("order", [P, E], fp32)
            epsc = sb("zepsc", [P, 1], fp32)
            stats = sb("zstats", [P, BT, 6], fp32)
            aggr = sb("zaggr", [P, BT, 2], fp32)
            mv = sb("zmv", [P, NT, 2], fp32)
            std = sb("zstd", [P, NT], fp32)
            rstd = sb("zrstd", [P, NT], fp32)
            xhat = sb("zxhat", [P, 2, BT, D], fp32)
            xb = sb("zxb", [P, 2, KC, BLK], fp32)
            s0 = sb("s0", [P, NT, E], fp32)
            s1 = sb("s1", [P, NT, E], fp32)
            c1 = sb("c1", [P, NT, E], fp32)
            o1 = sb("o1", [P, NT, E], fp32)
            o2 = sb("o2", [P, NT, E], fp32)
            ms = sb("ms", [P, NT], fp32)
            gate = sb("gate", [P, NT, E], fp32)
            gp = sb("gp", [P, NT, 2 * E], fp32r)
            pT = pb("zpT", [P, 2, KC, BLK], fp32)
            pL = pb("pL", [P, 2, 512], fp32)
            pg = pb("pgT", [2 * E, 2, BLK], fp32)

            s_raw = [sem(f"z_raw{i}") for i in range(2)]
            s_split = sem("z_split")
            s_wr = sem("z_router")
            s_const = sem("z_const")
            s_aggr = sem("z_aggr")
            s_mv = sem("z_mv")
            s_std = sem("z_std")
            s_rstd = sem("z_rstd")
            s_xhat = sem("z_xhat")
            s_tr = sem("z_tr")
            s_xb = sem("z_xb")
            s_xT = sem("z_xT")
            s_lg = sem("z_lg")
            s_lgs = sem("z_lgs")
            s_sig = sem("z_sig")
            s_r = sem("z_r")
            s_gp = sem("z_gp")
            s_gt = sem("z_gt")
            s_gts = sem("z_gts")

            pieces = [(wg, 0), (wg, 1), (wu, 0), (wu, 1), (wd, 0), (wd, 1)]
            loads = [2, 2, 2, 2, 1, 3]

            with nc.Block() as block:
                @block.sync
                def _(sp):
                    sp.dma_start(wr[:, :, :], d["router"].rearrange("(c p) e -> p c e", p=P)).then_inc(s_wr, 16)
                    sp.dma_start(eb[:, :], d["ebias"].partition_broadcast(P)).then_inc(s_wr, 16)
                    sp.wait_ge(s_const, 1)
                    for n, (dst, part) in enumerate(pieces):
                        if n >= 2:
                            sp.wait_ge(s_split, 2 * (n - 1))
                        r = raw[:, n % 2, :]
                        if dst is not wd:
                            e, s = ("eg", "sg") if dst is wg else ("eu", "su")
                            sp.dma_start(r[:, 0:E * F].rearrange("p (e f) -> p e f", f=F),
                                         d[e][:, part * P:(part + 1) * P, :].rearrange("e p f -> p e f")).then_inc(s_raw[n % 2], 16)
                            sp.dma_start(r[:, E * F:FW], d[s][part * P:(part + 1) * P, :]).then_inc(s_raw[n % 2], 16)
                            continue
                        flat = d["ed"].rearrange("e f o -> (e f) o")
                        lo, hi = part * CH // 2, min((part + 1) * CH // 2, GC)
                        sp.dma_start(r[:, 0:(hi - lo) * D].rearrange("p (c o) -> p c o", o=D),
                                     flat[lo * P:hi * P, :].rearrange("(c p) o -> p c o", p=P)).then_inc(s_raw[n % 2], 16)
                        if part == 1:
                            for c in (GC, GC + 1):
                                sp.dma_start(raw[0:rows[c], n % 2, (c - lo) * D:(c - lo + 1) * D],
                                             d["sd"][(c - GC) * P:(c - GC) * P + rows[c], :]).then_inc(s_raw[n % 2], 16)

                @block.gpsimd
                def _(pool):
                    nc.gpsimd.memset(raw[:, 1, :], 0.0).then_inc(s_const, 1)
                    nc.gpsimd.memset(epsc[:, :], EPS).then_inc(s_const, 1)
                    for e in range(E):
                        nc.gpsimd.memset(order[:, e:e + 1], float(E - e)).then_inc(s_const, 1)

                    def split(n):
                        dst, part = pieces[n]
                        pool.wait_ge(s_raw[n % 2], 16 * sum(loads[n % 2:n + 1:2]))
                        if dst is wd:
                            hi, lo = (w[:, part * CH // 2:(part + 1) * CH // 2, :].rearrange("p c o -> p (c o)") for w in dst)
                            r = raw[:, n % 2, :]
                        else:
                            hi, lo = (w[:, part, :] for w in dst)
                            r = raw[:, n % 2, 0:FW]
                        nc.gpsimd.tensor_copy(hi, r).then_inc(s_split, 1)
                        pool.wait_ge(s_split, 2 * n + 1)
                        nc.gpsimd.tensor_tensor(lo, r, hi.bitcast(fp32), ALU.subtract).then_inc(s_split, 1)

                    for n in range(len(pieces)):
                        split(n)

                @block.tensor
                def _(pe):
                    pe.wait_ge(s_wr, 32)

                    def logits(k, par):
                        pe.wait_ge(s_xb, k + 1)
                        pe.wait_ge(s_lgs, k + 1)
                        for i in range(BT):
                            for c in range(KC):
                                last = nc.tensor.matmul(pL[:, par, i * E:(i + 1) * E], xb[:, par, c, i * P:(i + 1) * P],
                                                        wr[:, c, :], start=c == 0, stop=c == KC - 1)
                        last.then_inc(s_lg, 1)

                    with pe.Fori(0, NBLK // 2) as kk:
                        for par in range(2):
                            k = kk * 2 + par
                            for i in range(BT):
                                pe.wait_ge(s_xhat, k * BT + i + 1)
                                for c in range(KC):
                                    last = nc.tensor.transpose(pT[:, par, c, i * P:(i + 1) * P],
                                                               xhat[:, par, i, c * P:(c + 1) * P], t.ident[:, :])
                            last.then_inc(s_tr, 1)
                        for par in range(2):
                            logits(kk * 2 + par, par)
                    for k in range(NBLK):
                        pe.wait_ge(s_gp, 2)
                        if k >= 2:
                            pe.wait_ge(s_gts, k - 1)
                        for i in range(BT):
                            last = nc.tensor.transpose(pg[:, k % 2, i * P:(i + 1) * P],
                                                       gp[:, k * BT + i, :].bitcast(fp32), t.ident[:, :])
                        last.then_inc(s_gt, 1)

                @block.scalar
                def _(act):
                    act.wait_ge(s_const, 2)
                    act.wait_ge(s_mv, NBLK)
                    nc.scalar.activation(std[:, :], mv[:, :, 1], ACT.Sqrt, bias=epsc[:, :]).then_inc(s_std, 1)
                    with act.Fori(0, NBLK // 2) as kk:
                        for par in range(2):
                            k = kk * 2 + par
                            act.wait_ge(s_tr, k + 1)
                            act.wait_ge(s_xT, k + 1)
                            nc.scalar.activation(xb[:, par, :, :], pT[:, par, :, :], ACT.Copy).then_inc(s_xb, 1)
                    act.wait_ge(s_lgs, NBLK + 2)
                    nc.scalar.activation(s0[:, :, :], c1[:, :, :], ACT.Sigmoid).then_inc(s_sig, 1)
                    for k in range(NBLK):
                        act.wait_ge(s_gt, k + 1)
                        nc.scalar.activation(gT[:, k * BLK:(k + 1) * BLK], pg[:, k % 2, :], ACT.Copy).then_inc(s_gts, 1)

                @block.vector
                def _(dve):
                    dve.wait_ge(s_const, 2 + E)
                    dve.sem_inc(s_lgs, 2)
                    dve.sem_inc(s_xT, 2)
                    layer_statistics(nc, dve, t.x, stats, aggr, mv, s_aggr, s_mv)
                    dve.wait_ge(s_std, 1)
                    nc.vector.reciprocal(rstd[:, :], std[:, :]).then_inc(s_rstd, 1)
                    dve.wait_ge(s_rstd, 1)
                    with dve.Fori(0, NBLK // 2) as kk:
                        for par in range(2):
                            k = kk * 2 + par
                            for i in range(BT):
                                normalise_tile(nc, t.x, mv, rstd, xhat[:, par, i, :], k * BT + i).then_inc(s_xhat, 1)
                        for par in range(2):
                            k = kk * 2 + par
                            dve.wait_ge(s_xb, k + 1)
                            nc.vector.tensor_copy(xT[:, bass.ds(k, 1), :, :].rearrange("p k c n -> p (k c) n"),
                                                  xb[:, par, :, :]).then_inc(s_xT, 1)
                        for par in range(2):
                            k = kk * 2 + par
                            dve.wait_ge(s_lg, k + 1)
                            nc.vector.tensor_copy(c1[:, bass.ds(k * BT, BT), :],
                                                  pL[:, par, 0:BT * E].rearrange("p (t e) -> p t e", e=E)).then_inc(s_lgs, 1)
                    dve.wait_ge(s_sig, 1)
                    dve.wait_ge(s_wr, 32)
                    steps = [0]

                    def link(op):
                        steps[0] += 1
                        op.then_inc(s_r, 1)
                        dve.wait_ge(s_r, steps[0])

                    def wide(v):
                        return v.unsqueeze(2).to_broadcast([P, NT, E])

                    ebw = eb[:, :].unsqueeze(1).to_broadcast([P, NT, E])
                    orw = order[:, :].unsqueeze(1).to_broadcast([P, NT, E])
                    link(nc.vector.tensor_tensor(s1[:, :, :], s0[:, :, :], ebw, ALU.add))
                    for chosen in (o1, o2):
                        link(nc.vector.tensor_reduce(ms[:, :], s1[:, :, :], AX.X, ALU.max))
                        link(nc.vector.tensor_tensor(c1[:, :, :], s1[:, :, :], wide(ms[:, :]), ALU.is_equal))
                        link(nc.vector.tensor_tensor(c1[:, :, :], c1[:, :, :], orw, ALU.mult))
                        link(nc.vector.tensor_reduce(ms[:, :], c1[:, :, :], AX.X, ALU.max))
                        link(nc.vector.tensor_tensor(chosen[:, :, :], c1[:, :, :], wide(ms[:, :]), ALU.is_equal))
                        if chosen is o1:
                            link(nc.vector.scalar_tensor_tensor(s1[:, :, :], o1[:, :, :], -3e38, s1[:, :, :],
                                                                ALU.mult, ALU.add))
                    link(nc.vector.tensor_tensor(o1[:, :, :], o1[:, :, :], o2[:, :, :], ALU.add))
                    link(nc.vector.tensor_tensor(o1[:, :, :], o1[:, :, :], s0[:, :, :], ALU.mult))
                    link(nc.vector.tensor_reduce(ms[:, :], o1[:, :, :], AX.X, ALU.add))
                    link(nc.vector.tensor_scalar(ms[:, :], ms[:, :], 1e-20, None, ALU.add))
                    link(nc.vector.reciprocal(ms[:, :], ms[:, :]))
                    link(nc.vector.tensor_tensor(gate[:, :, :], o1[:, :, :], wide(ms[:, :]), ALU.mult))
                    nc.vector.tensor_copy(gp[:, :, 0:E], gate[:, :, :]).then_inc(s_gp, 1)
                    dve.wait_ge(s_gp, 1)
                    nc.vector.tensor_tensor(gp[:, :, E:2 * E], gate[:, :, :], gp[:, :, 0:E].bitcast(fp32),
                                            ALU.subtract).then_inc(s_gp, 1)

        with ExitStack() as ctx:
            def sb(name, shape, dt):
                return ctx.enter_context(nc.sbuf_tensor(name, shape, dt))

            def pb(name, shape, dt):
                return ctx.enter_context(nc.psum_tensor(name, shape, dt))

            sraw = sb("sraw", [2 * E, GC * P], fp32)
            spread = sb("spread", [2 * E, GC * P], fp32r)
            xh = sb("xh", [P, 2, KC, BLK], fp32r)
            xl = sb("xl", [P, 2, KC, BLK], fp32r)
            sg = sb("sg", [P, 2, BLK], fp32)
            hid = sb("hid", [P, 2, BLK], fp32)
            hh = sb("hh", [P, 2, BLK], fp32r)
            hl = sb("hl", [P, 2, BLK], fp32r)
            pG = pb("pG", [P, 2, BLK], fp32)
            pU = pb("zpU", [P, 2, BLK], fp32)
            pB = pb("zpB", [P, 2, BLK], fp32)
            pO = pb("zpO", [P, 2, 2, D], fp32)

            s_sel = sem("w_sel")
            s_spread = sem("w_spread")
            s_xh = sem("w_xh")
            s_xl = sem("w_xl")
            s_gu = sem("w_gu")
            s_sg = sem("w_sg")
            s_t1 = sem("w_t1")
            s_h = sem("w_h")
            s_free = sem("w_free")
            s_hi = sem("w_hi")
            s_lo = sem("w_lo")
            s_dn = sem("w_dn")
            s_acc = sem("w_acc")
            s_out = sem("w_out")

            def blocks(eng, step):
                step(0, False, True)
                with eng.Fori(1, NBLK - 1) as k:
                    step(k, True, True)
                step(NBLK - 1, True, False)

            def after(k, c, lag):
                return c >= lag or type(k) is not int or k > 0

            with nc.Block() as block:
                @block.sync
                def _(sp):
                    sp.dma_start(sraw[:, :], d["spread"]).then_inc(s_sel, 16)
                    for k in range(NBLK):
                        sp.wait_ge(s_acc, k + 1)
                        b, i = k // 2, k % 2 * BT
                        sp.dma_start(d["out"][b, i * P:(i + BT) * P, :].rearrange("(t p) e -> p t e", p=P),
                                     t.x[:, k * BT:(k + 1) * BT, :]).then_inc(s_out, 16)
                    sp.wait_ge(s_out, NBLK * 16)

                @block.tensor
                def _(pe):
                    pe.wait_ge(s_spread, 1)
                    terms = ((0, 0), (0, 1), (1, 0))

                    def up(k, c):
                        v, m, par = k * CH + c, rows[c], c % 2
                        if after(k, c, 2):
                            pe.wait_ge(s_h, v - 1)
                            pe.sem_inc(s_free, 1)
                        for w, bank in ((wg, pG), (wu, pU)):
                            n = 0
                            for kc in range(KC):
                                for a, b in terms:
                                    last = nc.tensor.matmul(bank[0:m, par, :], w[a][:, kc, c * P:c * P + m],
                                                            (xh, xl)[b][:, bass.ds(k % 2, 1), kc, :] if type(k) is not int
                                                            else (xh, xl)[b][:, k % 2, kc, :],
                                                            start=n == 0, stop=n == KC * 3 - 1)
                                    n += 1
                        if c < GC:
                            gates = gT[:, bass.ds(k * BLK, BLK)]
                            last = nc.tensor.matmul(pB[:, par, :], spread[:, c * P:(c + 1) * P], gates,
                                                    start=True, stop=True)
                        last.then_inc(s_gu, 1)

                    def down(k, c):
                        v, m, par = k * CH + c, rows[c], c % 2
                        pe.wait_ge(s_lo, v + 1)
                        if c == 0 and (type(k) is not int or k > 0):
                            pe.wait_ge(s_acc, k)
                        for i in range(BT):
                            for n, (a, b) in enumerate(terms):
                                last = nc.tensor.matmul(pO[:, i // 2, i % 2, :], (hh, hl)[a][0:m, par, i * P:(i + 1) * P],
                                                        wd[b][0:m, c, :], start=c == 0 and n == 0 and i % 2 == 0,
                                                        stop=c == CH - 1 and n == 2, skip_group_check=True)
                        last.then_inc(s_dn, 1)

                    def step(k, late, ahead):
                        pe.wait_ge(s_xl, k + 1)
                        for c in range(CH):
                            up(k, c)
                            if c >= 2:
                                down(k, c - 2)
                            elif late:
                                down(k - 1, c + CH - 2)
                    blocks(pe, step)
                    down(NBLK - 1, CH - 2)
                    down(NBLK - 1, CH - 1)

                @block.scalar
                def _(act):
                    def high(k, c):
                        v = k * CH + c
                        act.wait_ge(s_h, v + 1)
                        if after(k, c, 2):
                            act.wait_ge(s_dn, v - 1)
                        nc.scalar.activation(hh[0:rows[c], c % 2, :], hid[0:rows[c], c % 2, :], ACT.Copy).then_inc(s_hi, 1)

                    def xhigh(k):
                        nc.scalar.activation(xh[:, bass.ds(k % 2, 1), :, :].rearrange("p k c n -> p (k c) n"),
                                             xT[:, bass.ds(k, 1), :, :].rearrange("p k c n -> p (k c) n"),
                                             ACT.Copy).then_inc(s_xh, 1)

                    def step(k, late, ahead):
                        for c in range(CH):
                            if c > 0:
                                high(k, c - 1)
                            elif late:
                                high(k - 1, CH - 1)
                            act.wait_ge(s_gu, k * CH + c + 1)
                            nc.scalar.activation(sg[0:rows[c], c % 2, :], pG[0:rows[c], c % 2, :], ACT.Silu).then_inc(s_sg, 1)
                            if c == 8 and ahead:
                                xhigh(k + 1)
                    xhigh(0)
                    blocks(act, step)
                    high(NBLK - 1, CH - 1)

                @block.vector
                def _(dve):
                    dve.wait_ge(s_sel, 16)
                    nc.vector.tensor_copy(spread[:, :], sraw[:, :]).then_inc(s_spread, 1)

                    def low(k, c):
                        m, par = rows[c], c % 2
                        dve.wait_ge(s_hi, k * CH + c + 1)
                        nc.vector.tensor_tensor(hl[0:m, par, :], hid[0:m, par, :], hh[0:m, par, :].bitcast(fp32),
                                                ALU.subtract).then_inc(s_lo, 1)

                    def xlow(k):
                        dve.wait_ge(s_xh, k + 1)
                        nc.vector.tensor_tensor(xl[:, bass.ds(k % 2, 1), :, :].rearrange("p k c n -> p (k c) n"),
                                                xT[:, bass.ds(k, 1), :, :].rearrange("p k c n -> p (k c) n"),
                                                xh[:, bass.ds(k % 2, 1), :, :].rearrange("p k c n -> p (k c) n").bitcast(fp32),
                                                ALU.subtract).then_inc(s_xl, 1)

                    def hidden(k, c):
                        v, m, par = k * CH + c, rows[c], c % 2
                        dve.wait_ge(s_sg, v + 1)
                        if c < GC:
                            nc.vector.tensor_tensor(sg[0:m, par, :], sg[0:m, par, :], pU[0:m, par, :], ALU.mult).then_inc(s_t1, 1)
                            dve.wait_ge(s_t1, k * GC + c + 1)
                            nc.vector.tensor_tensor(hid[0:m, par, :], sg[0:m, par, :], pB[0:m, par, :], ALU.mult).then_inc(s_h, 1)
                        else:
                            nc.vector.tensor_tensor(hid[0:m, par, :], sg[0:m, par, :], pU[0:m, par, :], ALU.mult).then_inc(s_h, 1)

                    def total(k):
                        dve.wait_ge(s_dn, (k + 1) * CH)
                        for j in range(2):
                            xs = t.x[:, bass.ds(k * BT + 2 * j, 2), :]
                            last = nc.vector.tensor_tensor(xs, xs, pO[:, j, :, :], ALU.add)
                        last.then_inc(s_acc, 1)

                    def step(k, late, ahead):
                        for c in range(CH):
                            if c > 0:
                                low(k, c - 1)
                            elif late:
                                low(k - 1, CH - 1)
                            if c == 2 and late:
                                total(k - 1)
                            hidden(k, c)
                            if c == 8 and ahead:
                                xlow(k + 1)
                    xlow(0)
                    blocks(dve, step)
                    low(NBLK - 1, CH - 1)
                    total(NBLK - 1)


class Chip:
    pass


def build_program(nc, d):
    t = Chip()
    t.ctx = ExitStack()
    with t.ctx:
        def sb(ctx, name, shape):
            return ctx.enter_context(nc.sbuf_tensor(name, shape, fp32))

        t.x = sb(t.ctx, "x_sb", [P, NT, D])
        t.ident = sb(t.ctx, "ident_sb", [P, P])
        t.s_ident = t.ctx.enter_context(nc.semaphore("s_ident"))
        with ExitStack() as ctx:
            t.vx = sb(ctx, "vx", [P, NT, H, VW])
            build_projections(nc, t, d)
            build_attention(nc, t, d)
        with ExitStack() as ctx:
            t.qT = sb(ctx, "qT_sb", [P, NT, KC, P])
            t.kbd = sb(ctx, "kbd", [P, KC, B, H // KC, S2])
            t.cv = sb(ctx, "cv", [S2, B, H, VW])
            t.lncol = sb(ctx, "lncol_sb", [P, 4])
            build_cross_queries(nc, t, d)
            build_cross_attention(nc, t, d)
        build_experts(nc, t, d)


def constants():
    import numpy as np
    inv = (1.0 / np.float32(10000.0) ** (np.arange(0, D, 2, dtype=np.float32) / np.float32(D))).astype(np.float32)
    pos = np.arange(-(L - 1), L, dtype=np.float32)
    ang = (inv[:, None] * pos[None, :]).astype(np.float32)
    basis = np.zeros((D, RW), np.float32)
    basis[0::2, 1:] = np.sin(ang)
    basis[1::2, 1:] = np.cos(ang)
    sel = np.zeros((P, VW), np.float32)
    for p in range(P):
        if p % 32 < VW:
            sel[p, p % 32] = 1.0
    expert = np.arange(E * F) // F
    spread = (expert[None, :] == np.arange(2 * E)[:, None] % E).astype(np.float32)
    headmask = (np.arange(P)[:, None] // DH == np.arange(H // KC)[None, :]).astype(np.float32)
    mask = np.where(np.arange(S2)[None, :] <= np.arange(P)[:, None], 0.0, -1e30).astype(np.float32)
    return {"basis": basis, "ident": np.eye(P, dtype=np.float32), "sel": sel, "headmask": headmask, "mask": mask,
            "spread": spread}


def kernel(**inputs):
    import numpy as np
    import concourse.bacc as bacc
    from concourse.bass_utils import run_bass_kernel_spmd

    arrays = {"x": inputs["x"], "ctx": inputs["ctx_1024"]}
    for name, src in (("wq", "Wq"), ("wk", "Wk"), ("wv", "Wv"), ("wr", "Wr")):
        arrays[name] = np.asarray(inputs["L0_attn_" + src]).T
    uv = np.stack([np.asarray(inputs["L0_attn_u_bias"]), np.asarray(inputs["L0_attn_v_bias"])])
    arrays["uv"] = uv.reshape(2, KC, P).transpose(2, 0, 1)
    for name, src in (("xwq", "Wq"), ("xwk", "Wk"), ("xwv", "Wv"), ("xwo", "Wo"), ("bo", "bo")):
        arrays[name] = inputs["L0_xattn_" + src]
    cols = [np.asarray(inputs["L0_xattn_" + n]) for n in ("q_ln_w", "q_ln_b", "k_ln_w", "k_ln_b")]
    arrays["lncol"] = np.stack([np.tile(c, P // DH) for c in cols], axis=1)
    for name, src in (("router", "W_gate_router"), ("ebias", "expert_bias"), ("eg", "Wg"), ("eu", "Wu"), ("ed", "Wd"),
                      ("sg", "Wg_s"), ("su", "Wu_s"), ("sd", "Wd_s")):
        arrays[name] = inputs["L0_ffn_" + src]
    arrays.update(constants())
    arrays = {k: np.ascontiguousarray(a) for k, a in arrays.items()}
    nc = bacc.Bacc("TRN2", target_bir_lowering=False, num_devices=1)
    d = {k: nc.dram_tensor("in_" + k, a.shape, mybir.dt.from_np(a.dtype), kind="ExternalInput").ap()
         for k, a in arrays.items()}
    d["out"] = nc.dram_tensor("out_x", (B, L, D), fp32, kind="ExternalOutput").ap()
    d["qsplit"] = nc.dram_tensor("qsplit", (3, 3, D, B * L), bf16, kind="Internal").ap()
    d["rsplit"] = nc.dram_tensor("rsplit", (3, D, RW), bf16, kind="Internal").ap()
    d["ring"] = nc.dram_tensor("ring", (TPB, P, UW), fp32, kind="Internal").ap()
    build_program(nc, d)
    r = run_bass_kernel_spmd(nc, [{"in_" + k: a for k, a in arrays.items()}], core_ids=[0])
    return r.results[0]["out_x"]
```

```python
import concourse.bass as bass
from concourse import mybir
from contextlib import ExitStack

fp32 = mybir.dt.float32
bf16 = mybir.dt.bfloat16
ALU = mybir.AluOpType
ACT = mybir.ActivationFunctionType
AX = mybir.AxisListType

B, L, D = 4, 1024, 256
H, DH = 16, 16
S2 = 77
E, F = 8, 192
P = 128
NT = B * L // P
TPB = L // P
KC = D // P
BLK = 512
NBLK = B * L // BLK
BT = BLK // P
NH = B * H
RW = 2 * L
UW = L + P
UB = UW // 3
HP = P // 2
HW = L + HP
VW = DH + 1
EPS = 1e-5
TERMS = [(0, 0), (0, 1), (0, 2), (1, 0), (1, 1), (1, 2), (2, 0), (2, 1)]
QU, QV, KK = range(3)


def slots(eng, groups, size, tail, slot):
    def group(g):
        for u in range(size):
            def unit(lag):
                back = -(-max(lag - u, 0) // size)
                if type(g) is int and back > g:
                    return None
                return (g - back if back else g), u - lag + back * size
            slot(unit)
    peeled = -(-(tail + 1) // size)
    for g in range(peeled):
        group(g)
    with eng.Fori(peeled, groups) as g:
        group(g)
    for n in range(tail):
        def unit(lag):
            if n >= lag:
                return None
            back = -(-(lag - n) // size)
            return groups - back, n - lag + back * size
        slot(unit)


def earlier(g, u, size, n):
    return type(g) is not int or g * size + u >= n


def layer_statistics(nc, dve, x, stats, aggr, mv, s_aggr, s_mv):
    with dve.Fori(0, B) as b:
        for i in range(TPB):
            nc.vector.bn_stats(stats[:, i, :], x[:, bass.ds(b * TPB + i, 1), :])
        nc.vector.drain()
        for i in range(TPB):
            last = nc.vector.bn_aggr(aggr[:, i, :], stats[:, i, :])
        last.then_inc(s_aggr, 1)
        dve.wait_ge(s_aggr, b + 1)
        nc.vector.tensor_copy(mv[:, bass.ds(b * TPB, TPB), :], aggr[:, :, :]).then_inc(s_mv, 1)


def normalise_tile(nc, x, mv, rstd, xhat, tile):
    return nc.vector.tensor_scalar(xhat, x[:, bass.ds(tile, 1), :].rearrange("p t e -> p (t e)"),
                                   mv[:, bass.ds(tile, 1), 0:1].rearrange("p t v -> p (t v)"),
                                   rstd[:, bass.ds(tile, 1)], ALU.subtract, ALU.mult)


def build_projections(nc, t, d):
    ctx = ExitStack()
    with ctx:
        def sb(name, shape, dt):
            return ctx.enter_context(nc.sbuf_tensor(name, shape, dt))

        def sem(name):
            return t.ctx.enter_context(nc.semaphore(name))

        PAIR = 2
        SLOTS = 6
        FSLOTS = 4
        wT = sb("wT", [P, 4, KC, D], fp32)
        basis = sb("basis", [P, KC, RW], fp32)
        xhat = basis[:, 0, :].rearrange("p (a t e) -> p a t e", a=PAIR, t=BT)
        xT = basis[:, 1, :].rearrange("p (a c n) -> p a c n", a=PAIR, c=KC)
        uvcol = sb("uvcol", [P, 2, KC], fp32)
        uvs = sb("uvs", [P, 2, KC], fp32)
        epsc = sb("epsc", [P, 1], fp32)
        stats = sb("stats", [P, 2, BT, 6], fp32)
        mv = sb("mv", [P, NT, 2], fp32)
        std = sb("std", [P, NT], fp32)
        rstd = sb("rstd", [P, NT], fp32)
        full = sb("full", [P, FSLOTS, BLK], fp32)
        rest = sb("rest", [P, FSLOTS, BLK], fp32)
        parts = sb("parts", [P, SLOTS, 3, BLK], bf16)
        pT = ctx.enter_context(nc.psum_tensor("pT", [P, KC, BLK], fp32))
        pU = ctx.enter_context(nc.psum_tensor("pU", [P, 4, BLK], fp32))
        pV = ctx.enter_context(nc.psum_tensor("pV", [P, 2, 2, D], fp32))

        s_w = sem("s_weights")
        s_wr = sem("s_position_weights")
        s_basis = sem("s_basis")
        s_uv = sem("s_uv")
        s_x = [sem(f"s_x{i}") for i in range(B)]
        s_const = sem("s_const")
        s_uvs = sem("s_uvs")
        s_mv = sem("s_mv")
        s_std = sem("s_std")
        s_rstd = sem("s_rstd")
        s_xhat = sem("s_xhat")
        s_tr = sem("s_tr")
        s_xT = sem("s_xT")
        s_unit = sem("s_unit")
        s_full = sem("s_full")
        s_hi = sem("s_hi")
        s_rest = sem("s_rest")
        s_mid = sem("s_mid")
        s_lo = sem("s_lo")
        s_kept = [sem(f"s_kept{i}") for i in range(SLOTS)]
        s_v = sem("s_v")
        s_vx = sem("s_vx")

        RU = KC * RW // BLK
        UPB = 4
        CUTS = [(0, QU, 0), (0, QV, 0), (1, QU, 1), (1, QV, 1), (2, KK, 0), (3, KK, 1)]
        CPB = len(CUTS)
        GC = PAIR * CPB
        GROUPS = NBLK // PAIR
        NORM, TURN, COPY, WORK = 0, 3, 4, CPB
        SECOND = 2

        def block_of(unit):
            return None if unit is None or unit[1] % CPB else (unit[0], unit[1] // CPB)

        def ways(c):
            return c % SLOTS, c % FSLOTS

        with nc.Block() as block:
            @block.sync
            def _(sp):
                sp.dma_start(wT[:, 3, :, :], d["wr"].rearrange("(c p) o -> p c o", p=P)).then_inc(s_wr, 16)
                sp.dma_start(t.ident[:, :], d["ident"]).then_inc(t.s_ident, 16)
                sp.dma_start(basis[:, :, :], d["basis"].rearrange("(c p) o -> p c o", p=P)).then_inc(s_basis, 16)
                for b in range(B):
                    sp.dma_start(t.x[:, b * TPB:(b + 1) * TPB, :],
                                 d["x"][b, :, :].rearrange("(t p) e -> p t e", p=P)).then_inc(s_x[b], 16)
                for i, w in enumerate(("wq", "wk", "wv")):
                    sp.dma_start(wT[:, i, :, :], d[w].rearrange("(c p) o -> p c o", p=P)).then_inc(s_w, 16)
                sp.dma_start(uvcol[:, :, :], d["uv"]).then_inc(s_uv, 16)
                for c in range(RU):
                    sp.wait_ge(s_lo, c + 1)
                    sp.dma_start(d["rsplit"][:, (c % KC) * P:(c % KC + 1) * P,
                                             (c // KC) * BLK:(c // KC + 1) * BLK].rearrange("s p n -> p s n"),
                                 parts[:, c % SLOTS, :, :]).then_inc(s_kept[c % SLOTS], 16)
                with sp.Fori(0, GROUPS) as g:
                    for u in range(GC):
                        _, operand, chunk = CUTS[u % CPB]
                        token = sp.snap((g * PAIR + u // CPB) * BLK)
                        sp.wait_ge(s_lo, g * GC + RU + u + 1)
                        sp.dma_start(d["qsplit"][operand, :, chunk * P:(chunk + 1) * P,
                                                 bass.ds(token, BLK)].rearrange("s p n -> p s n"),
                                     parts[:, (RU + u) % SLOTS, :, :]).then_inc(s_kept[(RU + u) % SLOTS], 16)
                for slot in range(SLOTS):
                    sp.wait_ge(s_kept[slot], 16 * len([c for c in range(RU + GROUPS * GC) if c % SLOTS == slot]))

            @block.gpsimd
            def _(pool):
                nc.gpsimd.memset(epsc[:, :], EPS).then_inc(s_const, 1)
                nc.gpsimd.memset(t.vx[:, :, :, :], 1.0).then_inc(s_const, 1)

                def third(count, slot, fslot):
                    pool.wait_ge(s_mid, count)
                    nc.gpsimd.tensor_tensor(parts[:, slot, 2, :], rest[:, fslot, :], parts[:, slot, 1, :],
                                            ALU.subtract).then_inc(s_lo, 1)
                for c in range(RU):
                    third(c + 1, *ways(c))

                def group(g, positions):
                    for u in range(GC):
                        third(g * GC + RU + u + 1, *ways(RU + u))
                        if positions is not None and u % 3 == 2:
                            n = positions * (GC // 3) + u // 3
                            pool.dma_start(t.rp[n * DH:(n + 1) * DH, :, :],
                                           d["rsplit"][TERMS[n][1], :, :].rearrange("(h e) n -> e h n", e=DH)
                                           ).then_inc(t.s_rp, 16)
                for slot in range(SLOTS):
                    pool.wait_ge(s_kept[slot], 16 * len([c for c in range(RU) if c % SLOTS == slot]))
                for g in range(2):
                    group(g, g)
                with pool.Fori(2, GROUPS) as g:
                    group(g, None)

            @block.tensor
            def _(pe):
                pe.wait_ge(s_basis, 16)
                pe.wait_ge(s_wr, 16)
                for r in range(RU):
                    if r >= 4:
                        pe.wait_ge(s_full, r - 3)
                    for c in range(KC):
                        last = nc.tensor.matmul(pU[:, r % 4, :], wT[:, 3, c, (r % KC) * P:(r % KC + 1) * P],
                                                basis[:, c, (r // KC) * BLK:(r // KC + 1) * BLK],
                                                start=c == 0, stop=c == KC - 1)
                    last.then_inc(s_unit, 1)
                pe.wait_ge(s_w, 48)
                pe.wait_ge(t.s_ident, 16)

                def transposes(g, par):
                    k = g * PAIR + par
                    if earlier(g, par, PAIR, 1):
                        pe.wait_ge(s_xT, k)
                    for i in range(BT):
                        pe.wait_ge(s_xhat, k * BT + i + 1)
                        for c in range(KC):
                            last = nc.tensor.transpose(pT[:, c, i * P:(i + 1) * P],
                                                       xhat[:, par, i, c * P:(c + 1) * P], t.ident[:, :])
                    last.then_inc(s_tr, 1)

                def project(g, par, u):
                    pe.wait_ge(s_full, g * GC + par * CPB + RU - CPB + [2, 4, 5, 6][u] if earlier(g, par, PAIR, 1)
                               else RU)
                    w, oc = u // KC, u % KC
                    for c in range(KC):
                        last = nc.tensor.matmul(pU[:, u, :], wT[:, w, c, oc * P:(oc + 1) * P],
                                                xT[:, par, c, :], start=c == 0, stop=c == KC - 1)
                    last.then_inc(s_unit, 1)

                def values(g, par, pair):
                    pe.wait_ge(s_vx, (g * PAIR + par) * 2 + pair + 1)
                    for i in range(2):
                        for c in range(KC):
                            last = nc.tensor.matmul(pV[:, pair, i, :],
                                                    xT[:, par, c, (2 * pair + i) * P:(2 * pair + i + 1) * P],
                                                    wT[:, 2, c, :], start=c == 0, stop=c == KC - 1)
                    last.then_inc(s_v, 1)

                def slot(unit):
                    if block_of(unit(TURN)):
                        transposes(*block_of(unit(TURN)))
                    if unit(WORK):
                        g, u = unit(WORK)
                        par, j = u // CPB, u % CPB
                        if j == 0:
                            pe.wait_ge(s_xT, g * PAIR + par + 1)
                        if j in (1, 3):
                            values(g, par, j // 2)
                        else:
                            project(g, par, CUTS[j][0])
                slots(pe, GROUPS, GC, WORK, slot)

            @block.scalar
            def _(act):
                def first(g, c, unit, bank, scale, bias):
                    slot = c % FSLOTS
                    if type(g) is not int or g * GC + c >= SLOTS:
                        act.wait_ge(s_kept[c % SLOTS], (g * (GC // SLOTS) + c // SLOTS) * 16)
                    if type(g) is not int or g * GC + c >= FSLOTS:
                        act.wait_ge(s_rest, g * GC + c + 1 - FSLOTS)
                    act.wait_ge(s_unit, unit)
                    if bias is None:
                        nc.scalar.activation(full[:, slot, :], pU[:, bank, :], ACT.Copy, scale=scale).then_inc(s_full, 1)
                    else:
                        nc.scalar.activation(full[:, slot, :], pU[:, bank, :], ACT.Identity, scale=scale,
                                             bias=bias).then_inc(s_full, 1)

                def second(count, slot, fslot):
                    act.wait_ge(s_rest, count)
                    nc.scalar.activation(parts[:, slot, 1, :], rest[:, fslot, :], ACT.Copy).then_inc(s_mid, 1)

                for c in range(RU + SECOND):
                    if c < RU:
                        first(0, c, c + 1, c % 4, 1.0, None)
                    if c >= SECOND:
                        second(c - SECOND + 1, *ways(c - SECOND))
                act.wait_ge(s_const, 1)
                act.wait_ge(s_uvs, 1)
                act.wait_ge(s_mv, NBLK)
                nc.scalar.activation(std[:, :], mv[:, :, 1], ACT.Sqrt, bias=epsc[:, :]).then_inc(s_std, 1)

                def turned(g, par):
                    k = g * PAIR + par
                    act.wait_ge(s_tr, k + 1)
                    if earlier(g, par, PAIR, PAIR):
                        act.wait_ge(s_unit, RU + UPB * (k - 1))
                    nc.scalar.activation(xT[:, par, :, :], pT[:, :, :], ACT.Copy).then_inc(s_xT, 1)

                def slot(unit):
                    if unit(WORK):
                        g, u = unit(WORK)
                        bank, operand, chunk = CUTS[u % CPB]
                        bias = None if operand == KK else uvs[:, operand, chunk:chunk + 1]
                        first(g, RU + u, (g * PAIR + u // CPB) * UPB + RU + bank + 1, bank,
                              1.0 if operand == KK else -0.25, bias)
                    if block_of(unit(COPY)):
                        turned(*block_of(unit(COPY)))
                    if unit(WORK + SECOND):
                        g, u = unit(WORK + SECOND)
                        second(g * GC + RU + u + 1, *ways(RU + u))
                slots(act, GROUPS, GC, WORK + SECOND, slot)

            @block.vector
            def _(dve):
                dve.sem_inc(s_vx, 2)

                def cut(g, c):
                    slot, fslot = ways(c)
                    count = g * GC + c + 1
                    dve.wait_ge(s_full, count)
                    nc.vector.tensor_copy(parts[:, slot, 0, :], full[:, fslot, :]).then_inc(s_hi, 1)
                    dve.wait_ge(s_hi, count)
                    if type(g) is not int or count > FSLOTS:
                        dve.wait_ge(s_lo, count - FSLOTS)
                    nc.vector.tensor_tensor(rest[:, fslot, :], full[:, fslot, :], parts[:, slot, 0, :],
                                            ALU.subtract).then_inc(s_rest, 1)
                for c in range(RU):
                    cut(0, c)
                    if c % 2 == 0:
                        dve.wait_ge(s_x[c // 2], 16)
                    for i in range(BT):
                        nc.vector.bn_stats(stats[:, c % 2, i, :], t.x[:, c * BT + i, :])
                    nc.vector.drain()
                    for i in range(BT):
                        last = nc.vector.bn_aggr(mv[:, c * BT + i, :], stats[:, c % 2, i, :])
                    last.then_inc(s_mv, 1)
                dve.wait_ge(s_uv, 16)
                nc.vector.tensor_scalar(uvs[:, :, :], uvcol[:, :, :], -0.25, None, ALU.mult).then_inc(s_uvs, 1)
                dve.wait_ge(s_const, 2)
                dve.wait_ge(s_std, 1)
                nc.vector.reciprocal(rstd[:, :], std[:, :]).then_inc(s_rstd, 1)
                dve.wait_ge(s_rstd, 1)
                dve.wait_ge(s_unit, RU)

                def normalised(g, par):
                    k = g * PAIR + par
                    if earlier(g, par, PAIR, PAIR):
                        dve.wait_ge(s_tr, k - 1)
                    for i in range(BT):
                        normalise_tile(nc, t.x, mv, rstd, xhat[:, par, i, :], k * BT + i).then_inc(s_xhat, 1)

                def slot(unit):
                    if block_of(unit(NORM)):
                        normalised(*block_of(unit(NORM)))
                    if unit(WORK):
                        g, u = unit(WORK)
                        cut(g, RU + u)
                        if u % CPB in (2, 4):
                            k, pair = g * PAIR + u // CPB, u % CPB // 2 - 1
                            dve.wait_ge(s_v, k * 2 + pair + 1)
                            nc.vector.tensor_copy(
                                t.vx[:, bass.ds(k * BT + 2 * pair, 2), :, 0:DH],
                                pV[:, pair, :, :].rearrange("p i (h e) -> p i h e", e=DH)).then_inc(s_vx, 1)
                slots(dve, GROUPS, GC, WORK, slot)


def build_attention(nc, t, d):
    ctx = ExitStack()
    with ctx:
        def sb(name, shape, dt):
            return ctx.enter_context(nc.sbuf_tensor(name, shape, dt))

        def sem(name):
            return t.ctx.enter_context(nc.semaphore(name))

        QW = L + 2
        qv = sb("qv", [P, 4, QW], bf16)
        qu = sb("qu", [P, 4, L], bf16)
        kk = sb("kk", [P, 4, L], bf16)
        ub = sb("ub", [P, 2, UW], fp32)
        bd = sb("bd", [P, 4, L], fp32)
        sc = sb("sc", [P, 4, L], fp32)
        pt = sb("pt", [P, 2, L], fp32)
        mn = sb("mn", [P, 4], fp32)
        rs = sb("rs", [P, TPB], fp32)
        on = sb("on", [P, TPB, VW], fp32)
        vh = sb("vh", [P, TPB, 32], fp32)
        pb = sb("pb", [P, 2, P], fp32)
        sel = sb("sel", [P, VW], fp32)
        pu = ctx.enter_context(nc.psum_tensor("pu", [P, 3, 512], fp32))
        pa = ctx.enter_context(nc.psum_tensor("pa", [P, L], fp32))
        pp = ctx.enter_context(nc.psum_tensor("pp", [P, 2, 512], fp32))
        po = ctx.enter_context(nc.psum_tensor("po", [P, 512], fp32))

        s_pad = sem("s_pad")
        s_qv = sem("s_qv")
        s_kq = sem("s_kq")
        s_u = sem("s_u")
        s_ub = sem("s_ub")
        s_wr = [sem(f"s_wr{i}") for i in range(TPB)]
        s_rd = [sem(f"s_rd{i}") for i in range(4)]
        s_ac = sem("s_ac")
        s_sc = sem("s_sc")
        s_exp = sem("s_exp")
        s_tr = sem("s_trp")
        s_pt = sem("s_pt")
        s_pv = sem("s_pv")
        s_fin = sem("s_fin")
        s_sel = sem("s_sel")
        s_vh = sem("s_vh")
        s_pb = sem("s_pb")
        s_comb = sem("s_comb")
        s_fs = sem("s_fs")
        s_go = sem("s_go")
        s_sp = sem("s_sp")

        ring = d["ring"]

        def steps(eng, step):
            step(0, True, False, False)
            step(1, True, True, False)
            with eng.Fori(2, NH) as m:
                step(m, True, True, True)
            step(NH, False, True, True)

        with nc.Block() as block:
            @block.gpsimd
            def _(pool):
                nc.gpsimd.memset(qv[:, :, L:QW], 0.0).then_inc(s_pad, 1)
                nc.gpsimd.memset(vh[:, :, :], 0.0).then_inc(s_pad, 1)

                def load(dst, operand, two, side, s):
                    b, h = two // (H // 2), two % (H // 2)
                    for g, term in enumerate(TERMS):
                        pool.dma_start(dst[g * DH:(g + 1) * DH, bass.ds(two % 2 * 2, 2), 0:L],
                                       d["qsplit"][operand, term[side], bass.ds(h * 2 * DH, 2 * DH),
                                                   bass.ds(b * L, L)].rearrange("(a e) n -> e a n", e=DH)).then_inc(s, 16)
                load(qv, QV, 0, 0, s_qv)
                load(kk, KK, 0, 1, s_kq)
                load(qu, QU, 0, 0, s_kq)
                with pool.Fori(0, NH // 2 - 1) as two:
                    pool.wait_ge(s_u, two * 2 * TPB + 1)
                    load(qv, QV, two + 1, 0, s_qv)
                    pool.wait_ge(s_ac, two * 2 * TPB + 1)
                    load(kk, KK, two + 1, 1, s_kq)
                    load(qu, QU, two + 1, 0, s_kq)

            @block.sync
            def _(sp):
                sp.dma_start(sel[:, :], d["sel"]).then_inc(s_sel, 16)

                def step(m, ahead, main, tail):
                    for it in range(TPB):
                        r = (it + 3) % TPB
                        n = m - 1 if it + 3 < TPB else m
                        reads = it + 3 < TPB and main or it + 3 >= TPB and ahead
                        reused = reads and (it + 3 < TPB or main) and (type(n) is not int or n * TPB + r >= 4)
                        if ahead:
                            sp.wait_ge(s_ub, m * TPB + it + 1)
                            sp.sem_inc(s_sp, 1)
                            if main:
                                sp.wait_ge(s_rd[it % 4], (m * 2 - 1 + it // 4) * 16)
                            for half in range(2):
                                flat = ring[it, :, :].rearrange("p w -> (p w)")[half * HP * (UW - 1):]
                                sp.dma_start(flat[0:HP * UW].rearrange("(p w) -> p w", w=UW)[:, 0:HW],
                                             ub[half * HP:(half + 1) * HP, it % 2, HP - half * HP:HP - half * HP + HW]
                                             ).then_inc(s_wr[it], 16)
                        if reads:
                            sp.wait_ge(s_wr[r], (n + 1) * 32)
                            sp.sem_inc(s_sp, 1)
                            if reused:
                                sp.wait_ge(s_sc, n * TPB + r - 3)
                            skew = ring[r, :, :].rearrange("p w -> (p w)")[HP - 1:HP - 1 + P * (UW - 1)]
                            sp.dma_start(bd[:, r % 4, :],
                                         skew.rearrange("(p w) -> p w", p=P)[:, 0:L]).then_inc(s_rd[r % 4], 16)
                steps(sp, step)

            @block.tensor
            def _(pe):
                pe.wait_ge(t.s_rp, 16 * len(TERMS))
                pe.wait_ge(s_pad, 1)
                pe.wait_ge(s_sel, 16)
                pe.wait_ge(t.s_ident, 16)

                def unshifted(m, h, par, it):
                    i0 = it * P
                    edge = i0 + P
                    if type(m) is not int or m * TPB + it > 0:
                        pe.wait_ge(s_ub, m * TPB + it)
                    cuts = sorted({0, UB, 2 * UB, UW, edge})
                    for a, b in zip(cuts, cuts[1:]):
                        low = a < edge
                        col = RW - edge + a if low else a - edge
                        row = i0 if low else i0 + 1
                        last = nc.tensor.matmul(pu[:, a // UB, a % UB:a % UB + b - a],
                                                qv[:, par, row:row + P],
                                                t.rp[:, h, col:col + b - a], start=True, stop=True)
                    last.then_inc(s_u, 1)

                def scores(n, par, it):
                    if type(n) is not int or n * TPB + it > 0:
                        pe.wait_ge(s_sc, n * TPB + it)
                    for c in range(2):
                        last = nc.tensor.matmul(pa[:, c * 512:(c + 1) * 512], qu[:, par, it * P:(it + 1) * P],
                                                kk[:, par, c * 512:(c + 1) * 512], start=True, stop=True)
                    last.then_inc(s_ac, 1)

                def transposes(n, it):
                    g = n * TPB + it
                    pe.wait_ge(s_exp, g + 1)
                    for c in range(2):
                        if type(n) is not int or g > 0:
                            pe.wait_ge(s_pt, g * 2 - 1 + c)
                        for j in range(4):
                            last = nc.tensor.transpose(pp[:, c, j * P:(j + 1) * P],
                                                       sc[:, it % 4, (4 * c + j) * P:(4 * c + j + 1) * P],
                                                       t.ident[:, :])
                        last.then_inc(s_tr, 1)

                def weighted(n, it):
                    g = n * TPB + it
                    pe.wait_ge(s_pt, g * 2 + 2)
                    if it == 0:
                        pe.wait_ge(s_vh, n + 1)
                        if type(n) is not int or n > 0:
                            pe.wait_ge(s_fin, n)
                    if type(n) is not int or g > 0:
                        pe.wait_ge(s_pb, g)
                    for j in range(TPB):
                        c = 32 * (j % 4)
                        last = nc.tensor.matmul(po[c:c + 32, 0:P], vh[:, j, :], pt[:, it % 2, j * P:(j + 1) * P],
                                                start=j < 4, stop=j >= 4)
                    last.then_inc(s_pv, 1)

                def combine(n, it):
                    pe.wait_ge(s_pb, n * TPB + it + 1)
                    nc.tensor.matmul(po[:, P + it * VW:P + (it + 1) * VW], pb[:, it % 2, :], sel[:, :],
                                     start=True, stop=True).then_inc(s_comb, 1)

                def dyn(x):
                    return x if type(x) is int else bass.ds(x, 1)

                def step(m, ahead, main, tail):
                    if ahead:
                        pe.wait_ge(s_qv, (m // 2 + 1) * 128)
                    if main:
                        pe.wait_ge(s_kq, ((m + 1) // 2) * 256)
                    n = m - 1
                    for it in range(TPB):
                        late = [(n, it - 2)] if it >= 2 and main else [(n - 1, it + 6)] if it < 2 and tail else []
                        for nn, i in late:
                            transposes(nn, i)
                        if ahead:
                            unshifted(m, dyn(m % H), dyn(m % 4), it)
                        if main:
                            scores(n, dyn(n % 4), it)
                        if it >= 3 and main:
                            combine(n, it - 3)
                        if it < 3 and tail:
                            combine(n - 1, it + 5)
                        for nn, i in late:
                            weighted(nn, i)
                steps(pe, step)
                for i in (TPB - 2, TPB - 1):
                    transposes(NH - 1, i)
                    combine(NH - 1, i - 1)
                    weighted(NH - 1, i)
                combine(NH - 1, TPB - 1)

            @block.scalar
            def _(act):
                def exponential(n, it):
                    act.wait_ge(s_sc, n * TPB + it + 1)
                    nc.scalar.activation(sc[:, it % 4, :], sc[:, it % 4, :], ACT.Exp, scale=-1.0,
                                         bias=mn[:, it % 4:it % 4 + 1]).then_inc(s_exp, 1)

                def step(m, ahead, main, tail):
                    for it in range(TPB):
                        if it >= 1 and main:
                            exponential(m - 1, it - 1)
                        if it == 0 and tail:
                            exponential(m - 2, TPB - 1)
                        if ahead:
                            act.wait_ge(s_u, m * TPB + it + 1)
                            if it >= 2 or main:
                                act.wait_ge(s_wr[(it - 2) % TPB], (m + (1 if it >= 2 else 0)) * 32)
                            nc.scalar.activation(ub[:, it % 2, :].rearrange("p (c n) -> p c n", c=3),
                                                 pu[:, :, 0:UB], ACT.Copy).then_inc(s_ub, 1)
                steps(act, step)
                exponential(NH - 1, TPB - 1)

            @block.vector
            def _(dve):
                dve.wait_ge(s_pad, 2)

                def evacuate(n, it):
                    g = n * TPB + it
                    for c in range(2):
                        dve.wait_ge(s_tr, g * 2 + c + 1)
                        if c == 0 and (type(n) is not int or g >= 2):
                            dve.wait_ge(s_pv, g - 1)
                        nc.vector.tensor_copy(pt[:, it % 2, c * 512:(c + 1) * 512], pp[:, c, :]).then_inc(s_pt, 1)

                def total(n, it):
                    g = n * TPB + it
                    dve.wait_ge(s_ac, g + 1)
                    dve.wait_ge(s_rd[it % 4], (n * 2 + it // 4 + 1) * 16)
                    if type(n) is not int or g >= 4:
                        dve.wait_ge(s_tr, g * 2 - 6)
                    dve.sem_inc(s_go, 1)
                    nc.vector.tensor_tensor_reduce(out=sc[:, it % 4, :], in0=pa[:, :], in1=bd[:, it % 4, :],
                                                   scale=1.0, scalar=3e38, op0=ALU.add, op1=ALU.min,
                                                   accum_out=mn[:, it % 4:it % 4 + 1]).then_inc(s_sc, 1)

                def partials(n, it):
                    g = n * TPB + it
                    dve.wait_ge(s_pv, g + 1)
                    if type(n) is not int or g >= 2:
                        dve.wait_ge(s_comb, g - 1)
                    nc.vector.tensor_copy(pb[:, it % 2, :], po[:, 0:P]).then_inc(s_pb, 1)

                def values(n):
                    if type(n) is not int or n > 0:
                        dve.wait_ge(s_pv, n * TPB)
                    nc.vector.tensor_copy(vh[:, :, 0:VW].unsqueeze(2),
                                          t.vx[:, bass.ds((n // H) * TPB, TPB), bass.ds(n % H, 1), :]).then_inc(s_vh, 1)

                def finish(n):
                    dve.wait_ge(s_comb, n * TPB + TPB)
                    nc.vector.tensor_copy(on[:, :, :], po[:, P:P + TPB * VW].rearrange("p (i e) -> p i e", e=VW))\
                      .then_inc(s_fin, 1)
                    dve.wait_ge(s_fin, n + 1)
                    nc.vector.reciprocal(rs[:, :], on[:, :, DH]).then_inc(s_fs, 1)
                    dve.wait_ge(s_fs, n * 3 + 1)
                    nc.vector.tensor_tensor(on[:, :, 0:DH], on[:, :, 0:DH],
                                            rs[:, :].unsqueeze(2).to_broadcast([P, TPB, DH]), ALU.mult).then_inc(s_fs, 1)
                    dve.wait_ge(s_fs, n * 3 + 2)
                    xs = t.x[:, bass.ds((n // H) * TPB, TPB), bass.ds((n % H) * DH, DH)]
                    nc.vector.tensor_tensor(xs, xs, on[:, :, 0:DH], ALU.add).then_inc(s_fs, 1)

                def step(m, ahead, main, tail):
                    for it in range(TPB):
                        if it == 2 and main:
                            values(m - 1)
                        if it >= 2 and main:
                            evacuate(m - 1, it - 2)
                        if it < 2 and tail:
                            evacuate(m - 2, it + 6)
                        if main:
                            total(m - 1, it)
                        if it == 2 and tail:
                            finish(m - 2)
                        if it >= 2 and main:
                            partials(m - 1, it - 2)
                        if it < 2 and tail:
                            partials(m - 2, it + 6)
                steps(dve, step)
                for i in (TPB - 2, TPB - 1):
                    evacuate(NH - 1, i)
                    partials(NH - 1, i)
                finish(NH - 1)


def build_cross_queries(nc, t, d):
    ctx = ExitStack()
    with ctx:
        def sb(name, shape, dt):
            return ctx.enter_context(nc.sbuf_tensor(name, shape, dt))

        def pb(name, shape, dt):
            return ctx.enter_context(nc.psum_tensor(name, shape, dt))

        def sem(name):
            return t.ctx.enter_context(nc.semaphore(name))

        G = BT * H
        w = sb("xw", [P, 3, KC, D], fp32)
        cx = sb("cx", [S2, B, D], fp32)
        cT = sb("cT", [P, KC, B * S2], fp32)
        ks = sb("ks", [S2, B * H, DH], fp32)
        ksq = sb("ksq", [S2, B * H, DH], fp32)
        k1 = sb("k1", [S2, B * H], fp32)
        k2 = sb("k2", [S2, B * H], fp32)
        kT = sb("kT", [P, KC, B, S2], fp32)
        hm = sb("hm", [P, H // KC], fp32)
        epsc = sb("xepsc", [P, 1], fp32)
        stats = sb("xstats", [P, TPB, 6], fp32)
        aggr = sb("xaggr", [P, TPB, 2], fp32)
        mv = sb("xmv", [P, NT, 2], fp32)
        std = sb("xstd", [P, NT], fp32)
        rstd = sb("xrstd", [P, NT], fp32)
        xhat = sb("xxhat", [P, 2, BT, D], fp32)
        xT = sb("xxT", [P, 2, KC, BLK], fp32)
        centred = sb("qc", [P, NBLK * G, DH], fp32)
        squares = sb("qs", [P, 2, G, DH], fp32)
        head_sums = sb("m1", [P, 2, G], fp32)
        square_sums = sb("m2", [P, NBLK * G], fp32)
        head_reciprocals = sb("m3", [P, NBLK * G], fp32)
        normalised_q = sb("qn", [P, 2, G, DH], fp32)
        pT = pb("xpT", [P, 2, KC, BLK], fp32)
        pQ = pb("pQ", [P, 2, BT, D], fp32)
        pC = pT[:, 0, :, :]
        pK = pQ[0:S2, 0, :, :]

        weights_loaded = sem("x_weights_loaded")
        context_loaded = sem("x_context_loaded")
        columns_loaded = sem("x_columns_loaded")
        constants_set = sem("x_constants_set")
        context_turned = sem("x_context_turned")
        context_kept = sem("x_context_kept")
        keys_ready = sem("x_keys_ready")
        keys_read = sem("x_keys_read")
        keys_stepped = sem("x_keys_stepped")
        keys_squared = sem("x_keys_squared")
        values_ready = sem("x_values_ready")
        values_kept = sem("x_values_kept")
        keys_turned = sem("x_keys_turned")
        aggregated = sem("x_aggregated")
        moments_ready = sem("x_moments_ready")
        deviations_ready = sem("x_deviations_ready")
        reciprocals_ready = sem("x_reciprocals_ready")
        tile_normalised = sem("x_tile_normalised")
        block_turned = sem("x_block_turned")
        block_kept = sem("x_block_kept")
        queries_ready = sem("x_queries_ready")
        head_sums_ready = sem("x_head_sums_ready")
        queries_centred = sem("x_queries_centred")
        squares_ready = sem("x_squares_ready")
        square_sums_ready = sem("x_square_sums_ready")
        head_deviations_ready = sem("x_head_deviations_ready")
        head_reciprocals_ready = sem("x_head_reciprocals_ready")
        queries_normalised = sem("x_queries_normalised")
        queries_turned = sem("x_queries_turned")
        queries_kept = sem("x_queries_kept")

        TRANSPOSE, PROJECT, CENTRE, SQUARE, SUM = 0, 1, 2, 2, 3
        PAIR = 2

        def heads(v, parts, n):
            return v.unsqueeze(2).to_broadcast([parts, n, DH])

        def of_block(v, k):
            return v[:, bass.ds(k * G, G)] if len(v.shape) == 2 else v[:, bass.ds(k * G, G), :]

        with nc.Block() as block:
            @block.sync
            def _(sp):
                sp.dma_start(cx[:, :, :], d["ctx"].rearrange("b s e -> s b e")).then_inc(context_loaded, 16)
                for i, n in enumerate(("xwq", "xwk", "xwv")):
                    sp.dma_start(w[:, i, :, :], d[n].rearrange("(c p) o -> p c o", p=P)).then_inc(weights_loaded, 16)
                sp.dma_start(t.lncol[:, :], d["lncol"]).then_inc(columns_loaded, 16)
                sp.dma_start(hm[:, :], d["headmask"]).then_inc(columns_loaded, 16)

            @block.gpsimd
            def _(pool):
                nc.gpsimd.memset(epsc[:, :], EPS).then_inc(constants_set, 1)
                nc.gpsimd.memset(t.cv[:, :, :, :], 1.0).then_inc(constants_set, 1)
                pool.wait_ge(keys_stepped, 7)
                pool.wait_ge(columns_loaded, 32)
                for c in range(KC):
                    for b in range(B):
                        nc.gpsimd.tensor_tensor(t.kbd[:, c, b, :, :],
                                                kT[:, c, b:b + 1, :].to_broadcast([P, H // KC, S2]),
                                                hm[:, :].unsqueeze(2).to_broadcast([P, H // KC, S2]), ALU.mult)

            @block.tensor
            def _(pe):
                pe.wait_ge(context_loaded, 16)
                for c in range(KC):
                    for b in range(B):
                        last = nc.tensor.transpose(pC[:, c, b * S2:(b + 1) * S2], cx[:, b, c * P:(c + 1) * P],
                                                   t.ident[0:S2, 0:S2])
                last.then_inc(context_turned, 1)
                pe.wait_ge(weights_loaded, 48)
                pe.wait_ge(context_kept, 1)
                for i in (1, 2):
                    if i == 2:
                        pe.wait_ge(keys_read, 1)
                    for b in range(B):
                        for c in range(KC):
                            last = nc.tensor.matmul(pK[:, b, :], cT[:, c, b * S2:(b + 1) * S2], w[:, i, c, :],
                                                    start=c == 0, stop=c == KC - 1)
                    last.then_inc(keys_ready if i == 1 else values_ready, 1)
                pe.wait_ge(keys_stepped, 6)
                for c in range(KC):
                    for b in range(B):
                        last = nc.tensor.transpose(pC[:, c, b * S2:(b + 1) * S2],
                                                   ks[:, b * H + c * H // KC:b * H + (c + 1) * H // KC, :]
                                                   .rearrange("s h e -> s (h e)"), t.ident[0:S2, 0:S2])
                last.then_inc(keys_turned, 1)
                pe.wait_ge(keys_stepped, 7)
                pe.wait_ge(values_kept, 1)

                def transposes(g, par):
                    k = g * PAIR + par
                    if earlier(g, par, PAIR, 2):
                        pe.wait_ge(block_kept, k - 1)
                    for i in range(BT):
                        pe.wait_ge(tile_normalised, k * BT + i + 1)
                        for c in range(KC):
                            last = nc.tensor.transpose(pT[:, par, c, i * P:(i + 1) * P],
                                                       xhat[:, par, i, c * P:(c + 1) * P], t.ident[:, :])
                    last.then_inc(block_turned, 1)

                def project(g, par):
                    k = g * PAIR + par
                    pe.wait_ge(block_kept, k + 1)
                    if earlier(g, par, PAIR, 2):
                        pe.wait_ge(queries_centred, k - 1)
                    for i in range(BT):
                        for c in range(KC):
                            last = nc.tensor.matmul(pQ[:, par, i, :], xT[:, par, c, i * P:(i + 1) * P], w[:, 0, c, :],
                                                    start=c == 0, stop=c == KC - 1)
                    last.then_inc(queries_ready, 1)

                def slot(unit):
                    if unit(TRANSPOSE):
                        transposes(*unit(TRANSPOSE))
                    if unit(PROJECT):
                        project(*unit(PROJECT))
                slots(pe, NBLK // PAIR, PAIR, SUM, slot)
                pe.wait_ge(queries_centred, NBLK)
                pe.sem_inc(queries_kept, PAIR)
                with pe.Fori(0, NBLK // PAIR) as g:
                    for par in range(PAIR):
                        k = g * PAIR + par
                        pe.wait_ge(queries_normalised, k + 1)
                        pe.wait_ge(queries_kept, k + 1)
                        for i in range(BT):
                            for c in range(KC):
                                hs = slice(i * H + c * H // KC, i * H + (c + 1) * H // KC)
                                last = nc.tensor.transpose(pQ[:, par, i, c * P:(c + 1) * P],
                                                           normalised_q[:, par, hs, :].rearrange("p h e -> p (h e)"), t.ident[:, :])
                        last.then_inc(queries_turned, 1)

            @block.scalar
            def _(act):
                act.wait_ge(context_turned, 1)
                nc.scalar.activation(cT[:, :, :], pC[:, :, 0:B * S2], ACT.Copy).then_inc(context_kept, 1)
                act.wait_ge(constants_set, 2)
                act.wait_ge(moments_ready, B)
                nc.scalar.activation(std[:, :], mv[:, :, 1], ACT.Sqrt, bias=epsc[:, :]).then_inc(deviations_ready, 1)
                act.wait_ge(keys_stepped, 3)
                nc.scalar.activation(ksq[:, :, :], ks[:, :, :], ACT.Square).then_inc(keys_squared, 1)
                act.wait_ge(keys_stepped, 4)
                nc.scalar.activation(k2[:, :], k1[:, :], ACT.Sqrt, scale=1.0 / DH, bias=epsc[0:S2, :]).then_inc(keys_squared, 1)
                act.wait_ge(values_ready, 1)
                nc.scalar.activation(t.cv[:, :, :, 0:DH], pK[:, :, :].rearrange("s b (h e) -> s b h e", e=DH),
                                     ACT.Copy).then_inc(values_kept, 1)

                def turned(g, par):
                    act.wait_ge(block_turned, g * PAIR + par + 1)
                    if earlier(g, par, PAIR, 2):
                        act.wait_ge(queries_ready, g * PAIR + par - 1)
                    nc.scalar.activation(xT[:, par, :, :], pT[:, par, :, :], ACT.Copy).then_inc(block_kept, 1)

                def square(g, par):
                    k = g * PAIR + par
                    act.wait_ge(queries_centred, k + 1)
                    if earlier(g, par, PAIR, 2):
                        act.wait_ge(square_sums_ready, k - 1)
                    nc.scalar.activation(squares[:, par, :, :], of_block(centred, k), ACT.Square).then_inc(squares_ready, 1)

                def slot(unit):
                    if unit(TRANSPOSE):
                        turned(*unit(TRANSPOSE))
                    if unit(SQUARE):
                        square(*unit(SQUARE))
                slots(act, NBLK // PAIR, PAIR, SUM, slot)
                act.wait_ge(square_sums_ready, NBLK)
                nc.scalar.activation(square_sums[:, :], square_sums[:, :], ACT.Sqrt, scale=1.0 / DH, bias=epsc[:, :]).then_inc(head_deviations_ready, 1)
                with act.Fori(0, NBLK // PAIR) as g:
                    for par in range(PAIR):
                        k = g * PAIR + par
                        act.wait_ge(queries_turned, k + PAIR + 1)
                        nc.scalar.activation(t.qT[:, bass.ds(k * BT, BT), :, :].rearrange("p t c n -> p t (c n)"),
                                             pQ[:, par, :, :], ACT.Copy).then_inc(queries_kept, 1)

            @block.vector
            def _(dve):
                dve.wait_ge(constants_set, 2)
                layer_statistics(nc, dve, t.x, stats, aggr, mv, aggregated, moments_ready)
                dve.wait_ge(keys_ready, 1)
                kp = pK[:, :, :].rearrange("s b (h e) -> s (b h) e", e=DH)
                nc.vector.tensor_reduce(k1[:, :], kp, AX.X, ALU.add).then_inc(keys_stepped, 1)
                dve.wait_ge(keys_stepped, 1)
                nc.vector.tensor_scalar(k2[:, :], k1[:, :], 1.0 / DH, None, ALU.mult).then_inc(keys_stepped, 1)
                dve.wait_ge(keys_stepped, 2)
                nc.vector.tensor_tensor(ks[:, :, :], kp, heads(k2[:, :], S2, B * H), ALU.subtract).then_inc(keys_stepped, 1)
                dve.wait_ge(keys_stepped, 3)
                dve.sem_inc(keys_read, 1)
                dve.wait_ge(deviations_ready, 1)
                nc.vector.reciprocal(rstd[:, :], std[:, :]).then_inc(reciprocals_ready, 1)
                dve.wait_ge(keys_squared, 1)
                nc.vector.tensor_reduce(k1[:, :], ksq[:, :, :], AX.X, ALU.add).then_inc(keys_stepped, 1)
                dve.wait_ge(keys_squared, 2)
                nc.vector.reciprocal(k1[:, :], k2[:, :]).then_inc(keys_stepped, 1)
                dve.wait_ge(keys_stepped, 5)
                nc.vector.tensor_tensor(ks[:, :, :], ks[:, :, :], heads(k1[:, :], S2, B * H), ALU.mult).then_inc(keys_stepped, 1)
                dve.wait_ge(keys_turned, 1)
                dve.wait_ge(columns_loaded, 32)
                nc.vector.tensor_scalar(kT[:, :, :, :].rearrange("p c b s -> p c (b s)"), pC[:, :, 0:B * S2],
                                        t.lncol[:, 2:3], t.lncol[:, 3:4], ALU.mult, ALU.add).then_inc(keys_stepped, 1)
                dve.wait_ge(reciprocals_ready, 1)

                def normalised(g, par):
                    k = g * PAIR + par
                    if earlier(g, par, PAIR, 2):
                        dve.wait_ge(block_turned, k - 1)
                    for i in range(BT):
                        normalise_tile(nc, t.x, mv, rstd, xhat[:, par, i, :], k * BT + i).then_inc(tile_normalised, 1)

                def centre(g, par):
                    k = g * PAIR + par
                    dve.wait_ge(queries_ready, k + 1)
                    qp = pQ[:, par, :, :].rearrange("p t (h e) -> p (t h) e", e=DH)
                    nc.vector.tensor_reduce(head_sums[:, par, :], qp, AX.X, ALU.add).then_inc(head_sums_ready, 1)
                    dve.wait_ge(head_sums_ready, k * 2 + 1)
                    nc.vector.tensor_scalar(head_sums[:, par, :], head_sums[:, par, :], 1.0 / DH, None, ALU.mult).then_inc(head_sums_ready, 1)
                    dve.wait_ge(head_sums_ready, k * 2 + 2)
                    nc.vector.tensor_tensor(of_block(centred, k), qp, heads(head_sums[:, par, :], P, G), ALU.subtract).then_inc(queries_centred, 1)

                def sums(g, par):
                    k = g * PAIR + par
                    dve.wait_ge(squares_ready, k + 1)
                    nc.vector.tensor_reduce(of_block(square_sums, k), squares[:, par, :, :], AX.X, ALU.add).then_inc(square_sums_ready, 1)

                def slot(unit):
                    if unit(TRANSPOSE):
                        normalised(*unit(TRANSPOSE))
                    if unit(CENTRE):
                        centre(*unit(CENTRE))
                    if unit(SUM):
                        sums(*unit(SUM))
                slots(dve, NBLK // PAIR, PAIR, SUM, slot)
                dve.wait_ge(head_deviations_ready, 1)
                nc.vector.reciprocal(head_reciprocals[:, :], square_sums[:, :]).then_inc(head_reciprocals_ready, 1)
                dve.wait_ge(head_reciprocals_ready, 1)
                dve.sem_inc(queries_turned, PAIR)
                with dve.Fori(0, NBLK // PAIR) as g:
                    for par in range(PAIR):
                        k = g * PAIR + par
                        dve.wait_ge(queries_turned, k + 1)
                        nc.vector.tensor_tensor(normalised_q[:, par, :, :], of_block(centred, k),
                                                heads(of_block(head_reciprocals, k), P, G), ALU.mult).then_inc(queries_normalised, 1)


def build_cross_attention(nc, t, d):
    ctx = ExitStack()
    with ctx:
        def sb(name, shape, dt):
            return ctx.enter_context(nc.sbuf_tensor(name, shape, dt))

        def pb(name, shape, dt):
            return ctx.enter_context(nc.psum_tensor(name, shape, dt))

        def sem(name):
            return t.ctx.enter_context(nc.semaphore(name))

        HC = H // KC
        UN = TPB * KC
        SLOTS = 4
        wo = sb("wo", [P, KC, D], fp32)
        bo = sb("bo", [P, D], fp32)
        mask = sb("mask", [P, S2], fp32)
        divided = sb("od", [P, 2, D], fp32)
        qT = sb("qT", [P, 2, KC, P], fp32)
        probs = sb("ss", [P, SLOTS, HC, S2], fp32)
        maxima = sb("mx", [P, 2, HC], fp32)
        probs_T = sb("ypT", [S2, 2, HC, P], fp32)
        result = sb("yon", [P, 2, H, VW], fp32)
        reciprocals = sb("yrr", [P, 2, H], fp32)
        divided_T = sb("oT", [P, 2, KC, P], fp32)
        values_sb = sb("ycv", [S2, H, 32], fp32)
        result_T = sb("pos", [P, 2, H // 4, P], fp32)
        scores_ps = pb("yps", [P, 2, 2, 512], fp32)
        probs_T_ps = pb("ypt", [S2, 2, 512], fp32)
        result_ps = pb("ypo", [P, H // 4, P], fp32)
        product_ps = pb("pw", [P, 2, D], fp32)

        loaded = sem("y_loaded")
        bias_added = sem("y_bias_added")
        queries_placed = sem("y_queries_placed")
        scores_ready = sem("y_scores_ready")
        maximum_ready = sem("y_maximum_ready")
        scores_reduced = sem("y_scores_reduced")
        probs_ready = sem("y_probs_ready")
        probs_turned = sem("y_probs_turned")
        turned_probs_kept = sem("y_turned_probs_kept")
        weighted_ready = sem("y_weighted_ready")
        values_placed = sem("y_values_placed")
        result_kept = sem("y_result_kept")
        result_gathered = sem("y_result_gathered")
        result_taken = sem("y_result_taken")
        reciprocal_ready = sem("y_reciprocal_ready")
        result_divided = sem("y_result_divided")
        result_turned = sem("y_result_turned")
        turned_result_kept = sem("y_turned_result_kept")
        product_ready = sem("y_product_ready")
        tile_added = sem("y_tile_added")
        masked = sem("y_masked")

        QUERIES, SCORES, TURN, WEIGHT, GATHER, DIVIDE, BACK, PRODUCT, ADD = 0, 1, 2, 3, 5, 5, 6, 7, 8

        def tile_of(unit):
            return None if unit is None or unit[1] % 2 else (unit[0], unit[1] // 2)

        with nc.Block() as block:
            @block.sync
            def _(sp):
                sp.dma_start(wo[:, :, :], d["xwo"].rearrange("(c p) o -> p c o", p=P)).then_inc(loaded, 16)
                sp.dma_start(bo[:, :], d["bo"].partition_broadcast(P)).then_inc(loaded, 16)
                sp.dma_start(mask[:, :], d["mask"]).then_inc(loaded, 16)

            @block.gpsimd
            def _(pool):
                nc.gpsimd.memset(values_sb[:, :, :], 0.0).then_inc(values_placed, 1)
                pool.wait_ge(loaded, 48)
                for b in range(B):
                    nc.gpsimd.tensor_tensor(t.x[:, b * TPB:(b + 1) * TPB, :], t.x[:, b * TPB:(b + 1) * TPB, :],
                                            bo[:, :].unsqueeze(1).to_broadcast([P, TPB, D]), ALU.add).then_inc(bias_added, 1)

            @block.tensor
            def _(pe):
                pe.wait_ge(loaded, 48)

                def scores(b, u):
                    tile, c = u // KC, u % KC
                    if c == 0:
                        pe.wait_ge(queries_placed, b * TPB + tile + 1)
                    if earlier(b, u, UN, 2):
                        pe.wait_ge(scores_reduced, b * UN + u - 1)
                    for j in range(2):
                        last = nc.tensor.matmul(scores_ps[:, u % 2, j, 0:HC // 2 * S2], qT[:, tile % 2, c, :],
                                                t.kbd[:, c, bass.ds(b, 1), j * HC // 2:(j + 1) * HC // 2, :],
                                                start=True, stop=True)
                    last.then_inc(scores_ready, 1)

                def transposes(b, u):
                    pe.wait_ge(probs_ready, b * UN + u + 1)
                    if earlier(b, u, UN, 1):
                        pe.wait_ge(turned_probs_kept, b * UN + u)
                    for h in range(HC):
                        last = nc.tensor.transpose(probs_T_ps[:, h // 4, h % 4 * P:(h % 4 + 1) * P], probs[:, u % SLOTS, h, :],
                                                   t.ident[:, :])
                    last.then_inc(probs_turned, 1)

                def weighted(b, u):
                    tile, c = u // KC, u % KC
                    pe.wait_ge(turned_probs_kept, b * UN + u + 1)
                    if u == 0:
                        pe.wait_ge(values_placed, b + 2)
                    if c == 0 and earlier(b, u, UN, KC):
                        pe.wait_ge(result_taken, b * TPB + tile)
                    for h in range(HC):
                        row = h % 4 * 32
                        last = nc.tensor.matmul(result_ps[row:row + 32, (c * HC + h) // 4, :], values_sb[:, c * HC + h, :],
                                                probs_T[:, u % 2, h, :], start=True, stop=True)
                    last.then_inc(weighted_ready, 1)

                def gathered(b, tile):
                    pe.wait_ge(result_kept, b * TPB + tile + 1)
                    for j in range(H // 4):
                        last = nc.tensor.transpose(result_ps[:, j, :], result_T[:, tile % 2, j, :],
                                                   t.ident[:, :])
                    last.then_inc(result_gathered, 1)

                def turned(b, tile):
                    pe.wait_ge(result_divided, b * TPB + tile + 1)
                    if earlier(b, tile * KC, UN, KC):
                        pe.wait_ge(tile_added, b * TPB + tile)
                    for c in range(KC):
                        last = nc.tensor.transpose(product_ps[:, 0, c * P:(c + 1) * P],
                                                   divided[:, tile % 2, c * P:(c + 1) * P], t.ident[:, :])
                    last.then_inc(result_turned, 1)

                def output(b, tile):
                    pe.wait_ge(turned_result_kept, b * TPB + tile + 1)
                    for c in range(KC):
                        last = nc.tensor.matmul(product_ps[:, 1, :], divided_T[:, tile % 2, c, :], wo[:, c, :],
                                                start=c == 0, stop=c == KC - 1)
                    last.then_inc(product_ready, 1)

                def slot(unit):
                    if unit(SCORES):
                        scores(*unit(SCORES))
                    if unit(TURN):
                        transposes(*unit(TURN))
                    if tile_of(unit(GATHER)):
                        gathered(*tile_of(unit(GATHER)))
                    if tile_of(unit(PRODUCT)):
                        output(*tile_of(unit(PRODUCT)))
                    if unit(WEIGHT):
                        weighted(*unit(WEIGHT))
                    if tile_of(unit(BACK)):
                        turned(*tile_of(unit(BACK)))
                slots(pe, B, UN, ADD, slot)

            @block.scalar
            def _(act):
                act.wait_ge(loaded, 48)

                def queries(b, tile):
                    if earlier(b, tile * KC, UN, 2 * KC):
                        act.wait_ge(scores_ready, b * UN + (tile - 1) * KC)
                    nc.scalar.activation(qT[:, tile % 2, :, :], t.qT[:, bass.ds(b * TPB + tile, 1), :, :]
                                         .rearrange("p t c n -> p (t c) n"),
                                         ACT.Identity, scale=t.lncol[:, 0:1], bias=t.lncol[:, 1:2]).then_inc(queries_placed, 1)

                def back(b, tile):
                    act.wait_ge(result_turned, b * TPB + tile + 1)
                    nc.scalar.activation(divided_T[:, tile % 2, :, :], product_ps[:, 0, :].rearrange("p (c n) -> p c n", c=KC),
                                         ACT.Copy).then_inc(turned_result_kept, 1)

                def transposed(b, u):
                    act.wait_ge(probs_turned, b * UN + u + 1)
                    if earlier(b, u, UN, 2):
                        act.wait_ge(weighted_ready, b * UN + u - 1)
                    nc.scalar.activation(probs_T[:, u % 2, :, :].rearrange("s (j h) n -> s j (h n)", j=2),
                                         probs_T_ps[:, :, :], ACT.Copy).then_inc(turned_probs_kept, 1)

                def exponentials(b, u):
                    act.wait_ge(scores_reduced, b * UN + u + 1)
                    nc.scalar.activation(probs[:, u % SLOTS, :, :], probs[:, u % SLOTS, :, :], ACT.Exp,
                                         scale=D ** -0.5).then_inc(probs_ready, 1)

                def keep_result(b, tile):
                    act.wait_ge(weighted_ready, b * UN + 2 * tile + 2)
                    if earlier(b, tile * KC, UN, 2 * KC):
                        act.wait_ge(result_gathered, b * TPB + tile - 1)
                    nc.scalar.activation(result_T[:, tile % 2, :, :], result_ps[:, :, :], ACT.Copy).then_inc(result_kept, 1)

                def slot(unit):
                    if tile_of(unit(GATHER)):
                        keep_result(*tile_of(unit(GATHER)))
                    if tile_of(unit(QUERIES)):
                        queries(*tile_of(unit(QUERIES)))
                    if tile_of(unit(BACK + 1)):
                        back(*tile_of(unit(BACK + 1)))
                    if unit(TURN):
                        transposed(*unit(TURN))
                    if unit(SCORES):
                        exponentials(*unit(SCORES))
                slots(act, B, UN, ADD, slot)

            @block.vector
            def _(dve):
                dve.wait_ge(loaded, 48)
                dve.wait_ge(values_placed, 1)

                def less_maximum(b, u):
                    tile = u // KC
                    dve.wait_ge(scores_ready, b * UN + u + 1)
                    if earlier(b, u, UN, SLOTS):
                        dve.wait_ge(probs_turned, b * UN + u - SLOTS + 1)
                    sp4 = scores_ps[:, u % 2, :, 0:HC // 2 * S2].rearrange("p j (h s) -> p j h s", s=S2)
                    out4 = probs[:, u % SLOTS, :, :].rearrange("p (j h) s -> p j h s", j=2)
                    if tile == 0:
                        m4 = mask[:, :].unsqueeze(1).to_broadcast([P, HC // 2, S2])
                        for j in range(2):
                            nc.vector.tensor_tensor(out4[:, j, :, :], sp4[:, j, :, :], m4, ALU.add).then_inc(masked, 1)
                        dve.wait_ge(masked, b * 4 + u * 2 + 2)
                        src = out4
                    else:
                        src = sp4
                    nc.vector.tensor_reduce(maxima[:, u % 2, :].rearrange("p (j h) -> p j h", j=2), src, AX.X,
                                            ALU.max).then_inc(maximum_ready, 1)
                    dve.wait_ge(maximum_ready, b * UN + u + 1)
                    for j in range(2):
                        last = nc.vector.tensor_tensor(
                            out4[:, j, :, :], src[:, j, :, :],
                            maxima[:, u % 2, j * HC // 2:(j + 1) * HC // 2].unsqueeze(2).to_broadcast([P, HC // 2, S2]),
                            ALU.subtract)
                    last.then_inc(scores_reduced, 1)

                def divide(b, tile):
                    dve.wait_ge(result_gathered, b * TPB + tile + 1)
                    nc.vector.tensor_copy(result[:, tile % 2, :, :], result_ps[:, :, :].rearrange("p j (h e) -> p (j h) e", e=32)
                                          [:, :, 0:VW]).then_inc(result_taken, 1)
                    dve.wait_ge(result_taken, b * TPB + tile + 1)
                    nc.vector.reciprocal(reciprocals[:, tile % 2, :], result[:, tile % 2, :, DH]).then_inc(reciprocal_ready, 1)
                    dve.wait_ge(reciprocal_ready, b * TPB + tile + 1)
                    nc.vector.tensor_tensor(divided[:, tile % 2, :].rearrange("p (h e) -> p h e", e=DH),
                                            result[:, tile % 2, :, 0:DH],
                                            reciprocals[:, tile % 2, :].unsqueeze(2).to_broadcast([P, H, DH]),
                                            ALU.mult).then_inc(result_divided, 1)

                def add(b, tile):
                    if tile == 0:
                        dve.wait_ge(bias_added, b + 1)
                    dve.wait_ge(product_ready, b * TPB + tile + 1)
                    xs = t.x[:, bass.ds(b * TPB + tile, 1), :]
                    nc.vector.tensor_tensor(xs, xs, product_ps[:, 1, :].unsqueeze(1), ALU.add).then_inc(tile_added, 1)

                def values(b):
                    if earlier(b, 0, UN, 1):
                        dve.wait_ge(weighted_ready, b * UN)
                    nc.vector.tensor_copy(values_sb[:, :, 0:VW].unsqueeze(1), t.cv[:, bass.ds(b, 1), :, :]).then_inc(values_placed, 1)

                def slot(unit):
                    if unit(WEIGHT) and unit(WEIGHT)[1] == 0:
                        values(unit(WEIGHT)[0])
                    if tile_of(unit(ADD)):
                        add(*tile_of(unit(ADD)))
                    if unit(SCORES):
                        less_maximum(*unit(SCORES))
                    if tile_of(unit(DIVIDE)):
                        divide(*tile_of(unit(DIVIDE)))
                slots(dve, B, UN, ADD, slot)


def build_experts(nc, t, d):
    fp32r = mybir.dt.float32r
    NE = E + 1
    FW = NE * F
    CH = -(-FW // P)
    GC = E * F // P
    rows = [min(P, FW - c * P) for c in range(CH)]
    outer = ExitStack()
    with outer:
        def sem(name):
            return t.ctx.enter_context(nc.semaphore(name))

        def keep(name, shape, dt):
            return outer.enter_context(nc.sbuf_tensor(name, shape, dt))

        wg = [keep(f"wg{n}", [P, KC, FW], fp32r) for n in ("_high", "_low")]
        wu = [keep(f"wu{n}", [P, KC, FW], fp32r) for n in ("_high", "_low")]
        wd = [keep(f"wd{n}", [P, CH, D], fp32r) for n in ("_high", "_low")]
        xT = keep("zxT", [P, NBLK, KC, BLK], fp32)
        gT = keep("gT", [2 * E, NT * P], fp32r)

        with ExitStack() as ctx:
            def sb(name, shape, dt):
                return ctx.enter_context(nc.sbuf_tensor(name, shape, dt))

            def pb(name, shape, dt):
                return ctx.enter_context(nc.psum_tensor(name, shape, dt))

            PIECE = CH // 2 * D
            raw = sb("raw", [P, 2, PIECE], fp32)
            router = sb("zwr", [P, KC, E], fp32)
            expert_bias = sb("eb", [P, E], fp32)
            order = sb("order", [P, E], fp32)
            epsc = sb("zepsc", [P, 1], fp32)
            stats = sb("zstats", [P, TPB, 6], fp32)
            aggr = sb("zaggr", [P, TPB, 2], fp32)
            mv = sb("zmv", [P, NT, 2], fp32)
            std = sb("zstd", [P, NT], fp32)
            rstd = sb("zrstd", [P, NT], fp32)
            xhat = sb("zxhat", [P, 2, BT, D], fp32)
            logits_T = sb("lT", [E, 2, BLK], fp32)
            scores = sb("s0", [P, NT, E], fp32)
            biased = sb("s1", [P, NT, E], fp32)
            candidates = sb("c1", [P, NT, E], fp32)
            first_choice = sb("o1", [P, NT, E], fp32)
            second_choice = sb("o2", [P, NT, E], fp32)
            best = sb("ms", [P, NT], fp32)
            gate = sb("gate", [P, NT, E], fp32)
            gate_parts = sb("gp", [P, NT, 2 * E], fp32r)
            pT = pb("zpT", [P, 2, KC, BLK], fp32)
            logits_T_ps = pb("pLT", [E, BLK], fp32)
            logits_ps = pb("pL", [P, 512], fp32)
            gates_T_ps = pb("pgT", [2 * E, 2, BLK], fp32)

            piece_loaded = [sem(f"z_raw{i}") for i in range(2)]
            high_part_ready = sem("z_high_part_ready")
            low_part_ready = sem("z_low_part_ready")
            router_loaded = sem("z_router_loaded")
            constants_set = sem("z_constants_set")
            aggregated = sem("z_aggregated")
            moments_ready = sem("z_moments_ready")
            deviations_ready = sem("z_deviations_ready")
            reciprocals_ready = sem("z_reciprocals_ready")
            tile_normalised = sem("z_tile_normalised")
            block_turned = sem("z_block_turned")
            block_kept = sem("z_block_kept")
            logits_T_ready = sem("z_logits_T_ready")
            logits_T_kept = sem("z_logits_T_kept")
            logits_ready = sem("z_logits_ready")
            logits_kept = sem("z_logits_kept")
            scores_ready = sem("z_scores_ready")
            routing_stepped = sem("z_routing_stepped")
            wait_taken = sem("z_wait_taken")
            gate_parts_ready = sem("z_gate_parts_ready")
            gates_turned = sem("z_gates_turned")
            gates_kept = sem("z_gates_kept")

            NORM, TURN, LOGITS, BACK = 0, 0, 1, 2
            PAIR = 2

            pieces = [(wg, 0), (wg, 1), (wu, 0), (wu, 1), (wd, 0), (wd, 1)]
            loads = [2, 2, 2, 2, 1, 3]
            BY_ACT = 4

            def piece(n):
                dst, part = pieces[n]
                if dst is wd:
                    hi, lo = (w[:, part * CH // 2:(part + 1) * CH // 2, :].rearrange("p c o -> p (c o)") for w in dst)
                    return raw[:, n % 2, :], hi, lo
                return raw[:, n % 2, 0:FW], dst[0][:, part, :], dst[1][:, part, :]

            def loaded(eng, n):
                eng.wait_ge(piece_loaded[n % 2], 16 * sum(loads[n % 2:n + 1:2]))

            with nc.Block() as block:
                @block.sync
                def _(sp):
                    sp.dma_start(router[:, :, :], d["router"].rearrange("(c p) e -> p c e", p=P)).then_inc(router_loaded, 16)
                    sp.dma_start(expert_bias[:, :], d["ebias"].partition_broadcast(P)).then_inc(router_loaded, 16)
                    sp.wait_ge(constants_set, 1)
                    for n, (dst, part) in enumerate(pieces):
                        if n >= 2:
                            sp.wait_ge(low_part_ready, n - 1)
                        r = raw[:, n % 2, :]
                        if dst is not wd:
                            e, s = ("eg", "sg") if dst is wg else ("eu", "su")
                            sp.dma_start(r[:, 0:E * F].rearrange("p (e f) -> p e f", f=F),
                                         d[e][:, part * P:(part + 1) * P, :].rearrange("e p f -> p e f")).then_inc(piece_loaded[n % 2], 16)
                            sp.dma_start(r[:, E * F:FW], d[s][part * P:(part + 1) * P, :]).then_inc(piece_loaded[n % 2], 16)
                            continue
                        flat = d["ed"].rearrange("e f o -> (e f) o")
                        lo, hi = part * CH // 2, min((part + 1) * CH // 2, GC)
                        sp.dma_start(r[:, 0:(hi - lo) * D].rearrange("p (c o) -> p c o", o=D),
                                     flat[lo * P:hi * P, :].rearrange("(c p) o -> p c o", p=P)).then_inc(piece_loaded[n % 2], 16)
                        if part == 1:
                            for c in (GC, GC + 1):
                                sp.dma_start(raw[0:rows[c], n % 2, (c - lo) * D:(c - lo + 1) * D],
                                             d["sd"][(c - GC) * P:(c - GC) * P + rows[c], :]).then_inc(piece_loaded[n % 2], 16)

                @block.gpsimd
                def _(pool):
                    nc.gpsimd.memset(raw[:, 1, :], 0.0).then_inc(constants_set, 1)
                    nc.gpsimd.memset(epsc[:, :], EPS).then_inc(constants_set, 1)
                    for e in range(E):
                        nc.gpsimd.memset(order[:, e:e + 1], float(E - e)).then_inc(constants_set, 1)

                    for n in range(len(pieces)):
                        r, hi, lo = piece(n)
                        loaded(pool, n)
                        if n >= BY_ACT:
                            nc.gpsimd.tensor_copy(hi, r).then_inc(high_part_ready, 1)
                        pool.wait_ge(high_part_ready, n + 1)
                        nc.gpsimd.tensor_tensor(lo, r, hi.bitcast(fp32), ALU.subtract).then_inc(low_part_ready, 1)

                @block.tensor
                def _(pe):
                    pe.wait_ge(router_loaded, 32)

                    def transposes(g, par):
                        k = g * PAIR + par
                        if earlier(g, par, PAIR, 2):
                            pe.wait_ge(block_kept, k - 1)
                        for i in range(BT):
                            pe.wait_ge(tile_normalised, k * BT + i + 1)
                            for c in range(KC):
                                last = nc.tensor.transpose(pT[:, par, c, i * P:(i + 1) * P],
                                                           xhat[:, par, i, c * P:(c + 1) * P], t.ident[:, :])
                        last.then_inc(block_turned, 1)

                    def logits(g, par):
                        k = g * PAIR + par
                        pe.wait_ge(block_kept, k + 1)
                        if earlier(g, par, PAIR, 1):
                            pe.wait_ge(logits_T_kept, k)
                        pe.sem_inc(wait_taken, 1)
                        for c in range(KC):
                            last = nc.tensor.matmul(logits_T_ps[:, :], router[:, c, :],
                                                    xT[:, bass.ds(k, 1), c, :].rearrange("p k n -> p (k n)"),
                                                    start=c == 0, stop=c == KC - 1)
                        last.then_inc(logits_T_ready, 1)

                    def back(g, par):
                        k = g * PAIR + par
                        pe.wait_ge(logits_T_kept, k + 1)
                        if earlier(g, par, PAIR, 1):
                            pe.wait_ge(logits_kept, k)
                        pe.sem_inc(wait_taken, 1)
                        for i in range(BT):
                            last = nc.tensor.transpose(logits_ps[:, i * E:(i + 1) * E], logits_T[:, par, i * P:(i + 1) * P],
                                                       t.ident[0:E, 0:E])
                        last.then_inc(logits_ready, 1)

                    def slot(unit):
                        if unit(TURN):
                            transposes(*unit(TURN))
                        if unit(LOGITS):
                            logits(*unit(LOGITS))
                        if unit(BACK):
                            back(*unit(BACK))
                    slots(pe, NBLK // PAIR, PAIR, BACK, slot)
                    for k in range(NBLK):
                        pe.wait_ge(gate_parts_ready, 2)
                        if k >= 2:
                            pe.wait_ge(gates_kept, k - 1)
                        for i in range(BT):
                            last = nc.tensor.transpose(gates_T_ps[:, k % 2, i * P:(i + 1) * P],
                                                       gate_parts[:, k * BT + i, :].bitcast(fp32), t.ident[:, :])
                        last.then_inc(gates_turned, 1)

                @block.scalar
                def _(act):
                    for n in range(BY_ACT):
                        r, hi, _ = piece(n)
                        loaded(act, n)
                        nc.scalar.activation(hi, r, ACT.Copy).then_inc(high_part_ready, 1)
                    act.wait_ge(constants_set, 2)
                    act.wait_ge(moments_ready, B)
                    nc.scalar.activation(std[:, :], mv[:, :, 1], ACT.Sqrt, bias=epsc[:, :]).then_inc(deviations_ready, 1)

                    def turned(g, par):
                        k = g * PAIR + par
                        act.wait_ge(block_turned, k + 1)
                        nc.scalar.activation(xT[:, bass.ds(k, 1), :, :].rearrange("p k c n -> p (k c) n"),
                                             pT[:, par, :, :], ACT.Copy).then_inc(block_kept, 1)

                    def flat(g, par):
                        k = g * PAIR + par
                        act.wait_ge(logits_T_ready, k + 1)
                        if earlier(g, par, PAIR, 2):
                            act.wait_ge(logits_ready, k - 1)
                        nc.scalar.activation(logits_T[:, par, :], logits_T_ps[:, :], ACT.Copy).then_inc(logits_T_kept, 1)

                    def slot(unit):
                        if unit(TURN):
                            turned(*unit(TURN))
                        if unit(LOGITS):
                            flat(*unit(LOGITS))
                    slots(act, NBLK // PAIR, PAIR, LOGITS, slot)
                    act.wait_ge(logits_kept, NBLK)
                    nc.scalar.activation(scores[:, :, :], candidates[:, :, :], ACT.Sigmoid).then_inc(scores_ready, 1)
                    for k in range(NBLK):
                        act.wait_ge(gates_turned, k + 1)
                        nc.scalar.activation(gT[:, k * BLK:(k + 1) * BLK], gates_T_ps[:, k % 2, :], ACT.Copy).then_inc(gates_kept, 1)

                @block.vector
                def _(dve):
                    dve.wait_ge(constants_set, 2 + E)
                    layer_statistics(nc, dve, t.x, stats, aggr, mv, aggregated, moments_ready)
                    dve.wait_ge(deviations_ready, 1)
                    nc.vector.reciprocal(rstd[:, :], std[:, :]).then_inc(reciprocals_ready, 1)
                    dve.wait_ge(reciprocals_ready, 1)

                    def normalised(g, par):
                        k = g * PAIR + par
                        if earlier(g, par, PAIR, 2):
                            dve.wait_ge(block_turned, k - 1)
                        for i in range(BT):
                            normalise_tile(nc, t.x, mv, rstd, xhat[:, par, i, :], k * BT + i).then_inc(tile_normalised, 1)

                    def keep_logits(g, par):
                        k = g * PAIR + par
                        dve.wait_ge(logits_ready, k + 1)
                        nc.vector.tensor_copy(candidates[:, bass.ds(k * BT, BT), :],
                                              logits_ps[:, 0:BT * E].rearrange("p (t e) -> p t e", e=E)).then_inc(logits_kept, 1)

                    def slot(unit):
                        if unit(NORM):
                            normalised(*unit(NORM))
                        if unit(BACK + 1):
                            keep_logits(*unit(BACK + 1))
                    slots(dve, NBLK // PAIR, PAIR, BACK + 1, slot)
                    dve.wait_ge(scores_ready, 1)
                    dve.wait_ge(router_loaded, 32)
                    steps = [0]

                    def link(op):
                        steps[0] += 1
                        op.then_inc(routing_stepped, 1)
                        dve.wait_ge(routing_stepped, steps[0])

                    def wide(v):
                        return v.unsqueeze(2).to_broadcast([P, NT, E])

                    ebw = expert_bias[:, :].unsqueeze(1).to_broadcast([P, NT, E])
                    orw = order[:, :].unsqueeze(1).to_broadcast([P, NT, E])
                    link(nc.vector.tensor_tensor(biased[:, :, :], scores[:, :, :], ebw, ALU.add))
                    for chosen in (first_choice, second_choice):
                        link(nc.vector.tensor_reduce(best[:, :], biased[:, :, :], AX.X, ALU.max))
                        link(nc.vector.tensor_tensor(candidates[:, :, :], biased[:, :, :], wide(best[:, :]), ALU.is_equal))
                        link(nc.vector.tensor_tensor(candidates[:, :, :], candidates[:, :, :], orw, ALU.mult))
                        link(nc.vector.tensor_reduce(best[:, :], candidates[:, :, :], AX.X, ALU.max))
                        link(nc.vector.tensor_tensor(chosen[:, :, :], candidates[:, :, :], wide(best[:, :]), ALU.is_equal))
                        if chosen is first_choice:
                            link(nc.vector.scalar_tensor_tensor(biased[:, :, :], first_choice[:, :, :], -3e38, biased[:, :, :],
                                                                ALU.mult, ALU.add))
                    link(nc.vector.tensor_tensor(first_choice[:, :, :], first_choice[:, :, :], second_choice[:, :, :], ALU.add))
                    link(nc.vector.tensor_tensor(first_choice[:, :, :], first_choice[:, :, :], scores[:, :, :], ALU.mult))
                    link(nc.vector.tensor_reduce(best[:, :], first_choice[:, :, :], AX.X, ALU.add))
                    link(nc.vector.tensor_scalar(best[:, :], best[:, :], 1e-20, None, ALU.add))
                    link(nc.vector.reciprocal(best[:, :], best[:, :]))
                    link(nc.vector.tensor_tensor(gate[:, :, :], first_choice[:, :, :], wide(best[:, :]), ALU.mult))
                    nc.vector.tensor_copy(gate_parts[:, :, 0:E], gate[:, :, :]).then_inc(gate_parts_ready, 1)
                    dve.wait_ge(gate_parts_ready, 1)
                    nc.vector.tensor_tensor(gate_parts[:, :, E:2 * E], gate[:, :, :], gate_parts[:, :, 0:E].bitcast(fp32),
                                            ALU.subtract).then_inc(gate_parts_ready, 1)

        with ExitStack() as ctx:
            def sb(name, shape, dt):
                return ctx.enter_context(nc.sbuf_tensor(name, shape, dt))

            def pb(name, shape, dt):
                return ctx.enter_context(nc.psum_tensor(name, shape, dt))

            sraw = sb("sraw", [2 * E, GC * P], fp32)
            spread = sb("spread", [2 * E, GC * P], fp32r)
            x_high = sb("xh", [P, 2, KC, BLK], fp32r)
            x_low = sb("xl", [P, 2, KC, BLK], fp32r)
            silu = sb("sg", [P, 2, BLK], fp32)
            hidden_sb = sb("hid", [P, 2, BLK], fp32)
            hidden_high = sb("hh", [P, 2, BLK], fp32r)
            hidden_low = sb("hl", [P, 2, BLK], fp32r)
            gate_ps = pb("pG", [P, 2, BLK], fp32)
            up_ps = pb("zpU", [P, 2, BLK], fp32)
            spread_ps = pb("zpB", [P, 2, BLK], fp32)
            down_ps = pb("zpO", [P, 2, 2, D], fp32)

            spread_loaded = sem("w_spread_loaded")
            spread_ready = sem("w_spread_ready")
            x_high_ready = sem("w_x_high_ready")
            x_low_ready = sem("w_x_low_ready")
            gate_up_ready = sem("w_gate_up_ready")
            silu_ready = sem("w_silu_ready")
            product_ready = sem("w_product_ready")
            hidden_ready = sem("w_hidden_ready")
            banks_freed = sem("w_banks_freed")
            hidden_high_ready = sem("w_hidden_high_ready")
            hidden_low_ready = sem("w_hidden_low_ready")
            down_ready = sem("w_down_ready")
            block_added = sem("w_block_added")
            block_stored = sem("w_block_stored")

            def blocks(eng, step):
                step(0, False, True)
                with eng.Fori(1, NBLK - 1) as k:
                    step(k, True, True)
                step(NBLK - 1, True, False)

            def after(k, c, lag):
                return c >= lag or type(k) is not int or k > 0

            with nc.Block() as block:
                @block.sync
                def _(sp):
                    sp.dma_start(sraw[:, :], d["spread"]).then_inc(spread_loaded, 16)
                    for k in range(NBLK):
                        sp.wait_ge(block_added, k + 1)
                        b, i = k // 2, k % 2 * BT
                        sp.dma_start(d["out"][b, i * P:(i + BT) * P, :].rearrange("(t p) e -> p t e", p=P),
                                     t.x[:, k * BT:(k + 1) * BT, :]).then_inc(block_stored, 16)
                    sp.wait_ge(block_stored, NBLK * 16)

                @block.tensor
                def _(pe):
                    pe.wait_ge(spread_ready, 1)
                    terms = ((0, 0), (0, 1), (1, 0))

                    def up(k, c):
                        v, m, par = k * CH + c, rows[c], c % 2
                        if after(k, c, 2):
                            pe.wait_ge(hidden_ready, v - 1)
                            pe.sem_inc(banks_freed, 1)
                        for w, bank in ((wg, gate_ps), (wu, up_ps)):
                            n = 0
                            for kc in range(KC):
                                for a, b in terms:
                                    last = nc.tensor.matmul(bank[0:m, par, :], w[a][:, kc, c * P:c * P + m],
                                                            (x_high, x_low)[b][:, bass.ds(k % 2, 1), kc, :] if type(k) is not int
                                                            else (x_high, x_low)[b][:, k % 2, kc, :],
                                                            start=n == 0, stop=n == KC * 3 - 1)
                                    n += 1
                        if c < GC:
                            gates = gT[:, bass.ds(k * BLK, BLK)]
                            last = nc.tensor.matmul(spread_ps[:, par, :], spread[:, c * P:(c + 1) * P], gates,
                                                    start=True, stop=True)
                        last.then_inc(gate_up_ready, 1)

                    def down(k, c):
                        v, m, par = k * CH + c, rows[c], c % 2
                        pe.wait_ge(hidden_low_ready, v + 1)
                        if c == 0 and (type(k) is not int or k > 0):
                            pe.wait_ge(block_added, k)
                        for i in range(BT):
                            for n, (a, b) in enumerate(terms):
                                last = nc.tensor.matmul(down_ps[:, i // 2, i % 2, :], (hidden_high, hidden_low)[a][0:m, par, i * P:(i + 1) * P],
                                                        wd[b][0:m, c, :], start=c == 0 and n == 0 and i % 2 == 0,
                                                        stop=c == CH - 1 and n == 2, skip_group_check=True)
                        last.then_inc(down_ready, 1)

                    def step(k, late, ahead):
                        pe.wait_ge(x_low_ready, k + 1)
                        for c in range(CH):
                            up(k, c)
                            if c >= 2:
                                down(k, c - 2)
                            elif late:
                                down(k - 1, c + CH - 2)
                    blocks(pe, step)
                    down(NBLK - 1, CH - 2)
                    down(NBLK - 1, CH - 1)

                @block.scalar
                def _(act):
                    def high(k, c):
                        v = k * CH + c
                        act.wait_ge(hidden_ready, v + 1)
                        if after(k, c, 2):
                            act.wait_ge(down_ready, v - 1)
                        nc.scalar.activation(hidden_high[0:rows[c], c % 2, :], hidden_sb[0:rows[c], c % 2, :], ACT.Copy).then_inc(hidden_high_ready, 1)

                    def xhigh(k):
                        nc.scalar.activation(x_high[:, bass.ds(k % 2, 1), :, :].rearrange("p k c n -> p (k c) n"),
                                             xT[:, bass.ds(k, 1), :, :].rearrange("p k c n -> p (k c) n"),
                                             ACT.Copy).then_inc(x_high_ready, 1)

                    def step(k, late, ahead):
                        for c in range(CH):
                            if c > 0:
                                high(k, c - 1)
                            elif late:
                                high(k - 1, CH - 1)
                            act.wait_ge(gate_up_ready, k * CH + c + 1)
                            nc.scalar.activation(silu[0:rows[c], c % 2, :], gate_ps[0:rows[c], c % 2, :], ACT.Silu).then_inc(silu_ready, 1)
                            if c == 8 and ahead:
                                xhigh(k + 1)
                    xhigh(0)
                    blocks(act, step)
                    high(NBLK - 1, CH - 1)

                @block.vector
                def _(dve):
                    dve.wait_ge(spread_loaded, 16)
                    nc.vector.tensor_copy(spread[:, :], sraw[:, :]).then_inc(spread_ready, 1)

                    def low(k, c):
                        m, par = rows[c], c % 2
                        dve.wait_ge(hidden_high_ready, k * CH + c + 1)
                        nc.vector.tensor_tensor(hidden_low[0:m, par, :], hidden_sb[0:m, par, :], hidden_high[0:m, par, :].bitcast(fp32),
                                                ALU.subtract).then_inc(hidden_low_ready, 1)

                    def xlow(k):
                        dve.wait_ge(x_high_ready, k + 1)
                        nc.vector.tensor_tensor(x_low[:, bass.ds(k % 2, 1), :, :].rearrange("p k c n -> p (k c) n"),
                                                xT[:, bass.ds(k, 1), :, :].rearrange("p k c n -> p (k c) n"),
                                                x_high[:, bass.ds(k % 2, 1), :, :].rearrange("p k c n -> p (k c) n").bitcast(fp32),
                                                ALU.subtract).then_inc(x_low_ready, 1)

                    def hidden(k, c):
                        v, m, par = k * CH + c, rows[c], c % 2
                        dve.wait_ge(silu_ready, v + 1)
                        if c < GC:
                            nc.vector.tensor_tensor(silu[0:m, par, :], silu[0:m, par, :], up_ps[0:m, par, :], ALU.mult).then_inc(product_ready, 1)
                            dve.wait_ge(product_ready, k * GC + c + 1)
                            nc.vector.tensor_tensor(hidden_sb[0:m, par, :], silu[0:m, par, :], spread_ps[0:m, par, :], ALU.mult).then_inc(hidden_ready, 1)
                        else:
                            nc.vector.tensor_tensor(hidden_sb[0:m, par, :], silu[0:m, par, :], up_ps[0:m, par, :], ALU.mult).then_inc(hidden_ready, 1)

                    def total(k):
                        dve.wait_ge(down_ready, (k + 1) * CH)
                        for j in range(2):
                            xs = t.x[:, bass.ds(k * BT + 2 * j, 2), :]
                            last = nc.vector.tensor_tensor(xs, xs, down_ps[:, j, :, :], ALU.add)
                        last.then_inc(block_added, 1)

                    def step(k, late, ahead):
                        for c in range(CH):
                            if c > 0:
                                low(k, c - 1)
                            elif late:
                                low(k - 1, CH - 1)
                            if c == 2 and late:
                                total(k - 1)
                            hidden(k, c)
                            if c == 8 and ahead:
                                xlow(k + 1)
                    xlow(0)
                    blocks(dve, step)
                    low(NBLK - 1, CH - 1)
                    total(NBLK - 1)


class Chip:
    pass


def build_program(nc, d):
    t = Chip()
    t.ctx = ExitStack()
    with t.ctx:
        def sb(ctx, name, shape):
            return ctx.enter_context(nc.sbuf_tensor(name, shape, fp32))

        t.x = sb(t.ctx, "x_sb", [P, NT, D])
        t.ident = sb(t.ctx, "ident_sb", [P, P])
        t.s_ident = t.ctx.enter_context(nc.semaphore("s_ident"))
        t.s_rp = t.ctx.enter_context(nc.semaphore("s_rp"))
        with ExitStack() as ctx:
            t.rp = ctx.enter_context(nc.sbuf_tensor("rp", [P, H, RW], bf16))
            t.vx = sb(ctx, "vx", [P, NT, H, VW])
            build_projections(nc, t, d)
            build_attention(nc, t, d)
        with ExitStack() as ctx:
            t.qT = sb(ctx, "qT_sb", [P, NT, KC, P])
            t.kbd = sb(ctx, "kbd", [P, KC, B, H // KC, S2])
            t.cv = sb(ctx, "cv", [S2, B, H, VW])
            t.lncol = sb(ctx, "lncol_sb", [P, 4])
            build_cross_queries(nc, t, d)
            build_cross_attention(nc, t, d)
        build_experts(nc, t, d)


def constants():
    import numpy as np
    inv = (1.0 / np.float32(10000.0) ** (np.arange(0, D, 2, dtype=np.float32) / np.float32(D))).astype(np.float32)
    pos = np.arange(-(L - 1), L, dtype=np.float32)
    ang = (inv[:, None] * pos[None, :]).astype(np.float32)
    basis = np.zeros((D, RW), np.float32)
    basis[0::2, 1:] = np.sin(ang)
    basis[1::2, 1:] = np.cos(ang)
    sel = np.zeros((P, VW), np.float32)
    for p in range(P):
        if p % 32 < VW:
            sel[p, p % 32] = 1.0
    expert = np.arange(E * F) // F
    spread = (expert[None, :] == np.arange(2 * E)[:, None] % E).astype(np.float32)
    headmask = (np.arange(P)[:, None] // DH == np.arange(H // KC)[None, :]).astype(np.float32)
    mask = np.where(np.arange(S2)[None, :] <= np.arange(P)[:, None], 0.0, -1e30).astype(np.float32)
    return {"basis": basis, "ident": np.eye(P, dtype=np.float32), "sel": sel, "headmask": headmask, "mask": mask,
            "spread": spread}


def kernel(**inputs):
    import numpy as np
    import concourse.bacc as bacc
    from concourse.bass_utils import run_bass_kernel_spmd

    arrays = {"x": inputs["x"], "ctx": inputs["ctx_1024"]}
    for name, src in (("wq", "Wq"), ("wk", "Wk"), ("wv", "Wv"), ("wr", "Wr")):
        arrays[name] = np.asarray(inputs["L0_attn_" + src]).T
    uv = np.stack([np.asarray(inputs["L0_attn_u_bias"]), np.asarray(inputs["L0_attn_v_bias"])])
    arrays["uv"] = uv.reshape(2, KC, P).transpose(2, 0, 1)
    for name, src in (("xwq", "Wq"), ("xwk", "Wk"), ("xwv", "Wv"), ("xwo", "Wo"), ("bo", "bo")):
        arrays[name] = inputs["L0_xattn_" + src]
    cols = [np.asarray(inputs["L0_xattn_" + n]) for n in ("q_ln_w", "q_ln_b", "k_ln_w", "k_ln_b")]
    arrays["lncol"] = np.stack([np.tile(c, P // DH) for c in cols], axis=1)
    for name, src in (("router", "W_gate_router"), ("ebias", "expert_bias"), ("eg", "Wg"), ("eu", "Wu"), ("ed", "Wd"),
                      ("sg", "Wg_s"), ("su", "Wu_s"), ("sd", "Wd_s")):
        arrays[name] = inputs["L0_ffn_" + src]
    arrays.update(constants())
    arrays = {k: np.ascontiguousarray(a) for k, a in arrays.items()}
    nc = bacc.Bacc("TRN2", target_bir_lowering=False, num_devices=1)
    d = {k: nc.dram_tensor("in_" + k, a.shape, mybir.dt.from_np(a.dtype), kind="ExternalInput").ap()
         for k, a in arrays.items()}
    d["out"] = nc.dram_tensor("out_x", (B, L, D), fp32, kind="ExternalOutput").ap()
    d["qsplit"] = nc.dram_tensor("qsplit", (3, 3, D, B * L), bf16, kind="Internal").ap()
    d["rsplit"] = nc.dram_tensor("rsplit", (3, D, RW), bf16, kind="Internal").ap()
    d["ring"] = nc.dram_tensor("ring", (TPB, P, UW), fp32, kind="Internal").ap()
    build_program(nc, d)
    r = run_bass_kernel_spmd(nc, [{"in_" + k: a for k, a in arrays.items()}], core_ids=[0])
    return r.results[0]["out_x"]
```
